# Optimizing a Trainium2 kernel written in Bass

```python
import numpy as np
import jax
import jax.numpy as jnp

def _softmax(x, axis=-1):
    return jax.nn.softmax(x, axis=axis)

def _gelu(x):
    return jax.nn.gelu(x, approximate=True)

def _silu(x):
    return jax.nn.silu(x)

def _sigmoid(x):
    return jax.nn.sigmoid(x)

def _layernorm(x, axis=-1, eps=1e-05):
    m = jnp.mean(x, axis=axis, keepdims=True)
    v = jnp.var(x, axis=axis, keepdims=True)
    return (x - m) / jnp.sqrt(v + eps)

def _scatter_add(tgt, idx, src, axis=0):
    return tgt.at[idx].add(src)

def _segment_sum(src, seg, n):
    return jax.ops.segment_sum(src, seg, n)
kernel_name = 'mk_adaln_attn_ffn_d1_seqx_r4_f5008b'

def setup_inputs(seed: int=0):
    np.random.seed(seed)
    _w = jnp.asarray

    def _rec_inputs():
        import jax
        import jax.numpy as jnp
        _rk = jax.random.key(seed)
        x = -0.0002928 + 1 * jax.random.normal(jax.random.fold_in(_rk, 1), (8, 512, 256), jnp.float32)
        _lenS = 512 - jax.random.randint(jax.random.fold_in(_rk, 7), (8,), 0, max(1, 512 // 4) + 1, jnp.int32)
        _lenS2 = 512 - jax.random.randint(jax.random.fold_in(_rk, 8), (8,), 0, max(1, 512 // 4) + 1, jnp.int32)
        cond_64 = -0.0184271 + 1.00439 * jax.random.normal(jax.random.fold_in(_rk, 12), (8, 64), jnp.float32)
        _validS = jnp.arange(512)[None, :] < _lenS[:, None]
        _validS2 = jnp.arange(512)[None, :] < _lenS2[:, None]
        _causal = jnp.tril(jnp.ones((512, 512), dtype=bool))
        mask_BxS_bf1 = jnp.ones((8, 512), dtype=bool)
        return (x, cond_64, mask_BxS_bf1)
    x, cond_64, mask_BxS_bf1 = _rec_inputs()

    def _L0_cond_setup():
        import jax, jax.numpy as jnp
        import numpy as np
        DIM = 256
        HEADS = 16
        DIM_HEAD = 64
        SCALE = 8.0

        def ln(x, g, eps=1e-05):
            mean = x.mean(axis=-1, keepdims=True)
            var = ((x - mean) ** 2).mean(axis=-1, keepdims=True)
            return (x - mean) * jax.lax.rsqrt(var + eps) * g

        def l2norm(t):
            n = jnp.maximum(jnp.linalg.norm(t, axis=-1, keepdims=True), 1e-12)
            return t / n

        def rel_pos_bias(n, w0, b0, g0, w1, b1, g1, w2, b2, dtype):
            pos = jnp.arange(-n + 1, n, dtype=dtype)[:, None]
            h = jax.nn.silu(ln(pos @ w0 + b0, g0))
            h = jax.nn.silu(ln(h @ w1 + b1, g1))
            h = h @ w2 + b2
            i = jnp.arange(n)
            idx = i[:, None] - i[None, :] + n - 1
            bias = h[idx]
            return jnp.transpose(bias, (2, 0, 1))
        key = jax.random.key(seed)
        ks = jax.random.split(key, 16)
        b, n = (2, 512)
        inner = HEADS * DIM_HEAD
        s = 0.02
        return {'x': jax.random.normal(ks[0], (b, n, DIM), jnp.float32), 'mask': jnp.ones((b, n), dtype=bool), 'g_norm': jnp.ones((DIM,), jnp.float32), 'Wq': jax.random.normal(ks[1], (DIM, inner), jnp.float32) * s, 'Wkv': jax.random.normal(ks[2], (DIM, 2 * DIM_HEAD), jnp.float32) * s, 'q_scale': jnp.ones((DIM_HEAD,), jnp.float32), 'k_scale': jnp.ones((DIM_HEAD,), jnp.float32), 'null_kv': jax.random.normal(ks[3], (2, DIM_HEAD), jnp.float32), 'null_attn_bias': jax.random.normal(ks[4], (HEADS,), jnp.float32), 'w0': jax.random.normal(ks[5], (1, DIM), jnp.float32) * s, 'b0': jnp.zeros((DIM,), jnp.float32), 'g0': jnp.ones((DIM,), jnp.float32), 'w1': jax.random.normal(ks[6], (DIM, DIM), jnp.float32) * s, 'b1': jnp.zeros((DIM,), jnp.float32), 'g1': jnp.ones((DIM,), jnp.float32), 'w2': jax.random.normal(ks[7], (DIM, HEADS), jnp.float32) * s, 'b2': jnp.zeros((HEADS,), jnp.float32), 'Wout': jax.random.normal(ks[8], (inner, DIM), jnp.float32) * s, 'g_out': jnp.ones((DIM,), jnp.float32)}
    _L0_cond_all = _L0_cond_setup()
    _L0_cond_in = {k: v for k, v in _L0_cond_all.items() if k in ('g_norm', 'Wq', 'Wkv', 'q_scale', 'k_scale', 'null_attn_bias', 'w0', 'b0', 'g0', 'w1', 'b1', 'g1', 'w2', 'b2', 'Wout', 'g_out')}
    del _L0_cond_all

    def _L0_attn_setup():
        import jax, jax.numpy as jnp
        import numpy as np
        CHUNK = 32

        def l2norm(x, eps=1e-06):
            return x * jax.lax.rsqrt(jnp.sum(x * x, axis=-1, keepdims=True) + eps)

        def rmsnorm(x, w, eps=1e-05):
            return x * jax.lax.rsqrt(jnp.mean(x * x, axis=-1, keepdims=True) + eps) * w

        def short_conv(x, w):
            K = w.shape[1]
            l = x.shape[1]
            xp = jnp.pad(x, ((0, 0), (K - 1, 0), (0, 0)))
            y = sum((xp[:, t:t + l, :] * w[:, t] for t in range(K)))
            return y * jax.nn.sigmoid(y)

        def build_sin_cos(l, d):
            inv_freq = 1.0 / 10000.0 ** (jnp.arange(0, d, 2, dtype=jnp.float32) / d)
            ang = jnp.arange(l, dtype=jnp.float32)[:, None] * inv_freq[None, :]
            return (jnp.sin(ang), jnp.cos(ang))

        def apply_rotary(x, sin, cos):
            s = sin[None, :, None, :]
            c = cos[None, :, None, :]
            x1, x2 = (x[..., ::2], x[..., 1::2])
            return jnp.concatenate([x1 * c - x2 * s, x1 * s + x2 * c], axis=-1)

        def delta_rule_chunkwise(q, k, v, beta, gamma, chunk=CHUNK):
            b, h, l, dk = q.shape
            dv = v.shape[-1]
            n = l // chunk
            q = l2norm(q)
            k = l2norm(k)
            v = v * beta[..., None]
            kb = k * beta[..., None]
            rs = lambda x: x.reshape(b, h, n, chunk, -1)
            q, k, v, kb = (rs(q), rs(k), rs(v), rs(kb))
            gm = gamma.reshape(b, h, n, chunk).mean(-1)
            idx = jnp.arange(chunk)
            strict_lower = (idx[:, None] > idx[None, :]).astype(q.dtype)
            A = -(kb @ jnp.swapaxes(k, -1, -2)) * strict_lower
            for i in range(1, chunk):
                A = A.at[..., i, :i].add(jnp.einsum('...j,...jc->...c', A[..., i, :i], A[..., :i, :i]))
            T = A + jnp.eye(chunk, dtype=A.dtype)
            u = T @ v
            w = T @ kb
            tril_inc = (idx[:, None] >= idx[None, :]).astype(q.dtype)

            def step(S, xs):
                qi, ki, ui, wi, g = xs
                attn = qi @ jnp.swapaxes(ki, -1, -2) * tril_inc
                u_t = ui - wi @ S
                o_i = qi @ S + attn @ u_t
                S_new = g[..., None, None] * S + jnp.einsum('bhck,bhcv->bhkv', ki, u_t)
                return (S_new, o_i)
            mv = lambda x: jnp.moveaxis(x, 2, 0)
            S0 = jnp.zeros((b, h, dk, dv), dtype=q.dtype)
            S, o = jax.lax.scan(step, S0, (mv(q), mv(k), mv(u), mv(w), mv(gm)))
            o = jnp.moveaxis(o, 0, 2).reshape(b, h, l, dv)
            return (o, S)

        def fractal_mixer(x, conv_w):
            out = 2.0 * x
            l = x.shape[1]
            for i in range(conv_w.shape[0]):
                dil = 2 ** i
                x_shift = jnp.pad(x, ((0, 0), (dil, 0), (0, 0)))[:, :l, :]
                out = out + x_shift * conv_w[i, :, 0] + x * conv_w[i, :, 1]
            return out
        key = jax.random.key(seed)
        ks = jax.random.split(key, 16)
        B, L, D, H = (2, 1024, 256, 4)
        hd = D // H
        s = 0.02
        return {'hidden_states': jax.random.normal(ks[0], (B, L, D), jnp.float32), 'Wq': jax.random.normal(ks[1], (D, D), jnp.float32) * s, 'Wk': jax.random.normal(ks[2], (D, D), jnp.float32) * s, 'Wv': jax.random.normal(ks[3], (D, D), jnp.float32) * s, 'Wb': jax.random.normal(ks[4], (D, H), jnp.float32) * s, 'Wgamma': jax.random.normal(ks[5], (D, H), jnp.float32) * s, 'rot_logit': jnp.zeros((H,), jnp.float32), 'conv_q': jax.random.normal(ks[6], (D, 4), jnp.float32) * 0.1, 'conv_k': jax.random.normal(ks[7], (D, 4), jnp.float32) * 0.1, 'conv_v': jax.random.normal(ks[8], (D, 4), jnp.float32) * 0.1, 'o_norm_w': jnp.ones((hd,), jnp.float32), 'Wo': jax.random.normal(ks[9], (D, D), jnp.float32) * s, 'frac_conv_w': jax.random.normal(ks[10], (4, D, 2), jnp.float32) * 0.02, 'frac_gate_w': jax.random.normal(ks[11], (D, 1), jnp.float32) * s, 'frac_gate_b': jnp.full((1,), -1.0, jnp.float32), 'mixer_norm_w': jnp.ones((D,), jnp.float32)}
    _L0_attn_all = _L0_attn_setup()
    _L0_attn_in = {k: v for k, v in _L0_attn_all.items() if k in ('Wq', 'Wk', 'Wv', 'Wb', 'Wgamma', 'rot_logit', 'conv_q', 'conv_k', 'conv_v', 'o_norm_w', 'Wo', 'frac_conv_w', 'frac_gate_w', 'frac_gate_b', 'mixer_norm_w')}
    del _L0_attn_all

    def _L0_cond2_setup():
        import jax, jax.numpy as jnp
        import numpy as np
        B, S, H = (4, 512, 256)
        E = 8
        M = 128
        K = 2
        N_SHARED = 2
        SM = M * N_SHARED
        G = 64
        GE_TEMP = 1.0
        ALPHA = 0.001
        SEQ_AUX = True
        NORM_TOPK = True
        COS_TEMP = 0.78
        CONS_ALPHA = 0.01
        LEAKY_SLOPE = 0.01
        EPS_COS = 1e-08

        def _leaky(x):
            return jnp.where(x >= 0, x, LEAKY_SLOPE * x)

        def _moe_forward(hidden_states, g, wt, wg, w_gate, w_up, w_down, sw_gate, sw_up, sw_down):
            b, s, h = hidden_states.shape
            x = hidden_states.reshape(-1, h)
            T = x.shape[0]
            logits_h = x @ wt.T
            logits_g = g @ wg.T
            logits_g = jnp.repeat(logits_g, s, axis=0)
            logits = (logits_h + logits_g / GE_TEMP) / (1.0 + 1.0 / GE_TEMP)
            scores = jax.nn.softmax(logits, axis=-1)
            topk_w, topk_idx = jax.lax.top_k(scores, K)
            if K > 1 and NORM_TOPK:
                topk_w = topk_w / (topk_w.sum(-1, keepdims=True) + 1e-20)
            onehot = jax.nn.one_hot(topk_idx.reshape(b, s * K), E, dtype=jnp.float32)
            ce = onehot.sum(1) / (s * K / E)
            aux_loss = (ce * scores.reshape(b, s, E).mean(1)).sum(1).mean() * ALPHA
            gp = _leaky(jnp.einsum('th,ehm->etm', x, w_gate))
            up = jnp.einsum('th,ehm->etm', x, w_up)
            y_all = jnp.einsum('etm,emh->eth', gp * up, w_down)
            y_sel = y_all[topk_idx, jnp.arange(T)[:, None], :]
            y = (y_sel * topk_w[..., None]).sum(1).reshape(b, s, h)
            p = _leaky(hidden_states @ sw_gate) * (hidden_states @ sw_up) @ sw_down
            y = y + p
            num = jnp.sum(y * p, -1)
            den = jnp.maximum(jnp.linalg.norm(y, axis=-1), EPS_COS) * jnp.maximum(jnp.linalg.norm(p, axis=-1), EPS_COS)
            closs = CONS_ALPHA * jnp.mean(num / den / (1.0 + COS_TEMP))
            return (y, aux_loss + closs)
        key = jax.random.key(seed)
        ks = jax.random.split(key, 12)
        sh = 1.0 / np.sqrt(H)
        sm = 1.0 / np.sqrt(M)
        ssm = 1.0 / np.sqrt(SM)
        sg = 1.0 / np.sqrt(G)
        return {'hidden_states': jax.random.normal(ks[0], (B, S, H), jnp.float32), 'g': jax.random.normal(ks[1], (B, G), jnp.float32), 'wt': jax.random.uniform(ks[2], (E, H), jnp.float32, -sh, sh), 'wg': jax.random.uniform(ks[3], (E, G), jnp.float32, -sg, sg), 'w_gate': jax.random.uniform(ks[4], (E, H, M), jnp.float32, -sh, sh), 'w_up': jax.random.uniform(ks[5], (E, H, M), jnp.float32, -sh, sh), 'w_down': jax.random.uniform(ks[6], (E, M, H), jnp.float32, -sm, sm), 'sw_gate': jax.random.uniform(ks[7], (H, SM), jnp.float32, -sh, sh), 'sw_up': jax.random.uniform(ks[8], (H, SM), jnp.float32, -sh, sh), 'sw_down': jax.random.uniform(ks[9], (SM, H), jnp.float32, -ssm, ssm)}
    _L0_cond2_all = _L0_cond2_setup()
    _L0_cond2_in = {k: v for k, v in _L0_cond2_all.items() if k in ('wt', 'wg', 'w_gate', 'w_up', 'w_down', 'sw_gate', 'sw_up', 'sw_down')}
    del _L0_cond2_all

    def _L0_ffn_setup():
        import jax, jax.numpy as jnp
        import numpy as np
        E = 16
        G = 4
        EPG = E // G
        K = 4
        TOPK_GROUP = 2
        PER_GROUP_K = K // TOPK_GROUP

        def _route(xf, router_w, correction_bias):
            S = xf.shape[0]
            logits = xf @ router_w.T
            scores = jax.nn.sigmoid(logits)
            sb = scores + correction_bias
            grp_top = jax.lax.top_k(sb.reshape(S, G, EPG), PER_GROUP_K)[0]
            group_scores = grp_top.sum(axis=-1)
            _, group_idx = jax.lax.top_k(group_scores, TOPK_GROUP)
            group_mask = jnp.zeros((S, G), sb.dtype).at[jnp.arange(S)[:, None], group_idx].set(1.0)
            score_mask = jnp.broadcast_to(group_mask[:, :, None], (S, G, EPG)).reshape(S, E)
            masked = jnp.where(score_mask > 0, sb, -jnp.inf)
            _, topk_idx = jax.lax.top_k(masked, K)
            w = jnp.take_along_axis(scores, topk_idx, axis=1)
            w = w / (w.sum(axis=-1, keepdims=True) + 1e-20)
            return (topk_idx, w, scores)
        key = jax.random.key(seed)
        ks = jax.random.split(key, 9)
        B, T, C, H, HS = (2, 256, 256, 64, 512)
        std = 0.02
        return {'x': jax.random.normal(ks[0], (B, T, C), jnp.float32), 'router_w': jax.random.normal(ks[1], (E, C), jnp.float32) * std, 'correction_bias': jnp.zeros((E,), jnp.float32), 'gate_w': jax.random.normal(ks[2], (E, C, H), jnp.float32) * std, 'up_w': jax.random.normal(ks[3], (E, C, H), jnp.float32) * std, 'down_w': jax.random.normal(ks[4], (E, H, C), jnp.float32) * std, 'shared_gate_w': jax.random.normal(ks[5], (HS, C), jnp.float32) * std, 'shared_up_w': jax.random.normal(ks[6], (HS, C), jnp.float32) * std, 'shared_down_w': jax.random.normal(ks[7], (C, HS), jnp.float32) * std}
    _L0_ffn_all = _L0_ffn_setup()
    _L0_ffn_in = {k: v for k, v in _L0_ffn_all.items() if k in ('router_w', 'correction_bias', 'gate_w', 'up_w', 'down_w', 'shared_gate_w', 'shared_up_w', 'shared_down_w')}
    del _L0_ffn_all
    return {'x': x, 'cond_64': cond_64, 'mask_BxS_bf1': mask_BxS_bf1, 'L0_cond_g_norm': _L0_cond_in['g_norm'], 'L0_cond_Wq': _L0_cond_in['Wq'], 'L0_cond_Wkv': _L0_cond_in['Wkv'], 'L0_cond_q_scale': _L0_cond_in['q_scale'], 'L0_cond_k_scale': _L0_cond_in['k_scale'], 'L0_cond_null_attn_bias': _L0_cond_in['null_attn_bias'], 'L0_cond_w0': _L0_cond_in['w0'], 'L0_cond_b0': _L0_cond_in['b0'], 'L0_cond_g0': _L0_cond_in['g0'], 'L0_cond_w1': _L0_cond_in['w1'], 'L0_cond_b1': _L0_cond_in['b1'], 'L0_cond_g1': _L0_cond_in['g1'], 'L0_cond_w2': _L0_cond_in['w2'], 'L0_cond_b2': _L0_cond_in['b2'], 'L0_cond_Wout': _L0_cond_in['Wout'], 'L0_cond_g_out': _L0_cond_in['g_out'], 'L0_attn_Wq': _L0_attn_in['Wq'], 'L0_attn_Wk': _L0_attn_in['Wk'], 'L0_attn_Wv': _L0_attn_in['Wv'], 'L0_attn_Wb': _L0_attn_in['Wb'], 'L0_attn_Wgamma': _L0_attn_in['Wgamma'], 'L0_attn_rot_logit': _L0_attn_in['rot_logit'], 'L0_attn_conv_q': _L0_attn_in['conv_q'], 'L0_attn_conv_k': _L0_attn_in['conv_k'], 'L0_attn_conv_v': _L0_attn_in['conv_v'], 'L0_attn_o_norm_w': _L0_attn_in['o_norm_w'], 'L0_attn_Wo': _L0_attn_in['Wo'], 'L0_attn_frac_conv_w': _L0_attn_in['frac_conv_w'], 'L0_attn_frac_gate_w': _L0_attn_in['frac_gate_w'], 'L0_attn_frac_gate_b': _L0_attn_in['frac_gate_b'], 'L0_attn_mixer_norm_w': _L0_attn_in['mixer_norm_w'], 'L0_cond2_wt': _L0_cond2_in['wt'], 'L0_cond2_wg': _L0_cond2_in['wg'], 'L0_cond2_w_gate': _L0_cond2_in['w_gate'], 'L0_cond2_w_up': _L0_cond2_in['w_up'], 'L0_cond2_w_down': _L0_cond2_in['w_down'], 'L0_cond2_sw_gate': _L0_cond2_in['sw_gate'], 'L0_cond2_sw_up': _L0_cond2_in['sw_up'], 'L0_cond2_sw_down': _L0_cond2_in['sw_down'], 'L0_ffn_router_w': _L0_ffn_in['router_w'], 'L0_ffn_correction_bias': _L0_ffn_in['correction_bias'], 'L0_ffn_gate_w': _L0_ffn_in['gate_w'], 'L0_ffn_up_w': _L0_ffn_in['up_w'], 'L0_ffn_down_w': _L0_ffn_in['down_w'], 'L0_ffn_shared_gate_w': _L0_ffn_in['shared_gate_w'], 'L0_ffn_shared_up_w': _L0_ffn_in['shared_up_w'], 'L0_ffn_shared_down_w': _L0_ffn_in['shared_down_w']}

def reference(x, cond_64, mask_BxS_bf1, L0_cond_g_norm, L0_cond_Wq, L0_cond_Wkv, L0_cond_q_scale, L0_cond_k_scale, L0_cond_null_attn_bias, L0_cond_w0, L0_cond_b0, L0_cond_g0, L0_cond_w1, L0_cond_b1, L0_cond_g1, L0_cond_w2, L0_cond_b2, L0_cond_Wout, L0_cond_g_out, L0_attn_Wq, L0_attn_Wk, L0_attn_Wv, L0_attn_Wb, L0_attn_Wgamma, L0_attn_rot_logit, L0_attn_conv_q, L0_attn_conv_k, L0_attn_conv_v, L0_attn_o_norm_w, L0_attn_Wo, L0_attn_frac_conv_w, L0_attn_frac_gate_w, L0_attn_frac_gate_b, L0_attn_mixer_norm_w, L0_cond2_wt, L0_cond2_wg, L0_cond2_w_gate, L0_cond2_w_up, L0_cond2_w_down, L0_cond2_sw_gate, L0_cond2_sw_up, L0_cond2_sw_down, L0_ffn_router_w, L0_ffn_correction_bias, L0_ffn_gate_w, L0_ffn_up_w, L0_ffn_down_w, L0_ffn_shared_gate_w, L0_ffn_shared_up_w, L0_ffn_shared_down_w):
    import jax
    import jax.numpy as jnp

    def _L0_cond_ref(x, mask, g_norm, Wq, Wkv, q_scale, k_scale, null_kv, null_attn_bias, w0, b0, g0, w1, b1, g1, w2, b2, Wout, g_out):
        import jax, jax.numpy as jnp
        import numpy as np
        DIM = 256
        HEADS = 16
        DIM_HEAD = 64
        SCALE = 8.0

        def ln(x, g, eps=1e-05):
            mean = x.mean(axis=-1, keepdims=True)
            var = ((x - mean) ** 2).mean(axis=-1, keepdims=True)
            return (x - mean) * jax.lax.rsqrt(var + eps) * g

        def l2norm(t):
            n = jnp.maximum(jnp.linalg.norm(t, axis=-1, keepdims=True), 1e-12)
            return t / n

        def rel_pos_bias(n, w0, b0, g0, w1, b1, g1, w2, b2, dtype):
            pos = jnp.arange(-n + 1, n, dtype=dtype)[:, None]
            h = jax.nn.silu(ln(pos @ w0 + b0, g0))
            h = jax.nn.silu(ln(h @ w1 + b1, g1))
            h = h @ w2 + b2
            i = jnp.arange(n)
            idx = i[:, None] - i[None, :] + n - 1
            bias = h[idx]
            return jnp.transpose(bias, (2, 0, 1))
        b, n, _ = x.shape
        xn = ln(x, g_norm)
        q = (xn @ Wq).reshape(b, n, HEADS, DIM_HEAD).transpose(0, 2, 1, 3)
        kv = xn @ Wkv
        k, v = (kv[..., :DIM_HEAD], kv[..., DIM_HEAD:])
        nk = jnp.broadcast_to(null_kv[0], (b, 1, DIM_HEAD))
        nv = jnp.broadcast_to(null_kv[1], (b, 1, DIM_HEAD))
        k = jnp.concatenate([nk, k], axis=1)
        v = jnp.concatenate([nv, v], axis=1)
        q = l2norm(q) * q_scale
        k = l2norm(k) * k_scale
        sim = jnp.einsum('bhid,bjd->bhij', q, k) * SCALE
        bias = rel_pos_bias(n, w0, b0, g0, w1, b1, g1, w2, b2, q.dtype)
        null_bias = jnp.broadcast_to(null_attn_bias[:, None, None], (HEADS, n, 1))
        attn_bias = jnp.concatenate([null_bias, bias], axis=-1)
        sim = sim + attn_bias
        neg = -jnp.finfo(sim.dtype).max
        causal = jnp.triu(jnp.ones((n, n + 1), dtype=bool), k=2)
        sim = jnp.where(causal, neg, sim)
        m = jnp.pad(mask, ((0, 0), (1, 0)), constant_values=True)[:, None, None, :]
        sim = jnp.where(m, sim, neg)
        attn = jax.nn.softmax(sim, axis=-1)
        out = jnp.einsum('bhij,bjd->bhid', attn, v)
        out = out.transpose(0, 2, 1, 3).reshape(b, n, HEADS * DIM_HEAD)
        return ln(out @ Wout, g_out)

    def _L0_attn_ref(hidden_states, Wq, Wk, Wv, Wb, Wgamma, rot_logit, conv_q, conv_k, conv_v, o_norm_w, Wo, frac_conv_w, frac_gate_w, frac_gate_b, mixer_norm_w):
        import jax, jax.numpy as jnp
        import numpy as np
        CHUNK = 32

        def l2norm(x, eps=1e-06):
            return x * jax.lax.rsqrt(jnp.sum(x * x, axis=-1, keepdims=True) + eps)

        def rmsnorm(x, w, eps=1e-05):
            return x * jax.lax.rsqrt(jnp.mean(x * x, axis=-1, keepdims=True) + eps) * w

        def short_conv(x, w):
            K = w.shape[1]
            l = x.shape[1]
            xp = jnp.pad(x, ((0, 0), (K - 1, 0), (0, 0)))
            y = sum((xp[:, t:t + l, :] * w[:, t] for t in range(K)))
            return y * jax.nn.sigmoid(y)

        def build_sin_cos(l, d):
            inv_freq = 1.0 / 10000.0 ** (jnp.arange(0, d, 2, dtype=jnp.float32) / d)
            ang = jnp.arange(l, dtype=jnp.float32)[:, None] * inv_freq[None, :]
            return (jnp.sin(ang), jnp.cos(ang))

        def apply_rotary(x, sin, cos):
            s = sin[None, :, None, :]
            c = cos[None, :, None, :]
            x1, x2 = (x[..., ::2], x[..., 1::2])
            return jnp.concatenate([x1 * c - x2 * s, x1 * s + x2 * c], axis=-1)

        def delta_rule_chunkwise(q, k, v, beta, gamma, chunk=CHUNK):
            b, h, l, dk = q.shape
            dv = v.shape[-1]
            n = l // chunk
            q = l2norm(q)
            k = l2norm(k)
            v = v * beta[..., None]
            kb = k * beta[..., None]
            rs = lambda x: x.reshape(b, h, n, chunk, -1)
            q, k, v, kb = (rs(q), rs(k), rs(v), rs(kb))
            gm = gamma.reshape(b, h, n, chunk).mean(-1)
            idx = jnp.arange(chunk)
            strict_lower = (idx[:, None] > idx[None, :]).astype(q.dtype)
            A = -(kb @ jnp.swapaxes(k, -1, -2)) * strict_lower
            for i in range(1, chunk):
                A = A.at[..., i, :i].add(jnp.einsum('...j,...jc->...c', A[..., i, :i], A[..., :i, :i]))
            T = A + jnp.eye(chunk, dtype=A.dtype)
            u = T @ v
            w = T @ kb
            tril_inc = (idx[:, None] >= idx[None, :]).astype(q.dtype)

            def step(S, xs):
                qi, ki, ui, wi, g = xs
                attn = qi @ jnp.swapaxes(ki, -1, -2) * tril_inc
                u_t = ui - wi @ S
                o_i = qi @ S + attn @ u_t
                S_new = g[..., None, None] * S + jnp.einsum('bhck,bhcv->bhkv', ki, u_t)
                return (S_new, o_i)
            mv = lambda x: jnp.moveaxis(x, 2, 0)
            S0 = jnp.zeros((b, h, dk, dv), dtype=q.dtype)
            S, o = jax.lax.scan(step, S0, (mv(q), mv(k), mv(u), mv(w), mv(gm)))
            o = jnp.moveaxis(o, 0, 2).reshape(b, h, l, dv)
            return (o, S)

        def fractal_mixer(x, conv_w):
            out = 2.0 * x
            l = x.shape[1]
            for i in range(conv_w.shape[0]):
                dil = 2 ** i
                x_shift = jnp.pad(x, ((0, 0), (dil, 0), (0, 0)))[:, :l, :]
                out = out + x_shift * conv_w[i, :, 0] + x * conv_w[i, :, 1]
            return out
        x = hidden_states
        b, l, d = x.shape
        H = rot_logit.shape[0]
        q = short_conv(x @ Wq, conv_q)
        k = short_conv(x @ Wk, conv_k)
        v = short_conv(x @ Wv, conv_v)
        dk = q.shape[-1] // H
        dv = v.shape[-1] // H
        q = q.reshape(b, l, H, dk)
        k = k.reshape(b, l, H, dk)
        v = v.reshape(b, l, H, dv)
        sin, cos = build_sin_cos(l, dk)
        mix = jax.nn.sigmoid(rot_logit)[None, None, :, None]
        q = mix * apply_rotary(q, sin, cos) + (1.0 - mix) * q
        k = mix * apply_rotary(k, sin, cos) + (1.0 - mix) * k
        beta = jax.nn.sigmoid(x @ Wb)
        gamma = jax.nn.sigmoid(x @ Wgamma)
        bh = lambda t: jnp.transpose(t, (0, 2, 1, 3))
        o, _ = delta_rule_chunkwise(bh(q), bh(k), bh(v), jnp.transpose(beta, (0, 2, 1)), jnp.transpose(gamma, (0, 2, 1)))
        o = jnp.transpose(o, (0, 2, 1, 3))
        o = rmsnorm(o, o_norm_w)
        core = o.reshape(b, l, H * dv) @ Wo
        frac = rmsnorm(fractal_mixer(x, frac_conv_w), mixer_norm_w)
        gate = jax.nn.sigmoid(x @ frac_gate_w + frac_gate_b)
        return core + gate * frac

    def _L0_cond2_ref(hidden_states, g, wt, wg, w_gate, w_up, w_down, sw_gate, sw_up, sw_down):
        import jax, jax.numpy as jnp
        import numpy as np
        B, S, H = (4, 512, 256)
        E = 8
        M = 128
        K = 2
        N_SHARED = 2
        SM = M * N_SHARED
        G = 64
        GE_TEMP = 1.0
        ALPHA = 0.001
        SEQ_AUX = True
        NORM_TOPK = True
        COS_TEMP = 0.78
        CONS_ALPHA = 0.01
        LEAKY_SLOPE = 0.01
        EPS_COS = 1e-08

        def _leaky(x):
            return jnp.where(x >= 0, x, LEAKY_SLOPE * x)

        def _moe_forward(hidden_states, g, wt, wg, w_gate, w_up, w_down, sw_gate, sw_up, sw_down):
            b, s, h = hidden_states.shape
            x = hidden_states.reshape(-1, h)
            T = x.shape[0]
            logits_h = x @ wt.T
            logits_g = g @ wg.T
            logits_g = jnp.repeat(logits_g, s, axis=0)
            logits = (logits_h + logits_g / GE_TEMP) / (1.0 + 1.0 / GE_TEMP)
            scores = jax.nn.softmax(logits, axis=-1)
            topk_w, topk_idx = jax.lax.top_k(scores, K)
            if K > 1 and NORM_TOPK:
                topk_w = topk_w / (topk_w.sum(-1, keepdims=True) + 1e-20)
            onehot = jax.nn.one_hot(topk_idx.reshape(b, s * K), E, dtype=jnp.float32)
            ce = onehot.sum(1) / (s * K / E)
            aux_loss = (ce * scores.reshape(b, s, E).mean(1)).sum(1).mean() * ALPHA
            gp = _leaky(jnp.einsum('th,ehm->etm', x, w_gate))
            up = jnp.einsum('th,ehm->etm', x, w_up)
            y_all = jnp.einsum('etm,emh->eth', gp * up, w_down)
            y_sel = y_all[topk_idx, jnp.arange(T)[:, None], :]
            y = (y_sel * topk_w[..., None]).sum(1).reshape(b, s, h)
            p = _leaky(hidden_states @ sw_gate) * (hidden_states @ sw_up) @ sw_down
            y = y + p
            num = jnp.sum(y * p, -1)
            den = jnp.maximum(jnp.linalg.norm(y, axis=-1), EPS_COS) * jnp.maximum(jnp.linalg.norm(p, axis=-1), EPS_COS)
            closs = CONS_ALPHA * jnp.mean(num / den / (1.0 + COS_TEMP))
            return (y, aux_loss + closs)
        y, _ = _moe_forward(hidden_states, g, wt, wg, w_gate, w_up, w_down, sw_gate, sw_up, sw_down)
        return y

    def _L0_ffn_ref(x, router_w, correction_bias, gate_w, up_w, down_w, shared_gate_w, shared_up_w, shared_down_w):
        import jax, jax.numpy as jnp
        import numpy as np
        E = 16
        G = 4
        EPG = E // G
        K = 4
        TOPK_GROUP = 2
        PER_GROUP_K = K // TOPK_GROUP

        def _route(xf, router_w, correction_bias):
            S = xf.shape[0]
            logits = xf @ router_w.T
            scores = jax.nn.sigmoid(logits)
            sb = scores + correction_bias
            grp_top = jax.lax.top_k(sb.reshape(S, G, EPG), PER_GROUP_K)[0]
            group_scores = grp_top.sum(axis=-1)
            _, group_idx = jax.lax.top_k(group_scores, TOPK_GROUP)
            group_mask = jnp.zeros((S, G), sb.dtype).at[jnp.arange(S)[:, None], group_idx].set(1.0)
            score_mask = jnp.broadcast_to(group_mask[:, :, None], (S, G, EPG)).reshape(S, E)
            masked = jnp.where(score_mask > 0, sb, -jnp.inf)
            _, topk_idx = jax.lax.top_k(masked, K)
            w = jnp.take_along_axis(scores, topk_idx, axis=1)
            w = w / (w.sum(axis=-1, keepdims=True) + 1e-20)
            return (topk_idx, w, scores)
        B, T, C = x.shape
        S = B * T
        xf = x.reshape(S, C)
        sg = xf @ shared_gate_w.T
        su = xf @ shared_up_w.T
        shared_out = jax.nn.silu(sg) * su @ shared_down_w.T
        topk_idx, w, _scores = _route(xf, router_w, correction_bias)
        combine = jnp.zeros((S, E), xf.dtype).at[jnp.arange(S)[:, None], topk_idx].add(w)
        g = jnp.einsum('sc,ech->esh', xf, gate_w)
        u = jnp.einsum('sc,ech->esh', xf, up_w)
        h = jax.nn.silu(g) * u
        hw = h * combine.T[:, :, None]
        routed = jnp.einsum('esh,ehc->sc', hw, down_w)
        return (shared_out + routed).reshape(B, T, C)
    x = x + _L0_attn_ref(_L0_cond_ref(x, mask_BxS_bf1, L0_cond_g_norm, L0_cond_Wq, L0_cond_Wkv, L0_cond_q_scale, L0_cond_k_scale, cond_64, L0_cond_null_attn_bias, L0_cond_w0, L0_cond_b0, L0_cond_g0, L0_cond_w1, L0_cond_b1, L0_cond_g1, L0_cond_w2, L0_cond_b2, L0_cond_Wout, L0_cond_g_out), L0_attn_Wq, L0_attn_Wk, L0_attn_Wv, L0_attn_Wb, L0_attn_Wgamma, L0_attn_rot_logit, L0_attn_conv_q, L0_attn_conv_k, L0_attn_conv_v, L0_attn_o_norm_w, L0_attn_Wo, L0_attn_frac_conv_w, L0_attn_frac_gate_w, L0_attn_frac_gate_b, L0_attn_mixer_norm_w)
    x = x + _L0_ffn_ref(_L0_cond2_ref(x, cond_64, L0_cond2_wt, L0_cond2_wg, L0_cond2_w_gate, L0_cond2_w_up, L0_cond2_w_down, L0_cond2_sw_gate, L0_cond2_sw_up, L0_cond2_sw_down), L0_ffn_router_w, L0_ffn_correction_bias, L0_ffn_gate_w, L0_ffn_up_w, L0_ffn_down_w, L0_ffn_shared_gate_w, L0_ffn_shared_up_w, L0_ffn_shared_down_w)
    return x

_drawn_inputs = setup_inputs


def setup_inputs(seed=0):
    import zlib

    import numpy as np

    out = dict(_drawn_inputs(seed))
    spreads = {'L0_cond_g_norm': (1.0, 0.2),
     'L0_cond_q_scale': (1.0, 0.2),
     'L0_cond_k_scale': (1.0, 0.2),
     'L0_cond_b0': (0.0, 0.1),
     'L0_cond_g0': (1.0, 0.2),
     'L0_cond_b1': (0.0, 0.1),
     'L0_cond_g1': (1.0, 0.2),
     'L0_cond_b2': (0.0, 0.1),
     'L0_cond_g_out': (1.0, 0.2),
     'L0_attn_rot_logit': (0.0, 0.1),
     'L0_attn_o_norm_w': (1.0, 0.2),
     'L0_attn_mixer_norm_w': (1.0, 0.2),
     'L0_ffn_correction_bias': (0.0, 0.1)}
    factors = {}
    for name, (base, spread) in spreads.items():
        noise = np.random.default_rng([zlib.crc32(name.encode()), seed]).standard_normal(out[name].shape)
        drawn = base * np.exp(spread * noise) if base else spread * noise
        out[name] = jnp.asarray(drawn.astype(out[name].dtype))
    for name, factor in factors.items():
        out[name] = (out[name] * factor).astype(out[name].dtype)
    return out
```

```python
from contextlib import ExitStack

import numpy as np
import concourse.bass as bass
from concourse import mybir

F32 = mybir.dt.float32
BF16 = mybir.dt.bfloat16
ALU = mybir.AluOpType
ACT = mybir.ActivationFunctionType
AX = mybir.AxisListType

P = 128
B, L, D = 8, 512, 256
KD = D // P
TT = L // P
NH, DH = 16, 64
QT = NH // 2
QW = NH * DH
SCALE = 8.0
NEG = float(-np.finfo(np.float32).max)
MASKED = -1.0e30
BIAS_W = L + P - 1

H2, CH, NC4 = 4, 32, 4
NCH = L // CH
E1, M1 = 8, 128
S1 = 256
E2, M2 = 16, 64
S2W = 512
G2 = 4


class Chain:

    def __init__(self, eng, sem):
        self.eng, self.sem, self.n = eng, sem, 0

    def __call__(self, ins):
        self.n += 1
        ins.then_inc(self.sem, 1)
        self.eng.wait_ge(self.sem, self.n)


def clear(nc, sems):
    with nc.Block() as block:
        @block.sync
        def _(sp):
            for s in sems:
                sp.sem_clear(s)


def space(nc, ctx, prefix):
    sems = []

    def sb(name, shape, dt=F32):
        return ctx.enter_context(nc.sbuf_tensor(f"{prefix}_{name}", shape, dt))

    def bank(name, dt=F32):
        return ctx.enter_context(nc.psum_tensor(f"{prefix}_{name}", [P, 2048 // (2 if dt == BF16 else 4)], dt))

    def sem(name):
        s = ctx.enter_context(nc.semaphore(f"{prefix}_{name}"))
        sems.append(s)
        return s

    return sb, bank, sem, sems


def row(ap, n):
    return bass.AP(tensor=ap.tensor, offset=ap.offset, ap=[[0, P], [1, n]])


def bias_phase(nc, a, bias_rows):
    with ExitStack() as ctx:
        sb, bank, sem, sems = space(nc, ctx, "r")
        pos = sb("pos", [P, TT])
        ident = sb("ident", [P, P])
        w0, b0, g0, b1, g1 = (sb(n, [P, D]) for n in ("w0", "b0", "g0", "b1", "g1"))
        w1 = sb("w1", [P, KD, D])
        w2 = sb("w2", [P, KD, NH])
        b2 = sb("b2", [NH, 1])
        h = sb("h", [P, TT, D])
        hn = sb("hn", [P, TT, D])
        hT = sb("hT", [P, KD, L])
        stats = sb("stats", [P, TT, 6])
        mv = sb("mv", [P, TT, 2])
        ve = sb("ve", [P, TT])
        half = sb("half", [P, TT])
        rstd = sb("rstd", [P, TT])
        rows = sb("rows", [NH, BIAS_W + 1])
        ps = [bank(f"ps{i}") for i in range(4)]

        loaded = sem("loaded")
        half_ready = sem("half_ready")
        var_ready = sem("var_ready")
        rstd_ready = sem("rstd_ready")
        h_normed = sem("h_normed")
        h_active = sem("h_active")
        hT_psum = sem("hT_psum")
        hT_ready = sem("hT_ready")
        prod_psum = sem("prod_psum")
        rows_ready = sem("rows_ready")
        rows_out = sem("rows_out")
        dve_chain = sem("dve_chain")

        with nc.Block() as block:
            @block.sync
            def _(sp):
                loads = [(pos[:], a["c_pos"]), (ident[:], a["c_ident"]), (w0[:], row(a["L0_cond_w0"], D)),
                         (b0[:], row(a["L0_cond_b0"], D)), (g0[:], row(a["L0_cond_g0"], D)),
                         (b1[:], row(a["L0_cond_b1"], D)), (g1[:], row(a["L0_cond_g1"], D)),
                         (w1[:], a["L0_cond_w1"].rearrange("(k p) n -> p k n", p=P)),
                         (w2[:], a["L0_cond_w2"].rearrange("(k p) n -> p k n", p=P)),
                         (b2[:], a["L0_cond_b2"].rearrange("(n o) -> n o", o=1))]
                for dst, src in loads:
                    sp.dma_start(dst, src).then_inc(loaded, 16)
                sp.wait_ge(rows_ready, 1)
                sp.dma_start(bias_rows[:, :], rows[:, :]).then_inc(rows_out, 16)
                sp.wait_ge(rows_out, 16)

            N_LOADS = 160

            @block.gpsimd
            def _(pool):
                pool.memset(half[:], -0.5).then_inc(half_ready, 1)
                pool.wait_ge(half_ready, 1)
                for layer in range(2):
                    pool.wait_ge(var_ready, layer + 1)
                    pool.tensor_tensor(rstd[:], ve[:], half[:], ALU.pow).then_inc(rstd_ready, 1)

            @block.vector
            def _(dve):
                link = Chain(dve, dve_chain)
                link(dve.memset(rows[:, L:], NEG))
                dve.wait_ge(loaded, N_LOADS)
                for layer in range(2):
                    gain = (g0, g1)[layer]
                    if layer == 0:
                        for t in range(TT):
                            last = dve.scalar_tensor_tensor(out=h[:, t], in0=w0[:], scalar=pos[:, t:t + 1],
                                                            in1=b0[:], op0=ALU.mult, op1=ALU.add)
                        link(last)
                    else:
                        for t in range(TT):
                            dve.wait_ge(prod_psum, t + 1)
                            last = dve.tensor_tensor(h[:, t], ps[t][:, 0:D], b1[:], ALU.add)
                        link(last)
                    for t in range(TT):
                        last = dve.bn_stats(stats[:, t], h[:, t])
                    link(last)
                    for t in range(TT):
                        last = dve.bn_aggr(mv[:, t], stats[:, t])
                    link(last)
                    dve.tensor_scalar(ve[:], mv[:, :, 1], 1e-5, None, ALU.add).then_inc(var_ready, 1)
                    dve.wait_ge(rstd_ready, layer + 1)
                    for t in range(TT):
                        last = dve.tensor_scalar(hn[:, t], h[:, t], mv[:, t, 0:1], rstd[:, t:t + 1],
                                                 ALU.subtract, ALU.mult)
                    link(last)
                    for t in range(TT):
                        last = dve.tensor_tensor(hn[:, t], hn[:, t], gain[:], ALU.mult)
                    last.then_inc(h_normed, 1)
                    for k in range(KD):
                        dve.wait_ge(hT_psum, KD * layer + k + 1)
                        dve.tensor_copy(hT[:, k], ps[k][:, :]).then_inc(hT_ready, 1)
                dve.wait_ge(prod_psum, TT + 1)
                dve.tensor_scalar(rows[:, 0:L], ps[2][0:NH, :], b2[:, 0:1], None, ALU.add).then_inc(rows_ready, 1)

            @block.scalar
            def _(act):
                for layer in range(2):
                    act.wait_ge(h_normed, layer + 1)
                    act.activation(hn[:], hn[:], ACT.Silu).then_inc(h_active, 1)

            @block.tensor
            def _(pe):
                pe.wait_ge(loaded, N_LOADS)
                for layer in range(2):
                    pe.wait_ge(h_active, layer + 1)
                    for k in range(KD):
                        for t in range(TT):
                            last = pe.transpose(ps[k][:, t * P:(t + 1) * P], hn[:, t, k * P:(k + 1) * P], ident[:])
                        last.then_inc(hT_psum, 1)
                    pe.wait_ge(hT_ready, KD * (layer + 1))
                    if layer == 0:
                        for t in range(TT):
                            for k in range(KD):
                                last = pe.matmul(ps[t][:, 0:D], hT[:, k, t * P:(t + 1) * P], w1[:, k],
                                                 start=k == 0, stop=k == KD - 1)
                            last.then_inc(prod_psum, 1)
                    else:
                        for k in range(KD):
                            last = pe.matmul(ps[2][0:NH, :], w2[:, k], hT[:, k], start=k == 0, stop=k == KD - 1)
                        last.then_inc(prod_psum, 1)
        clear(nc, sems)


def attention_phase(nc, a, bias_rows, hT_dram):
    with ExitStack() as ctx:
        sb, bank, sem, sems = space(nc, ctx, "a")
        ident = sb("ident", [P, P])
        turn = sb("turn", [P, P])
        wqkv = sb("wqkv", [P, KD, QW + 2 * DH])
        wout = sb("wout", [P, QT, D])
        bias = sb("bias", [P, NH, L])
        gn = sb("gn", [P, KD])
        go = sb("go", [P, KD])
        kscale = sb("kscale", [P, 3])
        nullk = sb("nullk", [P, 2])
        nullv = sb("nullv", [P, DH])
        nullb = sb("nullb", [P, NH])
        nkrow = sb("nkrow", [1, 3 * DH])
        half = sb("half", [P, NH + 2])
        ones = sb("ones", [1, P], BF16)
        mask_in = sb("mask_in", [1, L], mybir.dt.uint8)
        mask_row = sb("mask_row", [1, L], BF16)

        x = sb("x", [P, TT, D])
        stats = sb("stats", [P, 6])
        mv = sb("mv", [P, 2])
        ve = sb("ve", [P, 1])
        rstd = sb("rstd", [P, 1])
        xn = sb("xn", [P, D])
        xnT = sb("xnT", [P, KD, P])
        qraw = sb("qraw", [P, NH + 1, DH])
        sq = sb("sq", [P, NH + 1, DH])
        ss = sb("ss", [P, NH + 1])
        rr = sb("rr", [P, NH + 1])
        qn = sb("qn", [P, NH + 2, DH])
        qT = sb("qT", [P, 2, QT, P])
        kT = sb("kT", [P, L])
        v = sb("v", [P, TT, DH])
        nsn = sb("nsn", [P, 2, NH])
        S = sb("S", [P, 3, L])
        PT = sb("PT", [P, 2, L])
        nm = sb("nm", [P, 2, NH])
        den = sb("den", [P, 2, NH])
        dn = sb("dn", [P, NH])
        pn = sb("pn", [P, NH])
        dent = sb("dent", [P, NH])
        rden = sb("rden", [P, NH])
        pnr = sb("pnr", [P, NH])
        onull = sb("onull", [P, NH, DH])
        o = sb("o", [P, NH, DH])
        oT = sb("oT", [P, QT, P])
        stats2 = sb("stats2", [P, 6])
        mv2 = sb("mv2", [P, 2])
        ve2 = sb("ve2", [P, 1])
        rstd2 = sb("rstd2", [P, 1])
        hn = sb("hn", [P, D])
        hT = sb("hT", [P, TT, KD, P])

        SB = [bank(f"S{i}") for i in range(2)]
        TB = [bank(f"T{i}") for i in range(2)]
        OB = [bank(f"O{i}") for i in range(2)]
        FB = [bank(f"F{i}") for i in range(2)]

        loaded = sem("loaded")
        prep = sem("prep")
        prep_psum = sem("prep_psum")
        bias_psum = sem("bias_psum")
        bias_act = sem("bias_act")
        bias_dve = sem("bias_dve")
        dve_chain = sem("dve_chain")
        pool_chain = sem("pool_chain")

        with nc.Block() as block:
            @block.sync
            def _(sp):
                toeplitz = bass.AP(tensor=bias_rows.tensor, offset=0, ap=[[1, P], [BIAS_W + 1, NH], [1, L]])
                loads = [(ident[:], a["c_ident"]), (turn[:], a["c_turn"]),
                         (wqkv[:, :, 0:QW], a["L0_cond_Wq"].rearrange("(k p) n -> p k n", p=P)),
                         (wqkv[:, :, QW:], a["L0_cond_Wkv"].rearrange("(k p) n -> p k n", p=P)),
                         (wout[:], a["L0_cond_Wout"].rearrange("(k p) n -> p k n", p=P)),
                         (bias[:], toeplitz),
                         (gn[:], a["L0_cond_g_norm"]),
                         (go[:], a["L0_cond_g_out"]),
                         (kscale[0:DH, 0:1], a["L0_cond_q_scale"].rearrange("(n o) -> n o", o=1)),
                         (kscale[DH:P, 0:1], a["L0_cond_q_scale"].rearrange("(n o) -> n o", o=1)),
                         (kscale[0:DH, 1:2], a["L0_cond_k_scale"].rearrange("(n o) -> n o", o=1)),
                         (kscale[DH:P, 1:2], a["L0_cond_k_scale"].rearrange("(n o) -> n o", o=1)),
                         (nullv[:], row(a["cond_64"][1, :], DH)),
                         (nullb[:], row(a["L0_cond_null_attn_bias"], NH)),
                         (nkrow[:, 0:DH], a["cond_64"][0:1, :])]
                for dst, src in loads:
                    sp.dma_start(dst, src).then_inc(loaded, 16)
                sp.wait_ge(loaded, 16 * len(loads))

            @block.gpsimd
            def _(pool):
                pool.memset(half[:], -0.5).then_inc(pool_chain, 1)
                pool.wait_ge(prep, 1)
                pool.wait_ge(pool_chain, 1)
                pool.tensor_tensor(nkrow[:, 2 * DH + 2:2 * DH + 3], nkrow[:, 2 * DH + 1:2 * DH + 2],
                                   half[0:1, 0:1], ALU.pow).then_inc(pool_chain, 1)

            @block.vector
            def _(dve):
                link = Chain(dve, dve_chain)
                dve.memset(ones[:], 1.0)
                dve.memset(nullk[:], 0.0)
                dve.wait_ge(loaded, 16 * 15)
                for k in range(KD):
                    dve.tensor_scalar(wqkv[:, k], wqkv[:, k], gn[:, k:k + 1], None, ALU.mult)
                link(dve.tensor_scalar(kscale[:, 2:3], kscale[:, 0:1], kscale[:, 1:2], SCALE, ALU.mult, ALU.mult))
                link(dve.tensor_tensor_reduce(nkrow[:, DH:2 * DH], nkrow[:, 0:DH], nkrow[:, 0:DH], 1.0, 0.0,
                                              ALU.mult, ALU.add, nkrow[:, 2 * DH:2 * DH + 1]))
                dve.tensor_scalar(nkrow[:, 2 * DH + 1:2 * DH + 2], nkrow[:, 2 * DH:2 * DH + 1], 1e-24, None,
                                  ALU.max).then_inc(prep, 1)
                dve.wait_ge(pool_chain, 2)
                for half_of in range(2):
                    last = dve.tensor_scalar(S[0:1, 0, half_of * DH:(half_of + 1) * DH], nkrow[:, 0:DH],
                                             nkrow[:, 2 * DH + 2:2 * DH + 3], None, ALU.mult)
                last.then_inc(prep, 1)
                dve.wait_ge(prep_psum, 1)
                for half_of in range(2):
                    part = slice(half_of * DH, (half_of + 1) * DH)
                    dve.tensor_scalar(nullk[part, half_of:half_of + 1], FB[0][part, 0:1], kscale[part, 2:3], None,
                                      ALU.mult)
                for h in range(1, NH, 2):
                    dve.wait_ge(bias_psum, h + 1)
                    dve.tensor_copy(bias[:, h], (SB + TB)[h % 4][:, :]).then_inc(bias_dve, 1)

            @block.tensor
            def _(pe):
                pe.wait_ge(loaded, 16 * 15)
                pe.wait_ge(prep, 2)
                pe.matmul(FB[0][:, 0:1], S[0:1, 0, 0:P], ident[0:1, 0:1], start=True, stop=True).then_inc(prep_psum, 1)
                for h in range(NH):
                    if h >= 4:
                        pe.wait_ge((bias_act, bias_dve)[h % 2], (h - 4) // 2 + 1)
                    pe.matmul((SB + TB)[h % 4][:, :], turn[:], bias[:, h], start=True, stop=True).then_inc(bias_psum, 1)

            @block.scalar
            def _(act):
                for h in range(0, NH, 2):
                    act.wait_ge(bias_psum, h + 1)
                    act.copy(bias[:, h], (SB + TB)[h % 4][:, :]).then_inc(bias_act, 1)
        clear(nc, sems)

        x_in = sem("x_in")
        mask_ready = sem("mask_ready")
        x_var = sem("x_var")
        x_rstd = sem("x_rstd")
        xn_ready = sem("xn_ready")
        xnT_ready = sem("xnT_ready")
        q_ready = sem("q_ready")
        kv_ready = sem("kv_ready")
        sq_ready = sem("sq_ready")
        ss_ready = sem("ss_ready")
        qn_ready = sem("qn_ready")
        qT_act = sem("qT_act")
        qT_dve = sem("qT_dve")
        kT_ready = sem("kT_ready")
        null_ready = sem("null_ready")
        scores_psum = sem("scores_psum")
        scores_ready = sem("scores_ready")
        probs_ready = sem("probs_ready")
        probsT_psum = sem("probsT_psum")
        probsT_act = sem("probsT_act")
        probsT_dve = sem("probsT_dve")
        pv_done = sem("pv_done")
        null_diff = sem("null_diff")
        null_probs = sem("null_probs")
        weights_ready = sem("weights_ready")
        onull_ready = sem("onull_ready")
        o_scaled = sem("o_scaled")
        o_ready = sem("o_ready")
        oT_act = sem("oT_act")
        oT_dve = sem("oT_dve")
        out_var = sem("out_var")
        out_rstd = sem("out_rstd")
        hn_ready = sem("hn_ready")
        hT_ready = sem("hT_ready")
        hT_out = sem("hT_out")
        full = [sem(f"F{i}_filled") for i in range(2)]

        NEXT = {0: ["stat"], 1: ["xn"], 2: ["xT"], 4: ["q"], 6: ["kv"], 8: ["ss"], 9: ["qn"], 11: ["qT"],
                13: ["kT"]}
        LAST = {2: ["weigh"], 5: ["oT"], 7: ["outp"], 8: ["hn"], 10: ["hT"]}
        STEPS = []
        for names in NEXT.values():
            STEPS += [(n, 0) for n in names]
        for t in range(TT):
            for h in range(NH):
                STEPS.append(("head", NH * t + h))
                if t + 1 < TT:
                    STEPS += [(n, t + 1) for n in NEXT.get(h, [])]
                if t > 0:
                    STEPS += [(n, t - 1) for n in LAST.get(h, [])]
        LAG = 3
        STEPS += [("head", NH * TT + i) for i in range(LAG)]
        for names in LAST.values():
            STEPS += [(n, TT - 1) for n in names]

        FILLS = {"xT": [0], "q": [1, 0], "kv": [1], "qT": [0, 1], "kT": [0, 1], "oT": [0, 1], "outp": [0], "hT": [1]}
        filling, before, held = {}, {}, [[], []]
        for name, t in STEPS:
            for n in FILLS.get(name, []):
                filling[name, t, n] = len(held[n])
                before[name, t, n] = held[n][-1] if held[n] else None
                held[n].append((name, t, n))

        def drained(name, t, n):
            return {"xT": (xnT_ready, t + 1), "q": (q_ready, 2 * t + 2 - n), "kv": (kv_ready, 2 * t + 2),
                    "qT": ((qT_act, qT_dve)[n], t + 1), "kT": ((kT_ready, null_ready)[n], t + 1),
                    "oT": ((oT_act, oT_dve)[n], t + 1), "outp": (hn_ready, t + 1), "hT": (hT_ready, t + 1)}[name]

        def evac_by_act(n):
            return n % 3 == 0

        def count_act(n):
            return n // 3 + 1

        with nc.Fori(0, B) as b:
            with nc.Block() as block:
                @block.sync
                def _(sp):
                    sp.dma_start(x[:], a["x"][bass.ds(b, 1), :, :].rearrange("o (t p) d -> p (o t) d", p=P)).then_inc(x_in, 16)
                    sp.dma_start(mask_in[:], a["mask"][bass.ds(b, 1), :]).then_inc(x_in, 16)
                    for t in range(TT):
                        sp.wait_ge(hT_ready, t + 1)
                        sp.dma_start(hT_dram[bass.ds(b, 1), :, :, t * P:(t + 1) * P].rearrange("o p k n -> (o p) k n"),
                                     hT[:, t]).then_inc(hT_out, 16)
                    sp.wait_ge(hT_out, 16 * TT)

                def wait_evac(eng, n):
                    if evac_by_act(n):
                        eng.wait_ge(probsT_act, count_act(n))
                    else:
                        eng.wait_ge(probsT_dve, n + 1 - count_act(n))

                @block.tensor
                def _(pe):
                    def fill(name, t, n):
                        if before[name, t, n]:
                            pe.wait_ge(*drained(*before[name, t, n]))
                        return FB[n]

                    for name, t in STEPS:
                        if name == "head":
                            n = t
                            if n < NH * TT:
                                tile, h = divmod(n, NH)
                                w = P * (tile + 1)
                                part = slice(DH * (h % 2), DH * (h % 2) + DH)
                                if n == 0:
                                    pe.wait_ge(mask_ready, 1)
                                if h == 0:
                                    pe.wait_ge(qT_act, tile + 1)
                                    pe.wait_ge(qT_dve, tile + 1)
                                    pe.wait_ge(kT_ready, tile + 1)
                                if n >= 2:
                                    pe.wait_ge(scores_ready, n - 1)
                                s = SB[n % 2]
                                pe.matmul(s[:, 0:w], ones[:], mask_row[:, 0:w], start=True, stop=False)
                                pe.matmul(s[:, 0:w], qT[part, tile % 2, h // 2], kT[part, 0:w],
                                          start=False, stop=True).then_inc(scores_psum, 1)
                            n = t - 2
                            if 0 <= n < NH * TT:
                                tile = n // NH
                                pe.wait_ge(probs_ready, n + 1)
                                if n >= 2:
                                    wait_evac(pe, n - 2)
                                for j in range(tile + 1):
                                    last = pe.transpose(TB[n % 2][:, j * P:(j + 1) * P],
                                                        S[:, n % 3, j * P:(j + 1) * P], ident[:])
                                last.then_inc(probsT_psum, 1)
                            n = t - 3
                            if 0 <= n < NH * TT:
                                tile, h = divmod(n, NH)
                                wait_evac(pe, n)
                                if h % 8 == 0 and tile > 0:
                                    pe.wait_ge(o_scaled, 2 * (tile - 1) + h // 8 + 1)
                                for j in range(tile + 1):
                                    last = pe.matmul(OB[h // 8][:, (h % 8) * DH:(h % 8 + 1) * DH],
                                                     PT[:, n % 2, j * P:(j + 1) * P], v[:, j],
                                                     start=j == 0, stop=j == tile)
                                last.then_inc(pv_done, 1)
                        elif name == "xT":
                            pe.wait_ge(xn_ready, t + 1)
                            f = fill("xT", t, 0)
                            for k in range(KD):
                                last = pe.transpose(f[:, k * P:(k + 1) * P], xn[:, k * P:(k + 1) * P], ident[:])
                            last.then_inc(full[0], 1)
                        elif name == "q":
                            pe.wait_ge(xnT_ready, t + 1)
                            for i, n in enumerate((1, 0)):
                                f = fill("q", t, n)
                                for k in range(KD):
                                    last = pe.matmul(f[:, :], xnT[:, k], wqkv[:, k, i * 512:(i + 1) * 512],
                                                     start=k == 0, stop=k == KD - 1)
                                last.then_inc(full[n], 1)
                        elif name == "kv":
                            f = fill("kv", t, 1)
                            for k in range(KD):
                                last = pe.matmul(f[:, 0:2 * DH], xnT[:, k], wqkv[:, k, QW:],
                                                 start=k == 0, stop=k == KD - 1)
                            last.then_inc(full[1], 1)
                        elif name == "qT":
                            pe.wait_ge(qn_ready, t + 1)
                            for n in range(2):
                                f = fill("qT", t, n)
                                for j in range(4):
                                    i = 4 * n + j
                                    last = pe.transpose(f[:, j * P:(j + 1) * P],
                                                        qn[:, 2 * i:2 * i + 2].rearrange("p a d -> p (a d)"), ident[:])
                                last.then_inc(full[n], 1)
                        elif name == "kT":
                            f = fill("kT", t, 0)
                            pe.transpose(f[:, 0:P], qn[:, NH:NH + 2].rearrange("p a d -> p (a d)"),
                                         ident[:]).then_inc(full[0], 1)
                            pe.wait_ge(qT_act, t + 1)
                            pe.wait_ge(qT_dve, t + 1)
                            f = fill("kT", t, 1)
                            for i in range(QT):
                                last = pe.matmul(f[:, 2 * i:2 * i + 2], qT[:, t % 2, i], nullk[:], start=True, stop=True)
                            last.then_inc(full[1], 1)
                        elif name == "oT":
                            pe.wait_ge(o_ready, t + 1)
                            for n in range(2):
                                f = fill("oT", t, n)
                                for j in range(4):
                                    i = 4 * n + j
                                    last = pe.transpose(f[:, j * P:(j + 1) * P],
                                                        o[:, 2 * i:2 * i + 2].rearrange("p a d -> p (a d)"), ident[:])
                                last.then_inc(full[n], 1)
                        elif name == "outp":
                            pe.wait_ge(oT_act, t + 1)
                            pe.wait_ge(oT_dve, t + 1)
                            f = fill("outp", t, 0)
                            for i in range(QT):
                                last = pe.matmul(f[:, 0:D], oT[:, i], wout[:, i], start=i == 0, stop=i == QT - 1)
                            last.then_inc(full[0], 1)
                        elif name == "hT":
                            pe.wait_ge(hn_ready, t + 1)
                            f = fill("hT", t, 1)
                            for k in range(KD):
                                last = pe.transpose(f[:, k * P:(k + 1) * P], hn[:, k * P:(k + 1) * P], ident[:])
                            last.then_inc(full[1], 1)

                @block.vector
                def _(dve):
                    link = Chain(dve, dve_chain)

                    def filled(name, t, n):
                        dve.wait_ge(full[n], filling[name, t, n] + 1)
                        return FB[n]

                    dve.wait_ge(x_in, 32)
                    dve.tensor_scalar(mask_row[:], mask_in[:], -MASKED, MASKED, ALU.mult, ALU.add).then_inc(mask_ready, 1)
                    for name, t in STEPS:
                        if name == "head":
                            n = t
                            if n < NH * TT:
                                tile, h = divmod(n, NH)
                                w = P * (tile + 1)
                                if h == 0:
                                    dve.wait_ge(null_ready, tile + 1)
                                dve.wait_ge(scores_psum, n + 1)
                                if n >= 3:
                                    dve.wait_ge(probsT_psum, n - 2)
                                dve.tensor_tensor_reduce(S[:, n % 3, 0:w], SB[n % 2][:, 0:w],
                                                         bias[:, h, L - w:L], -1.0, nsn[:, tile % 2, h:h + 1],
                                                         ALU.add, ALU.min, nm[:, tile % 2, h:h + 1]).then_inc(scores_ready, 1)
                            n = t - 2
                            if 0 <= n < NH * TT and not evac_by_act(n):
                                dve.wait_ge(probsT_psum, n + 1)
                                if n >= 2:
                                    dve.wait_ge(pv_done, n - 1)
                                w = P * (n // NH + 1)
                                dve.tensor_copy(PT[:, n % 2, 0:w], TB[n % 2][:, 0:w]).then_inc(probsT_dve, 1)
                        elif name == "stat":
                            link(dve.bn_stats(stats[:], x[:, t]))
                            link(dve.bn_aggr(mv[:], stats[:]))
                            if t > 0:
                                dve.wait_ge(x_rstd, t)
                            dve.tensor_scalar(ve[:], mv[:, 1:2], 1e-5, None, ALU.add).then_inc(x_var, 1)
                        elif name == "xn":
                            dve.wait_ge(x_rstd, t + 1)
                            if t > 0:
                                dve.wait_ge(full[0], filling["xT", t - 1, 0] + 1)
                            dve.tensor_scalar(xn[:], x[:, t], mv[:, 0:1], rstd[:], ALU.subtract,
                                              ALU.mult).then_inc(xn_ready, 1)
                        elif name == "ss":
                            dve.wait_ge(sq_ready, t + 1)
                            link(dve.tensor_reduce(ss[:], sq[:], AX.X, ALU.add))
                            dve.tensor_scalar(ss[:], ss[:], 1e-24, None, ALU.max).then_inc(ss_ready, 1)
                        elif name == "qT":
                            f = filled("qT", t, 1)
                            dve.tensor_copy(qT[:, t % 2, 4:8].rearrange("p a n -> p (a n)"), f[:, :])\
                               .then_inc(qT_dve, 1)
                        elif name == "kT":
                            f = filled("kT", t, 0)
                            dve.tensor_scalar(kT[:, t * P:(t + 1) * P], f[:, 0:P], kscale[:, 2:3], None,
                                              ALU.mult).then_inc(kT_ready, 1)
                            f = filled("kT", t, 1)
                            dve.scalar_tensor_tensor(out=nsn[:, t % 2], in0=f[:, 0:NH], scalar=-1.0, in1=nullb[:],
                                                     op0=ALU.mult, op1=ALU.subtract).then_inc(null_ready, 1)
                        elif name == "weigh":
                            i = t % 2
                            dve.wait_ge(scores_ready, NH * (t + 1))
                            dve.tensor_tensor(dn[:], nm[:, i], nsn[:, i], ALU.subtract).then_inc(null_diff, 1)
                            dve.wait_ge(null_probs, t + 1)
                            dve.wait_ge(probs_ready, NH * (t + 1))
                            link(dve.tensor_tensor(dent[:], den[:, i], pn[:], ALU.add))
                            link(dve.reciprocal(rden[:], dent[:]))
                            if t > 0:
                                dve.wait_ge(onull_ready, t)
                            dve.tensor_tensor(pnr[:], pn[:], rden[:], ALU.mult).then_inc(weights_ready, 1)
                            for half_of in range(2):
                                dve.wait_ge(pv_done, NH * t + 8 * (half_of + 1))
                                if t > 0:
                                    dve.wait_ge(full[half_of], filling["oT", t - 1, half_of] + 1)
                                hs = slice(8 * half_of, 8 * half_of + 8)
                                dve.tensor_tensor(o[:, hs], OB[half_of][:, :].rearrange("p (h d) -> p h d", d=DH),
                                                  rden[:, hs].unsqueeze(2).broadcast_to([P, 8, DH]),
                                                  ALU.mult).then_inc(o_scaled, 1)
                        elif name == "oT":
                            f = filled("oT", t, 1)
                            if t > 0:
                                dve.wait_ge(full[0], filling["outp", t - 1, 0] + 1)
                            dve.tensor_copy(oT[:, 4:8].rearrange("p a n -> p (a n)"), f[:, :]).then_inc(oT_dve, 1)
                        elif name == "outp":
                            f = filled("outp", t, 0)
                            link(dve.bn_stats(stats2[:], f[:, 0:D]))
                            link(dve.bn_aggr(mv2[:], stats2[:]))
                            dve.tensor_scalar(ve2[:], mv2[:, 1:2], 1e-5, None, ALU.add).then_inc(out_var, 1)
                        elif name == "hn":
                            dve.wait_ge(out_rstd, t + 1)
                            if t > 0:
                                dve.wait_ge(full[1], filling["hT", t - 1, 1] + 1)
                            dve.tensor_scalar(hn[:], FB[0][:, 0:D], mv2[:, 0:1], rstd2[:], ALU.subtract,
                                              ALU.mult).then_inc(hn_ready, 1)

                @block.scalar
                def _(act):
                    def filled(name, t, n):
                        act.wait_ge(full[n], filling[name, t, n] + 1)
                        return FB[n]

                    for name, t in STEPS:
                        if name == "head":
                            n = t - 1
                            if 0 <= n < NH * TT:
                                tile, h = divmod(n, NH)
                                w = P * (tile + 1)
                                act.wait_ge(scores_ready, n + 1)
                                act.activation(S[:, n % 3, 0:w], S[:, n % 3, 0:w], ACT.Exp, scale=-1.0,
                                               bias=nm[:, tile % 2, h:h + 1],
                                               accum_out=den[:, tile % 2, h:h + 1]).then_inc(probs_ready, 1)
                            n = t - 2
                            if 0 <= n < NH * TT and evac_by_act(n):
                                act.wait_ge(probsT_psum, n + 1)
                                if n >= 2:
                                    act.wait_ge(pv_done, n - 1)
                                w = P * (n // NH + 1)
                                act.copy(PT[:, n % 2, 0:w], TB[n % 2][:, 0:w]).then_inc(probsT_act, 1)
                        elif name == "xT":
                            f = filled("xT", t, 0)
                            if t > 0:
                                act.wait_ge(full[1], filling["kv", t - 1, 1] + 1)
                            act.copy(xnT[:].rearrange("p k n -> p (k n)"), f[:, 0:D]).then_inc(xnT_ready, 1)
                        elif name == "q":
                            if t > 0:
                                act.wait_ge(qn_ready, t)
                            for i, n in enumerate((1, 0)):
                                f = filled("q", t, n)
                                act.copy(qraw[:, 8 * i:8 * i + 8].rearrange("p a d -> p (a d)"), f[:, :])\
                                   .then_inc(q_ready, 1)
                        elif name == "kv":
                            f = filled("kv", t, 1)
                            act.copy(v[:, t], f[:, DH:2 * DH]).then_inc(kv_ready, 1)
                            act.copy(qraw[:, NH], f[:, 0:DH]).then_inc(kv_ready, 1)
                        elif name == "qT":
                            f = filled("qT", t, 0)
                            act.copy(qT[:, t % 2, 0:4].rearrange("p a n -> p (a n)"), f[:, :]).then_inc(qT_act, 1)
                        elif name == "weigh":
                            act.wait_ge(null_diff, t + 1)
                            act.activation(pn[:], dn[:], ACT.Exp).then_inc(null_probs, 1)
                        elif name == "oT":
                            f = filled("oT", t, 0)
                            if t > 0:
                                act.wait_ge(full[0], filling["outp", t - 1, 0] + 1)
                            act.copy(oT[:, 0:4].rearrange("p a n -> p (a n)"), f[:, :]).then_inc(oT_act, 1)
                        elif name == "hT":
                            f = filled("hT", t, 1)
                            for k in range(KD):
                                last = act.activation(hT[:, t, k], f[:, k * P:(k + 1) * P], ACT.Copy,
                                                      scale=go[:, k:k + 1])
                            last.then_inc(hT_ready, 1)

                @block.gpsimd
                def _(pool):
                    link = Chain(pool, pool_chain)
                    for name, t in STEPS:
                        if name == "stat":
                            pool.wait_ge(x_var, t + 1)
                            if t > 0:
                                pool.wait_ge(xn_ready, t)
                            pool.tensor_tensor(rstd[:], ve[:], half[:, 0:1], ALU.pow).then_inc(x_rstd, 1)
                        elif name == "kv":
                            pool.wait_ge(q_ready, 2 * t + 2)
                            pool.wait_ge(kv_ready, 2 * t + 2)
                            if t > 0:
                                pool.wait_ge(ss_ready, t)
                            pool.tensor_tensor(sq[:], qraw[:], qraw[:], ALU.mult).then_inc(sq_ready, 1)
                        elif name == "qn":
                            pool.wait_ge(ss_ready, t + 1)
                            link(pool.tensor_tensor(rr[:], ss[:], half[:, 0:NH + 1], ALU.pow))
                            if t > 0:
                                pool.wait_ge(full[0], filling["kT", t - 1, 0] + 1)
                            pool.tensor_tensor(qn[:, 0:NH + 1], qraw[:],
                                               rr[:].unsqueeze(2).broadcast_to([P, NH + 1, DH]), ALU.mult)
                            pool.tensor_tensor(qn[:, NH + 1], qraw[:, NH],
                                               rr[:, NH:NH + 1].broadcast_to([P, DH]), ALU.mult).then_inc(qn_ready, 1)
                        elif name == "weigh":
                            pool.wait_ge(weights_ready, t + 1)
                            pool.tensor_tensor(onull[:], nullv[:].unsqueeze(1).broadcast_to([P, NH, DH]),
                                               pnr[:].unsqueeze(2).broadcast_to([P, NH, DH]),
                                               ALU.mult).then_inc(onull_ready, 1)
                            pool.wait_ge(onull_ready, t + 1)
                            pool.wait_ge(o_scaled, 2 * t + 2)
                            pool.tensor_tensor(o[:], o[:], onull[:], ALU.add).then_inc(o_ready, 1)
                        elif name == "outp":
                            pool.wait_ge(out_var, t + 1)
                            if t > 0:
                                pool.wait_ge(hn_ready, t)
                            pool.tensor_tensor(rstd2[:], ve2[:], half[:, 0:1], ALU.pow).then_inc(out_rstd, 1)
            clear(nc, sems)


def drained_before(order, drained):
    held, out = {}, {}
    for bank, step, n in order:
        out[bank, step, n] = drained(*held[bank]) if bank in held else []
        held[bank] = (step, n)
    return out


def delta_inputs_phase(nc, a, hT_dram, xg_dram, qk_dram, vb_dram, bg_dram, low_dram):
    PAD = 8
    with ExitStack() as ctx:
        sb, bank, sem, sems = space(nc, ctx, "b")
        ident = sb("ident", [P, P])
        wqkv = sb("wqkv", [P, KD, 3 * D])
        wsm = sb("wsm", [P, KD, 2 * H2 + 1])
        smb = sb("smb", [P, 2 * H2 + 1])
        conv = sb("conv", [P, 3, KD, 4])
        frac = sb("frac", [P, KD, 4, 2])
        own = sb("own", [P, KD])
        cos = sb("cos", [P, TT, DH // 2])
        sin = sb("sin", [P, TT, DH // 2])
        rot = sb("rot", [P, H2])
        cm = sb("cm", [P, TT, H2, DH // 2])
        sm = sb("sm", [P, TT, H2, DH // 2])
        omx = sb("omx", [P, H2, DH])
        mixw = sb("mixw", [P, D])
        strict = sb("strict", [P, CH])
        half = sb("half", [P, 8])

        h = sb("h", [P, KD, PAD + L])
        x = sb("x", [P, TT, D])
        proj = sb("proj", [P, 6, 3 + L])
        y = sb("y", [P, 6, L])
        gates_in = sb("gates_in", [P, TT, 2 * H2 + 1])
        gates = sb("gates", [P, TT, 2 * H2 + 1])
        nb = sb("nb", [P, TT, H2, CH])
        fr = sb("fr", [P, KD, L])
        ft = sb("ft", [P, L])
        fsq = sb("fsq", [P, TT, D])
        fss = sb("fss", [P, TT])
        fve = sb("fve", [P, TT])
        frs = sb("frs", [P, TT])
        fsc = sb("fsc", [P, TT])
        z = sb("z", [P, 2, 8, DH])
        zm = sb("zm", [P, 2, 8, DH])
        rb1 = sb("rb1", [P, 2, P])
        rb2 = sb("rb2", [P, 2, P])
        ra1 = sb("ra1", [P, 2, P])
        ra2 = sb("ra2", [P, 2, P])
        r = sb("r", [P, 2, 8, DH])
        rsq = sb("rsq", [P, 8, DH])
        rss = sb("rss", [P, 2, 8])
        rrn = sb("rrn", [P, 2, 8])
        qk = sb("qk", [P, TT, 8, DH])
        vb = sb("vb", [P, TT, H2, DH])
        kT = sb("kT", [P, TT, 2, P])
        low = sb("low", [P, TT, H2, CH])
        xg = sb("xg", [P, TT, D])

        J = [bank(f"J{i}") for i in range(2)]
        X = [bank(f"X{i}") for i in range(2)]
        V = bank("V")
        K = bank("K")
        G = [bank(f"G{i}") for i in range(2)]

        loaded = sem("loaded")
        dve_chain = sem("dve_chain")
        pool_chain = sem("pool_chain")
        rot_ready = sem("rot_ready")

        with nc.Block() as block:
            N_LOADS = 13

            @block.sync
            def _(sp):
                loads = [(ident[:], a["c_ident"]), (conv[:], a["conv"]), (frac[:], a["L0_attn_frac_conv_w"]),
                         (cos[:], a["c_cos"]), (sin[:], a["c_sin"]), (rot[:], row(a["L0_attn_rot_logit"], H2)),
                         (mixw[:], row(a["L0_attn_mixer_norm_w"], D)), (strict[:], a["c_strict"]),
                         (smb[:, 2 * H2:], row(a["L0_attn_frac_gate_b"], 1))]
                for i, n in enumerate(("Wq", "Wk", "Wv")):
                    loads.append((wqkv[:, :, i * D:(i + 1) * D], a[f"L0_attn_{n}"].rearrange("(k p) n -> p k n", p=P)))
                loads.append((wsm[:], a["gates"]))
                assert len(loads) == N_LOADS
                for dst, src in loads:
                    sp.dma_start(dst, src).then_inc(loaded, 16)

            @block.scalar
            def _(act):
                act.wait_ge(loaded, 16 * N_LOADS)
                act.activation(rot[:], rot[:], ACT.Sigmoid).then_inc(rot_ready, 1)

            @block.gpsimd
            def _(pool):
                pool.memset(half[:], -0.5)
                pool.memset(h[:, :, 0:PAD], 0.0)
                pool.memset(proj[:, :, 0:3], 0.0)

            @block.vector
            def _(dve):
                link = Chain(dve, dve_chain)
                dve.memset(smb[:, 0:2 * H2], 0.0)
                dve.wait_ge(loaded, 16 * N_LOADS)
                link(dve.tensor_reduce(own[:], frac[:, :, :, 1], AX.X, ALU.add))
                dve.tensor_scalar(own[:], own[:], 2.0, None, ALU.add)
                dve.wait_ge(rot_ready, 1)
                for t in range(TT):
                    for table, mixed in ((cos, cm), (sin, sm)):
                        dve.tensor_tensor(mixed[:, t], table[:, t].unsqueeze(1).broadcast_to([P, H2, DH // 2]),
                                          rot[:].unsqueeze(2).broadcast_to([P, H2, DH // 2]), ALU.mult)
                dve.tensor_scalar(omx[:], rot[:].unsqueeze(2).broadcast_to([P, H2, DH]), -1.0, 1.0, ALU.mult, ALU.add)
        clear(nc, sems)

        h_in = sem("h_in")
        proj_psum = sem("proj_psum")
        proj_ready = sem("proj_ready")
        conv_ready = sem("conv_ready")
        y_ready = sem("y_ready")
        gates_psum = sem("gates_psum")
        gates_read = sem("gates_read")
        gates_ready = sem("gates_ready")
        nb_ready = sem("nb_ready")
        frac_ready = sem("frac_ready")
        fracT_psum = sem("fracT_psum")
        frac_sums = sem("frac_sums")
        frac_var = sem("frac_var")
        frac_scale = sem("frac_scale")
        xg_ready = sem("xg_ready")
        z_psum = sem("z_psum")
        z_ready = sem("z_ready")
        pool_rot = sem("pool_rot")
        r_ready = sem("r_ready")
        rsq_ready = sem("rsq_ready")
        rss_ready = sem("rss_ready")
        rrn_ready = sem("rrn_ready")
        qk_ready = sem("qk_ready")
        v_psum = sem("v_psum")
        vb_ready = sem("vb_ready")
        kT_psum = sem("kT_psum")
        kT_ready = sem("kT_ready")
        gram_psum = sem("gram_psum")
        low_ready = sem("low_ready")
        stored = sem("stored")

        ORDER = ([("J", i % 2, "proj", i) for i in range(6)] + [("K", 0, "gates", 0)]
                 + [("X", t % 2, "z", t) for t in range(TT)] + [("V", 0, "v", 0), ("V", 0, "v", 1)]
                 + [("J", 0, "frac", 0), ("J", 1, "frac", 1)])
        for t in range(TT):
            ORDER.append(("K", 0, "kT", t))
            if t % 2:
                ORDER += [("G", e, "gram", 2 * (t // 2) + e) for e in range(2)]

        def drained(step, n):
            return {"proj": [(proj_ready, n + 1)], "gates": [(gates_read, 1)], "z": [(z_ready, n + 1)],
                    "v": [(vb_ready, n + 1)], "frac": [(xg_ready, 2 * n + 2)], "kT": [(kT_ready, n + 1)],
                    "gram": [(low_ready, 4 * (n + 1))]}[step]

        before = drained_before([((name, i), step, n) for name, i, step, n in ORDER], drained)
        BANKS = {"J": J, "X": X, "V": [V], "K": [K], "G": G}

        with nc.Fori(0, B) as b:
            with nc.Block() as block:
                @block.sync
                def _(sp):
                    sp.dma_start(h[:, :, PAD:], hT_dram[bass.ds(b, 1), :, :, :].rearrange("o p k n -> (o p) k n")).then_inc(h_in, 16)
                    sp.dma_start(x[:], a["x"][bass.ds(b, 1), :, :].rearrange("o (t p) d -> p (o t) d", p=P)).then_inc(h_in, 16)
                    sp.wait_ge(gates_ready, 1)
                    sp.dma_start(bg_dram[bass.ds(b, 1), :, :].rearrange("o p n -> (o p) n"),
                                 gates[:].rearrange("p t n -> p (t n)")).then_inc(stored, 16)
                    sp.wait_ge(vb_ready, 2)
                    sp.dma_start(vb_dram[bass.ds(b, 1), :, :].rearrange("o p n -> (o p) n"),
                                 vb[:].rearrange("p t h d -> p (t h d)")).then_inc(stored, 16)
                    sp.wait_ge(xg_ready, TT)
                    sp.dma_start(xg_dram[bass.ds(b, 1), :, :].rearrange("o p n -> (o p) n"),
                                 xg[:].rearrange("p t d -> p (t d)")).then_inc(stored, 16)
                    sp.wait_ge(qk_ready, TT)
                    sp.dma_start(qk_dram[bass.ds(b, 1), :, :].rearrange("o p n -> (o p) n"),
                                 qk[:].rearrange("p t h d -> p (t h d)")).then_inc(stored, 16)
                    sp.wait_ge(low_ready, 16)
                    for c in range(NC4):
                        sp.dma_start(low_dram[bass.ds(b, 1), :, :, c].rearrange("o t h i j -> i (o t h) j"),
                                     low[c * CH:(c + 1) * CH].rearrange("p t h j -> p (t h) j")).then_inc(stored, 16)
                    sp.wait_ge(stored, 16 * (4 + NC4))

                @block.tensor
                def _(pe):
                    def fill(name, i, step, n):
                        for s, value in before[(name, i), step, n]:
                            pe.wait_ge(s, value)
                        return BANKS[name][i]

                    pe.wait_ge(h_in, 32)
                    for i in range(6):
                        o = fill("J", i % 2, "proj", i)
                        for k in range(KD):
                            last = pe.matmul(o[:, :], wqkv[:, k, i * P:(i + 1) * P], h[:, k, PAD:],
                                             start=k == 0, stop=k == KD - 1)
                        last.then_inc(proj_psum, 1)
                    o = fill("K", 0, "gates", 0)
                    n = 2 * H2 + 1
                    for t in range(TT):
                        for k in range(KD):
                            last = pe.matmul(o[:, t * n:(t + 1) * n], h[:, k, PAD + t * P:PAD + (t + 1) * P],
                                             wsm[:, k], start=k == 0, stop=k == KD - 1)
                    last.then_inc(gates_psum, 1)
                    for t in range(TT):
                        if t == 0:
                            pe.wait_ge(y_ready, 4)
                        o = fill("X", t % 2, "z", t)
                        for i in range(4):
                            last = pe.transpose(o[:, i * P:(i + 1) * P], y[:, i, t * P:(t + 1) * P], ident[:])
                        last.then_inc(z_psum, 1)
                    pe.wait_ge(y_ready, 6)
                    for g in range(2):
                        o = fill("V", 0, "v", g)
                        for tt in range(2):
                            for i in range(2):
                                t = 2 * g + tt
                                last = pe.transpose(o[:, tt * D + i * P:tt * D + (i + 1) * P],
                                                    y[:, 4 + i, t * P:(t + 1) * P], ident[:])
                        last.then_inc(v_psum, 1)
                    pe.wait_ge(frac_ready, KD)
                    for g in range(2):
                        o = fill("J", g, "frac", g)
                        for tt in range(2):
                            for k in range(KD):
                                t = 2 * g + tt
                                last = pe.transpose(o[:, tt * D + k * P:tt * D + (k + 1) * P],
                                                    fr[:, k, t * P:(t + 1) * P], ident[:])
                        last.then_inc(fracT_psum, 1)
                    for t in range(TT):
                        pe.wait_ge(qk_ready, t + 1)
                        o = fill("K", 0, "kT", t)
                        for i in range(2):
                            last = pe.transpose(o[:, i * P:(i + 1) * P],
                                                qk[:, t, H2 + 2 * i:H2 + 2 * i + 2].rearrange("p a d -> p (a d)"), ident[:])
                        last.then_inc(kT_psum, 1)
                        if t % 2:
                            pe.wait_ge(kT_ready, t + 1)
                            for e in range(2):
                                o = fill("G", e, "gram", 2 * (t // 2) + e)
                                part = slice(e * DH, (e + 1) * DH)
                                for tt in range(2):
                                    for i in range(2):
                                        keys = kT[part, t - 1 + tt, i]
                                        j = 2 * tt + i
                                        last = pe.matmul(o[:, j * P:(j + 1) * P], keys, keys, start=True, stop=True)
                                last.then_inc(gram_psum, 1)

                @block.scalar
                def _(act):
                    for i in range(6):
                        act.wait_ge(proj_psum, i + 1)
                        act.copy(proj[:, i, 3:], J[i % 2][:, :]).then_inc(proj_ready, 1)
                    act.wait_ge(gates_read, 1)
                    act.activation(gates[:], gates_in[:], ACT.Sigmoid).then_inc(gates_ready, 1)
                    for i in range(6):
                        act.wait_ge(conv_ready, i + 1)
                        act.activation(y[:, i], y[:, i], ACT.Silu).then_inc(y_ready, 1)
                    for t in range(TT + 1):
                        if t < TT:
                            act.wait_ge(z_psum, t + 1)
                            if t >= 2:
                                act.wait_ge(r_ready, t - 1)
                                act.wait_ge(pool_rot, t - 1)
                            act.copy(z[:, t % 2].rearrange("p a d -> p (a d)"), X[t % 2][:, :]).then_inc(z_ready, 1)
                        if t > 0:
                            act.wait_ge(r_ready, t)
                            if t > 1:
                                act.wait_ge(rss_ready, t - 1)
                            act.activation(rsq[:], r[:, (t - 1) % 2], ACT.Square).then_inc(rsq_ready, 1)
                    for t in range(TT):
                        act.wait_ge(fracT_psum, t // 2 + 1)
                        act.activation(fsq[:, t], J[t // 2][:, (t % 2) * D:(t % 2 + 1) * D], ACT.Square,
                                       accum_out=fss[:, t:t + 1]).then_inc(frac_sums, 1)
                    for t in range(TT):
                        act.wait_ge(kT_psum, t + 1)
                        act.copy(kT[:, t].rearrange("p a n -> p (a n)"), K[:, 0:2 * P]).then_inc(kT_ready, 1)

                @block.gpsimd
                def _(pool):
                    link = Chain(pool, pool_chain)
                    pool.wait_ge(h_in, 32)
                    for k in range(KD):
                        link(pool.tensor_scalar(fr[:, k], h[:, k, PAD:], own[:, k:k + 1], None, ALU.mult))
                        for i in range(4):
                            dil = 2 ** i
                            link(pool.tensor_scalar(ft[:], h[:, k, PAD - dil:PAD - dil + L], frac[:, k, i, 0:1], None,
                                                    ALU.mult))
                            ins = pool.tensor_tensor(fr[:, k], fr[:, k], ft[:], ALU.add)
                            if i < 3:
                                link(ins)
                        ins.then_inc(frac_ready, 1)
                        pool.wait_ge(frac_ready, k + 1)
                    pool.wait_ge(gates_ready, 1)
                    for t in range(TT):
                        ins = pool.tensor_tensor(nb[:, t], gates[:, t, 0:H2].unsqueeze(2).broadcast_to([P, H2, CH]),
                                                 strict[:].unsqueeze(1).broadcast_to([P, H2, CH]), ALU.mult)
                    ins.then_inc(nb_ready, 1)
                    for t in range(TT + 1):
                        if t < TT:
                            pool.wait_ge(z_ready, t + 1)
                            if t >= 2:
                                pool.wait_ge(r_ready, t - 1)
                            zt = z[:, t % 2].rearrange("p a (d two) -> p two (a d)", two=2)
                            x1, x2 = (zt[:, i].rearrange("p (q n) -> p q n", q=2) for i in range(2))
                            c, s = (m[:, t].rearrange("p h d -> p (h d)").unsqueeze(1).broadcast_to([P, 2, P])
                                    for m in (cm, sm))
                            pool.tensor_tensor(zm[:, t % 2].rearrange("p (q h) d -> p q (h d)", q=2),
                                               z[:, t % 2].rearrange("p (q h) d -> p q (h d)", q=2),
                                               omx[:].rearrange("p h d -> p (h d)").unsqueeze(1).broadcast_to([P, 2, 2 * P]),
                                               ALU.mult)
                            if t > 0:
                                pool.wait_ge(r_ready, t)
                            pool.tensor_tensor(rb1[:], x1, s, ALU.mult)
                            link(pool.tensor_tensor(rb2[:], x2, c, ALU.mult))
                            pool.tensor_tensor(rb1[:], rb1[:], rb2[:], ALU.add).then_inc(pool_rot, 1)
                        if t > 0:
                            pool.wait_ge(rss_ready, t)
                            if t > 2:
                                pool.wait_ge(qk_ready, t - 2)
                            pool.tensor_tensor(rrn[:, (t - 1) % 2], rss[:, (t - 1) % 2], half[:], ALU.pow).then_inc(rrn_ready, 1)
                    pool.wait_ge(frac_var, 1)
                    link(pool.tensor_tensor(frs[:], fve[:], half[:, 0:TT], ALU.pow))
                    pool.tensor_tensor(fsc[:], frs[:], gates[:, :, 2 * H2], ALU.mult).then_inc(frac_scale, 1)

                @block.vector
                def _(dve):
                    link = Chain(dve, dve_chain)

                    def gates_step():
                        dve.wait_ge(gates_psum, 1)
                        n = 2 * H2 + 1
                        dve.tensor_tensor(gates_in[:], K[:, 0:TT * n].rearrange("p (t n) -> p t n", n=n),
                                          smb[:].unsqueeze(1).broadcast_to([P, TT, n]), ALU.add).then_inc(gates_read, 1)

                    for i in range(6):
                        w = conv[:, i // 2, i % 2]
                        dve.wait_ge(proj_ready, i + 1)
                        link(dve.tensor_scalar(y[:, i], proj[:, i, 0:L], w[:, 0:1], None, ALU.mult))
                        for j in range(1, 4):
                            ins = dve.scalar_tensor_tensor(out=y[:, i], in0=proj[:, i, j:j + L], scalar=w[:, j:j + 1],
                                                           in1=y[:, i], op0=ALU.mult, op1=ALU.add)
                            if j < 3:
                                link(ins)
                        ins.then_inc(conv_ready, 1)
                        if i == 3:
                            gates_step()
                    for t in range(TT + 1):
                        if t < TT:
                            dve.wait_ge(z_ready, t + 1)
                            if t > 0:
                                dve.wait_ge(r_ready, t)
                            zt = z[:, t % 2].rearrange("p a (d two) -> p two (a d)", two=2)
                            x1, x2 = (zt[:, i].rearrange("p (q n) -> p q n", q=2) for i in range(2))
                            c, s = (m[:, t].rearrange("p h d -> p (h d)").unsqueeze(1).broadcast_to([P, 2, P])
                                    for m in (cm, sm))
                            dve.tensor_tensor(ra1[:], x1, c, ALU.mult)
                            link(dve.tensor_tensor(ra2[:], x2, s, ALU.mult))
                            link(dve.tensor_tensor(ra1[:], ra1[:], ra2[:], ALU.subtract))
                            dve.wait_ge(pool_rot, t + 1)
                            rt, zt = r[:, t % 2], zm[:, t % 2]
                            dve.tensor_tensor(rt[:, :, 0:CH], zt[:, :, 0:CH],
                                              ra1[:].rearrange("p q (h d) -> p (q h) d", d=CH), ALU.add)
                            dve.tensor_tensor(rt[:, :, CH:], zt[:, :, CH:],
                                              rb1[:].rearrange("p q (h d) -> p (q h) d", d=CH), ALU.add).then_inc(r_ready, 1)
                        if t > 0:
                            i = (t - 1) % 2
                            dve.wait_ge(rsq_ready, t)
                            link(dve.tensor_reduce(rss[:, i], rsq[:], AX.X, ALU.add))
                            dve.tensor_scalar(rss[:, i], rss[:, i], 1e-6, None, ALU.add).then_inc(rss_ready, 1)
                            dve.wait_ge(rrn_ready, t)
                            dve.tensor_tensor(qk[:, t - 1], r[:, i], rrn[:, i].unsqueeze(2).broadcast_to([P, 8, DH]),
                                              ALU.mult).then_inc(qk_ready, 1)
                        if t in (2, 3):
                            g = t - 2
                            dve.wait_ge(v_psum, g + 1)
                            dve.wait_ge(gates_ready, 1)
                            for tt in range(2):
                                ins = dve.tensor_tensor(vb[:, 2 * g + tt], V[:, tt * D:(tt + 1) * D].rearrange(
                                    "p (h d) -> p h d", d=DH),
                                    gates[:, 2 * g + tt, 0:H2].unsqueeze(2).broadcast_to([P, H2, DH]), ALU.mult)
                            ins.then_inc(vb_ready, 1)
                    dve.wait_ge(frac_sums, TT)
                    dve.tensor_scalar(fve[:], fss[:], 1.0 / D, 1e-5, ALU.mult, ALU.add).then_inc(frac_var, 1)
                    for n in range(4):
                        g, e = divmod(n, 2)
                        dve.wait_ge(gram_psum, n + 1)
                        dve.wait_ge(nb_ready, 1)
                        for c in range(NC4):
                            part = slice(c * CH, (c + 1) * CH)
                            hs = slice(e, H2, 2)
                            src = G[e][part, :].rearrange("p (t i n) -> p t i n", t=2, i=2)[:, :, :, part]
                            dve.tensor_tensor(low[part, 2 * g:2 * g + 2, hs], src, nb[part, 2 * g:2 * g + 2, hs],
                                              ALU.mult).then_inc(low_ready, 1)
                    dve.wait_ge(frac_scale, 1)
                    for t in range(TT):
                        link(dve.scalar_tensor_tensor(out=xg[:, t], in0=J[t // 2][:, (t % 2) * D:(t % 2 + 1) * D],
                                                      scalar=fsc[:, t:t + 1], in1=mixw[:], op0=ALU.mult, op1=ALU.mult))
                        dve.tensor_tensor(xg[:, t], xg[:, t], x[:, t], ALU.add).then_inc(xg_ready, 1)
            clear(nc, sems)


def inverse_phase(nc, a, low_dram, inv_dram):
    with ExitStack() as ctx:
        sb, bank, sem, sems = space(nc, ctx, "i")
        A = sb("A", [P, NC4, CH, CH])
        AT = sb("AT", [P, NC4, CH, CH])
        prod = sb("prod", [P, NC4, CH * CH])
        upd = sb("upd", [P, NC4, CH])
        eye = sb("eye", [P, CH, CH])
        loaded = sem("loaded")
        turned = sem("turned")
        stored = sem("stored")
        dve_chain = sem("dve_chain")
        pool_chain = sem("pool_chain")

        def substitute(eng, link, cs):
            n = cs.stop - cs.start
            for i in range(1, CH):
                own_row = A[:, cs, i, 0:i].unsqueeze(2).broadcast_to([P, n, i, i])
                above = A[:, cs, 0:i, 0:i].rearrange("p c j k -> p c k j")
                pr = prod[:, cs, 0:i * i].rearrange("p c (k j) -> p c k j", j=i)
                link(eng.tensor_tensor(pr, above, own_row, ALU.mult))
                link(eng.tensor_reduce(upd[:, cs, 0:i], pr, AX.X, ALU.add))
                link(eng.tensor_tensor(A[:, cs, i, 0:i], A[:, cs, i, 0:i], upd[:, cs, 0:i], ALU.add))

        with nc.Block() as block:
            @block.sync
            def _(sp):
                sp.dma_start(A[:], low_dram.rearrange("b t h c i j -> (b t h) c i j")).then_inc(loaded, 16)
                sp.dma_start(eye[:], a["c_eye32"]).then_inc(loaded, 16)
                sp.wait_ge(turned, NC4)
                sp.dma_start(inv_dram.rearrange("b t h c i j -> (b t h) c i j"), AT[:]).then_inc(stored, 16)
                sp.wait_ge(stored, 16)

            @block.vector
            def _(dve):
                link = Chain(dve, dve_chain)
                dve.wait_ge(loaded, 32)
                substitute(dve, link, slice(0, NC4))
                for c in range(NC4):
                    dve.tensor_tensor(AT[:, c], A[:, c].rearrange("p i j -> p j i"), eye[:], ALU.add).then_inc(turned, 1)
        clear(nc, sems)


def delta_rule_phase(nc, a, xg_dram, qk_dram, vb_dram, bg_dram, inv_dram, x1_dram):
    NG = 2 * H2 + 1
    with ExitStack() as ctx:
        sb, bank, sem, sems = space(nc, ctx, "d")
        ident = sb("ident", [P, P])
        causal = sb("causal", [P, P])
        chunk_of = sb("chunk_of", [P, NC4])
        wo = sb("wo", [P, KD, D])
        onw = sb("onw", [P, 1])
        eye = sb("eye", [P, DH])
        half = sb("half", [P, TT * H2])
        qk = sb("qk", [P, TT, 8, DH])
        vk = sb("vk", [P, TT, H2, 2, DH])
        gates = sb("gates", [P, TT, NG])
        xg = sb("xg", [P, TT, D])
        inv = sb("inv", [P, TT, H2, P])
        gx = sb("gx", [P, TT, H2, DH])
        gm = sb("gm", [P, TT, 2, NC4])
        gI = sb("gI", [P, TT, NC4, 2, DH])
        qkT = sb("qkT", [P, TT, 4, P])
        attn = sb("attn", [P, 2, TT, 2, P])
        uw = sb("uw", [P, TT, H2, 2, DH])
        qpT = sb("qpT", [P, TT, 2, P])
        MT = sb("MT", [P, TT, NC4, 2, DH])
        kb_u = sb("kb_u", [P, TT, NC4, 2, DH])
        S = sb("S", [P, NCH + 1, 2, DH])
        osq = sb("osq", [P, 2, TT * 2, DH])
        oss = sb("oss", [P, 2, TT * 2])
        ors = sb("ors", [P, 2, TT * 2])
        on = sb("on", [P, TT, H2, DH])
        onT = sb("onT", [P, KD, L])
        x1 = sb("x1", [P, TT, D])
        R = [bank(f"R{i}") for i in range(8)]

        loaded = sem("loaded")
        dve_chain = sem("dve_chain")
        with nc.Block() as block:
            @block.sync
            def _(sp):
                loads = [(ident[:], a["c_ident"]), (causal[:], a["c_causal"]), (chunk_of[:], a["c_chunk_of"]),
                         (wo[:], a["L0_attn_Wo"].rearrange("(k p) n -> p k n", p=P)),
                         (onw[0:DH], a["L0_attn_o_norm_w"].rearrange("(n o) -> n o", o=1)),
                         (onw[DH:P], a["L0_attn_o_norm_w"].rearrange("(n o) -> n o", o=1)),
                         (eye[0:DH], a["c_ident"][0:DH, 0:DH]), (eye[DH:P], a["c_ident"][0:DH, 0:DH])]
                for dst, src in loads:
                    sp.dma_start(dst, src).then_inc(loaded, 16)

            @block.gpsimd
            def _(pool):
                pool.memset(half[:], -0.5)
                pool.memset(inv[:], 0.0)
                pool.memset(S[:, 0], 0.0)

            @block.vector
            def _(dve):
                dve.wait_ge(loaded, 16 * 8)
                for k in range(KD):
                    dve.tensor_scalar(wo[:, k], wo[:, k], onw[:, 0:1], None, ALU.mult)
        clear(nc, sems)

        rows_in = sem("rows_in")
        inv_in = sem("inv_in")
        kb_ready = sem("kb_ready")
        gx_ready = sem("gx_ready")
        gm_psum = sem("gm_psum")
        gm_ready = sem("gm_ready")
        gI_ready = sem("gI_ready")
        qkT_psum = sem("qkT_psum")
        qkT_ready = sem("qkT_ready")
        attn_psum = sem("attn_psum")
        attn_ready = sem("attn_ready")
        uw_psum = sem("uw_psum")
        uw_ready = sem("uw_ready")
        qp_psum = sem("qp_psum")
        qp_ready = sem("qp_ready")
        step_psum = sem("step_psum")
        MT_ready = sem("MT_ready")
        ku_ready = sem("ku_ready")
        state_psum = [sem(f"state_psum{e}") for e in range(2)]
        state_ready = [sem(f"state_ready{e}") for e in range(2)]
        o_psum = sem("o_psum")
        osq_ready = sem("osq_ready")
        oss_ready = sem("oss_ready")
        ors_ready = sem("ors_ready")
        on_ready = sem("on_ready")
        onT_psum = sem("onT_psum")
        onT_ready = sem("onT_ready")
        core_psum = sem("core_psum")
        x1_ready = sem("x1_ready")
        stored = sem("stored")

        ORDER = [(t % 2, "qkT", t) for t in range(TT)]
        ORDER += [(2 + e, "attn", e) for e in range(2)] + [(t, "uw", t) for t in range(2)]
        ORDER += [(2 + e, "attn", 2 + e) for e in range(2)] + [(t % 2, "uw", t) for t in (2, 3)]
        ORDER += [(4, "gm", 0), (2, "qp", 0), (3, "qp", 1)]
        ORDER += [(4 + c, "step", 4 * g + c) for g in range(2) for c in range(NC4)]
        ORDER += [(e, "o", e) for e in range(2)] + [(2 + e, "state", e) for e in range(2)]
        ORDER += [(4 + k, "onT", k) for k in range(KD)] + [(6 + g, "core", g) for g in range(2)]

        def drained(step, n):
            return {"qkT": [(qkT_ready, n + 1)], "attn": [(attn_ready, n + 1)], "uw": [(uw_ready, n + 1)],
                    "gm": [(gm_ready, 1)], "qp": [(qp_ready, n + 1)],
                    "step": [(MT_ready, n + 1), (ku_ready, n + 1)]}[step]

        before = drained_before(ORDER, drained)

        with nc.Fori(0, B) as b:
            with nc.Block() as block:
                @block.sync
                def _(sp):
                    sp.dma_start(gates[:].rearrange("p t n -> p (t n)"),
                                 bg_dram[bass.ds(b, 1), :, :].rearrange("o p n -> (o p) n")).then_inc(rows_in, 16)
                    sp.dma_start(qk[:].rearrange("p t h d -> p (t h d)"),
                                 qk_dram[bass.ds(b, 1), :, :].rearrange("o p n -> (o p) n")).then_inc(rows_in, 16)
                    sp.dma_start(vk[:, :, :, 0], vb_dram[bass.ds(b, 1), :, :].rearrange(
                        "o p (t h d) -> (o p) t h d", h=H2, d=DH)).then_inc(rows_in, 16)
                    for c in range(NC4):
                        part = slice(c * CH, (c + 1) * CH)
                        sp.dma_start(inv[part, :, :, part].rearrange("p t h i -> p (t h) i"),
                                     inv_dram[bass.ds(b, 1), :, :, c].rearrange("o t h j i -> j (o t h) i")).then_inc(inv_in, 16)
                    sp.dma_start(xg[:].rearrange("p t d -> p (t d)"),
                                 xg_dram[bass.ds(b, 1), :, :].rearrange("o p n -> (o p) n")).then_inc(inv_in, 16)
                    for g in range(2):
                        sp.wait_ge(x1_ready, g + 1)
                        sp.dma_start(x1_dram[bass.ds(b, 1), g * 2 * P:(g + 1) * 2 * P, :].rearrange(
                            "o (t p) d -> p (o t) d", p=P), x1[:, 2 * g:2 * g + 2]).then_inc(stored, 16)
                    sp.wait_ge(stored, 32)

                @block.gpsimd
                def _(pool):
                    pool.wait_ge(rows_in, 48)
                    for t in range(TT):
                        pool.tensor_tensor(vk[:, t, :, 1], qk[:, t, H2:],
                                           gates[:, t, 0:H2].unsqueeze(2).broadcast_to([P, H2, DH]), ALU.mult)\
                            .then_inc(kb_ready, 1)
                    for t in range(TT):
                        ins = pool.tensor_copy(gx[:, t], gates[:, t, H2:2 * H2].unsqueeze(2).broadcast_to([P, H2, DH]))
                    ins.then_inc(gx_ready, 1)
                    pool.wait_ge(gm_ready, 1)
                    for t in range(TT):
                        for c in range(NC4):
                            ins = pool.tensor_tensor(gI[:, t, c], eye[:].unsqueeze(1).broadcast_to([P, 2, DH]),
                                                     gm[:, t, :, c].unsqueeze(2).broadcast_to([P, 2, DH]), ALU.mult)
                        ins.then_inc(gI_ready, 1)
                    pool.wait_ge(oss_ready, 1)
                    pool.tensor_tensor(ors[:].rearrange("p e n -> p (e n)"), oss[:].rearrange("p e n -> p (e n)"),
                                       half[:], ALU.pow).then_inc(ors_ready, 1)

                @block.tensor
                def _(pe):
                    def fill(i, step, n):
                        for s, value in before[i, step, n]:
                            pe.wait_ge(s, value)
                        return R[i]

                    pe.wait_ge(rows_in, 48)
                    for t in range(TT):
                        o = fill(t % 2, "qkT", t)
                        for i in range(4):
                            last = pe.transpose(o[:, i * P:(i + 1) * P],
                                                qk[:, t, 2 * i:2 * i + 2].rearrange("p a d -> p (a d)"), ident[:])
                        last.then_inc(qkT_psum, 1)

                    def attention(g):
                        pe.wait_ge(qkT_ready, 2 * g + 2)
                        for e in range(2):
                            o = fill(2 + e, "attn", 2 * g + e)
                            part = slice(e * DH, (e + 1) * DH)
                            for tt in range(2):
                                for i in range(2):
                                    t, j = 2 * g + tt, 2 * tt + i
                                    last = pe.matmul(o[:, j * P:(j + 1) * P], qkT[part, t, 2 + i], qkT[part, t, i],
                                                     start=True, stop=True)
                            last.then_inc(attn_psum, 1)

                    def solve(t):
                        if t == 0:
                            pe.wait_ge(inv_in, 16 * (NC4 + 1))
                        pe.wait_ge(kb_ready, t + 1)
                        o = fill(t % 2, "uw", t)
                        for h in range(H2):
                            last = pe.matmul(o[:, h * P:(h + 1) * P], inv[:, t, h],
                                             vk[:, t, h].rearrange("p a d -> p (a d)"), start=True, stop=True)
                        last.then_inc(uw_psum, 1)

                    attention(0)
                    solve(0)
                    solve(1)
                    attention(1)
                    solve(2)
                    solve(3)
                    pe.wait_ge(gx_ready, 1)
                    o = fill(4, "gm", 0)
                    for t in range(TT):
                        for i in range(2):
                            j = (2 * t + i) * NC4
                            last = pe.matmul(o[:, j:j + NC4], gx[:, t, 2 * i:2 * i + 2].rearrange("p a d -> p (a d)"),
                                             chunk_of[:], start=True, stop=True)
                    last.then_inc(gm_psum, 1)
                    for g in range(2):
                        pe.wait_ge(uw_ready, 2 * g + 2)
                        pe.wait_ge(attn_ready, 2 * g + 2)
                        o = fill(2 + g, "qp", g)
                        for tt in range(2):
                            for h in range(H2):
                                t, i, e = 2 * g + tt, h // 2, h % 2
                                last = pe.matmul(o[e * DH:(e + 1) * DH, (2 * tt + i) * P:(2 * tt + i + 1) * P],
                                                 uw[:, t, h, 1], attn[:, e, t, i], start=True, stop=True)
                        last.then_inc(qp_psum, 1)
                    for g in range(2):
                        for c in range(NC4):
                            o = fill(4 + c, "step", 4 * g + c)
                            part = slice(c * CH, (c + 1) * CH)
                            for tt in range(2):
                                for h in range(H2):
                                    t, i, e = 2 * g + tt, h // 2, h % 2
                                    keys = qk[part, t, H2 + h]
                                    at = 4 * tt + i
                                    for lhs, rhs, j in ((uw[part, t, h, 1], keys, at), (keys, uw[part, t, h, 0], at + 2)):
                                        last = pe.matmul(o[e * DH:(e + 1) * DH, j * DH:(j + 1) * DH], lhs, rhs,
                                                         start=True, stop=True, tile_position=(c * CH, e * DH))
                            last.then_inc(step_psum, 1)
                    for n in range(NCH):
                        t, c = divmod(n, NC4)
                        for e in range(2):
                            part = slice(e * DH, (e + 1) * DH)
                            if n > 0:
                                pe.wait_ge(state_ready[e], n)
                            if n < NCH - 1:
                                if n == 0:
                                    fill(2 + e, "state", e)
                                pe.wait_ge(MT_ready, 4 * (t // 2) + c + 1)
                                for i in range(2):
                                    last = pe.matmul(R[2 + e][part, i * DH:(i + 1) * DH], MT[part, t, c, i], S[part, n, i],
                                                     start=True, stop=True)
                                last.then_inc(state_psum[e], 1)
                            if n == 0:
                                fill(e, "o", e)
                                pe.wait_ge(qp_ready, 2)
                            for i in range(2):
                                o = R[e][:, (2 * t + i) * DH:(2 * t + i + 1) * DH]
                                if c == 0:
                                    pe.matmul(o, attn[:, e, t, i], uw[:, t, 2 * i + e, 0], start=i == 0, stop=False,
                                              skip_group_check=True)
                            for i in range(2):
                                o = R[e][:, (2 * t + i) * DH:(2 * t + i + 1) * DH]
                                last = pe.matmul(o[c * CH:(c + 1) * CH], qpT[part, t, i, c * CH:(c + 1) * CH], S[part, n, i],
                                                 start=False, stop=c == NC4 - 1, skip_group_check=True,
                                                 tile_position=(e * DH, c * CH))
                            if n == NCH - 1:
                                last.then_inc(o_psum, 1)
                    pe.wait_ge(on_ready, 2)
                    for k in range(KD):
                        o = fill(4 + k, "onT", k)
                        for t in range(TT):
                            last = pe.transpose(o[:, t * P:(t + 1) * P],
                                                on[:, t, 2 * k:2 * k + 2].rearrange("p a d -> p (a d)"), ident[:])
                        last.then_inc(onT_psum, 1)
                    pe.wait_ge(onT_ready, KD)
                    for g in range(2):
                        o = fill(6 + g, "core", g)
                        for tt in range(2):
                            for k in range(KD):
                                t = 2 * g + tt
                                last = pe.matmul(o[:, tt * D:(tt + 1) * D], onT[:, k, t * P:(t + 1) * P], wo[:, k],
                                                 start=k == 0, stop=k == KD - 1)
                        last.then_inc(core_psum, 1)

                @block.scalar
                def _(act):
                    for t in range(TT):
                        act.wait_ge(qkT_psum, t + 1)
                        act.copy(qkT[:, t].rearrange("p a n -> p (a n)"), R[t % 2][:, :]).then_inc(qkT_ready, 1)
                    for t in range(TT):
                        act.wait_ge(uw_psum, t + 1)
                        act.copy(uw[:, t].rearrange("p h a d -> p (h a d)"), R[t % 2][:, :]).then_inc(uw_ready, 1)
                    for n in range(2 * NC4):
                        g, c = divmod(n, NC4)
                        act.wait_ge(step_psum, n + 1)
                        act.wait_ge(MT_ready, n + 1)
                        act.copy(kb_u[:, 2 * g:2 * g + 2, c].rearrange("p t i d -> p t (i d)"),
                                 R[4 + c][:, :].rearrange("p (t s n) -> p t s n", t=2, s=2)[:, :, 1]).then_inc(ku_ready, 1)
                    for e in range(2):
                        act.wait_ge(o_psum, e + 1)
                        act.activation(osq[:, e].rearrange("p n d -> p (n d)"), R[e][:, :], ACT.Square).then_inc(osq_ready, 1)
                    act.wait_ge(onT_psum, 1)
                    act.copy(onT[:, 0], R[4][:, :]).then_inc(onT_ready, 1)

                @block.vector
                def _(dve):
                    link = Chain(dve, dve_chain)

                    def mask(n):
                        g, e = divmod(n, 2)
                        dve.wait_ge(attn_psum, n + 1)
                        dve.tensor_tensor(attn[:, e, 2 * g:2 * g + 2].rearrange("p t i n -> p (t i) n"),
                                          R[2 + e][:, :].rearrange("p (j n) -> p j n", n=P),
                                          causal[:].unsqueeze(1).broadcast_to([P, 4, P]), ALU.mult).then_inc(attn_ready, 1)

                    for n in range(4):
                        mask(n)
                    dve.wait_ge(gm_psum, 1)
                    dve.tensor_copy(gm[:].rearrange("p t i c -> p (t i c)"), R[4][:, 0:TT * 2 * NC4]).then_inc(gm_ready, 1)
                    for g in range(2):
                        dve.wait_ge(qp_psum, g + 1)
                        dve.wait_ge(qkT_ready, TT)
                        dve.scalar_tensor_tensor(out=qpT[:, 2 * g:2 * g + 2].rearrange("p t i n -> p t (i n)"),
                                                 in0=R[2 + g][:, :].rearrange("p (t n) -> p t n", t=2), scalar=-1.0,
                                                 in1=qkT[:, 2 * g:2 * g + 2, 0:2].rearrange("p t i n -> p t (i n)"),
                                                 op0=ALU.mult, op1=ALU.add).then_inc(qp_ready, 1)
                    for n in range(2 * NC4):
                        g, c = divmod(n, NC4)
                        dve.wait_ge(step_psum, n + 1)
                        dve.wait_ge(gI_ready, 2 * g + 2)
                        dve.tensor_tensor(MT[:, 2 * g:2 * g + 2, c].rearrange("p t i d -> p t (i d)"),
                                          gI[:, 2 * g:2 * g + 2, c].rearrange("p t i d -> p t (i d)"),
                                          R[4 + c][:, :].rearrange("p (t s n) -> p t s n", t=2, s=2)[:, :, 0],
                                          ALU.subtract).then_inc(MT_ready, 1)
                    for n in range(NCH - 1):
                        t, c = divmod(n, NC4)
                        for e in range(2):
                            part = slice(e * DH, (e + 1) * DH)
                            dve.wait_ge(state_psum[e], n + 1)
                            dve.wait_ge(ku_ready, 4 * (t // 2) + c + 1)
                            dve.tensor_tensor(S[part, n + 1].rearrange("p i d -> p (i d)"), R[2 + e][part, 0:2 * DH],
                                              kb_u[part, t, c].rearrange("p i d -> p (i d)"), ALU.add)\
                               .then_inc(state_ready[e], 1)
                    dve.wait_ge(osq_ready, 2)
                    link(dve.tensor_reduce(oss[:].rearrange("p e n -> p (e n)"),
                                           osq[:].rearrange("p e n d -> p (e n) d"), AX.X, ALU.add))
                    dve.tensor_scalar(oss[:], oss[:], 1.0 / DH, 1e-5, ALU.mult, ALU.add).then_inc(oss_ready, 1)
                    dve.wait_ge(ors_ready, 1)
                    for e in range(2):
                        dve.tensor_tensor(on[:].rearrange("p t (i e) d -> p (t i) e d", e=2)[:, :, e],
                                          R[e][:, :].rearrange("p (n d) -> p n d", d=DH),
                                          ors[:, e].unsqueeze(2).broadcast_to([P, TT * 2, DH]), ALU.mult).then_inc(on_ready, 1)
                    dve.wait_ge(onT_psum, 2)
                    dve.tensor_copy(onT[:, 1], R[5][:, :]).then_inc(onT_ready, 1)
                    for g in range(2):
                        ts = slice(2 * g, 2 * g + 2)
                        dve.wait_ge(core_psum, g + 1)
                        dve.tensor_tensor(x1[:, ts].rearrange("p t d -> p (t d)"), R[6 + g][:, :],
                                          xg[:, ts].rearrange("p t d -> p (t d)"), ALU.add).then_inc(x1_ready, 1)
            clear(nc, sems)


def rank_below(dve, link, out, vals, lower, gt, ge, n_rows, n, k):
    other = vals.unsqueeze(2).broadcast_to([P, n_rows, n, n])
    own = vals.unsqueeze(3).broadcast_to([P, n_rows, n, n])
    g = gt[:, 0:n_rows * n * n].rearrange("p (r e f) -> p r e f", e=n, f=n)
    q = ge[:, 0:n_rows * n * n].rearrange("p (r e f) -> p r e f", e=n, f=n)
    dve.tensor_tensor(g, other, own, ALU.is_gt)
    link(dve.tensor_tensor(q, other, own, ALU.is_ge))
    link(dve.tensor_tensor(q, q, lower[:, 0:n, 0:n].unsqueeze(1).broadcast_to([P, n_rows, n, n]), ALU.mult))
    link(dve.tensor_tensor(g, g, q, ALU.max))
    link(dve.tensor_reduce(out, g, AX.X, ALU.add))
    link(dve.tensor_scalar(out, out, float(k), None, ALU.is_lt))


def mixtures_phase(nc, a, x1_dram, out):
    with ExitStack() as ctx:
        sb, bank, sem, sems = space(nc, ctx, "m")
        ident = sb("ident", [P, P])
        ident16 = sb("ident16", [P, P], BF16)
        lower = sb("lower", [P, E2, E2])
        pick_in = sb("pick_in", [3 * E2, 2, 8, P])
        pick = sb("pick", [3 * E2, 2, 8, P], BF16)
        wt = sb("wt", [P, KD, E1])
        wg = sb("wg", [DH, E1])
        cond_now = sb("cond_now", [DH, 1])
        condb = sb("condb", [DH, P])
        wr = sb("wr", [P, KD, E2])
        cb = sb("cb", [P, E2])
        N1S, N1 = S1 // P, S1 // P + E1
        N2S, N2 = S2W // P, S2W // P + E2 // 2
        gate = [sb("gate1", [P, KD, N1, P]), sb("gate2", [P, KD, N2, P])]
        up = [sb("up1", [P, KD, N1, P]), sb("up2", [P, KD, N2, P])]
        down = [sb("down1", [P, N1, D]), sb("down2", [P, N2, D])]

        x1 = sb("x1", [P, TT, D])
        inT = [sb("x1T", [P, KD, L]), sb("yT", [P, KD, L])]
        lg = sb("lg", [P, TT, E2])
        mx = sb("mx", [P, TT])
        ex = sb("ex", [P, TT, E2])
        sc = sb("sc", [P, TT, E2])
        sbias = sb("sbias", [P, TT, E2])
        sel = sb("sel", [P, TT, E2])
        gsum = sb("gsum", [P, TT, G2])
        gsel = sb("gsel", [P, TT, G2])
        goff = sb("goff", [P, TT, G2])
        gt = sb("gt", [P, TT * E2 * E2])
        ge = sb("ge", [P, TT * E2 * E2])
        wsum = sb("wsum", [P, TT])
        w = sb("w", [P, TT, E2])
        rest = sb("rest", [P, TT, E2])
        parts = sb("parts", [P, TT, 3 * E2], BF16)
        wT = sb("wT", [3 * E2, L], BF16)
        act_g = sb("act_g", [P, 2, L])
        hid = sb("hid", [P, 3, L])
        outT = sb("outT", [P, KD, L])
        res = sb("res", [P, TT, D])

        GB = [bank(f"G{i}") for i in range(2)]
        UB = [bank(f"U{i}") for i in range(2)]
        YB = [bank(f"Y{i}") for i in range(2)]
        WB = bank("W")
        MB = bank("M")
        MB16 = MB[:, :].bitcast(BF16)

        loaded = sem("loaded")
        dve_chain = sem("dve_chain")

        with nc.Block() as block:
            @block.sync
            def _(sp):
                loads = [(ident[:], a["c_ident"]), (lower[:], a["c_lower"]), (pick_in[:], a["c_pick"]),
                         (wt[:], a["L0_cond2_wt"]), (wg[:], a["L0_cond2_wg"]),
                         (wr[:], a["L0_ffn_router_w"]), (cb[:], row(a["L0_ffn_correction_bias"], E2)),
                         (down[0][:, 0:N1S], a["L0_cond2_sw_down"].rearrange("(i p) n -> p i n", p=P)),
                         (down[0][:, N1S:], a["L0_cond2_w_down"].rearrange("e m n -> m e n")),
                         (down[1][:, 0:N2S], a["L0_ffn_shared_down_w"].rearrange("(i p) n -> p i n", p=P)),
                         (down[1][:, N2S:], a["L0_ffn_down_w"].rearrange("(i e) m n -> (e m) i n", e=2))]
                for k in range(KD):
                    ks = slice(k * P, (k + 1) * P)
                    for dst, shared, own in ((gate, ("L0_cond2_sw_gate", "L0_ffn_shared_gate_w"),
                                              ("L0_cond2_w_gate", "L0_ffn_gate_w")),
                                             (up, ("L0_cond2_sw_up", "L0_ffn_shared_up_w"),
                                              ("L0_cond2_w_up", "L0_ffn_up_w"))):
                        for m, ns in ((0, N1S), (1, N2S)):
                            loads.append((dst[m][:, k, 0:ns].rearrange("p i n -> p (i n)"), a[shared[m]][ks, :]))
                            width = (M1, M2)[m]
                            loads.append((dst[m][:, k, ns:].rearrange("p i n -> p (i n)").rearrange(
                                "p (e m) -> p e m", m=width), a[own[m]][:, ks, :].rearrange("e p m -> p e m")))
                for dst, src in loads:
                    sp.dma_start(dst, src).then_inc(loaded, 16)
                sp.wait_ge(loaded, 16 * len(loads))

            @block.vector
            def _(dve):
                dve.wait_ge(loaded, 16 * 27)
                dve.tensor_copy(ident16[:], ident[:])
                dve.tensor_copy(pick[:], pick_in[:])
        clear(nc, sems)

        x_in = sem("x_in")
        turned = sem("turned")
        inT_act = sem("inT_act")
        inT_dve = sem("inT_dve")
        condb_ready = sem("condb_ready")
        logits_psum = sem("logits_psum")
        logits_read = sem("logits_read")
        shifted = sem("shifted")
        exps_ready = sem("exps_ready")
        parts_ready = sem("parts_ready")
        wT_psum = sem("wT_psum")
        wT_ready = sem("wT_ready")
        gate_psum = sem("gate_psum")
        up_psum = sem("up_psum")
        weight_psum = sem("weight_psum")
        gate_active = sem("gate_active")
        mult_up = sem("mult_up")
        hid_ready = sem("hid_ready")
        hid_used = sem("hid_used")
        y_done = sem("y_done")
        res_ready = sem("res_ready")
        res_out = sem("res_out")

        ITEMS = [(0, i) for i in range(N1)] + [(1, i) for i in range(N2)]
        SHARED = (N1S, N2S)
        NI = (N1, N2)

        def routed(q):
            m, i = ITEMS[q]
            return i >= SHARED[m]

        def n_routed(q):
            return sum(routed(j) for j in range(q + 1))

        with nc.Fori(0, B) as b:
            with nc.Block() as block:
                @block.sync
                def _(sp):
                    sp.dma_start(x1[:], x1_dram[bass.ds(b, 1), :, :].rearrange("o (t p) d -> p (o t) d", p=P)).then_inc(x_in, 16)
                    sp.dma_start(cond_now[:], a["c_cond"][bass.ds(b, 1), :, :].rearrange("o n k -> (o n) k")).then_inc(x_in, 16)
                    for half_of in range(2):
                        sp.wait_ge(res_ready, half_of + 1)
                        ts = slice(2 * half_of, 2 * half_of + 2)
                        sp.dma_start(out[bass.ds(b, 1), half_of * 2 * P:(half_of + 1) * 2 * P, :].rearrange(
                            "o (t p) d -> p (o t) d", p=P), res[:, ts]).then_inc(res_out, 16)
                    sp.wait_ge(res_out, 32)

                @block.tensor
                def _(pe):
                    pe.wait_ge(x_in, 32)
                    for k in range(KD):
                        for t in range(TT):
                            last = pe.transpose(GB[k][:, t * P:(t + 1) * P], x1[:, t, k * P:(k + 1) * P], ident[:])
                        last.then_inc(turned, 1)

                    def router(m):
                        pe.wait_ge(inT_act, m + 1)
                        pe.wait_ge(inT_dve, m + 1)
                        if m == 0:
                            pe.wait_ge(condb_ready, 1)
                        n = (E1, E2)[m]
                        for t in range(TT):
                            o = MB[:, t * n:(t + 1) * n]
                            for k in range(KD):
                                last = pe.matmul(o, inT[m][:, k, t * P:(t + 1) * P], (wt, wr)[m][:, k],
                                                 start=k == 0, stop=m == 1 and k == KD - 1)
                            if m == 0:
                                last = pe.matmul(o, condb[:], wg[:], start=False, stop=True)
                        last.then_inc(logits_psum, 1)

                    def weights_turned(m):
                        pe.wait_ge(parts_ready, m + 1)
                        n = 3 * (E1, E2)[m]
                        for t in range(TT):
                            last = pe.transpose(MB16[0:n, t * P:(t + 1) * P], parts[:, t, 0:n], ident16[:])
                        last.then_inc(wT_psum, 1)

                    def project(q):
                        m, i = ITEMS[q]
                        if q >= 2:
                            pe.wait_ge(gate_active, q - 1)
                            pe.wait_ge(mult_up, q - 1)
                        for dst, wts, psum in ((GB, gate, gate_psum), (UB, up, up_psum)):
                            for k in range(KD):
                                last = pe.matmul(dst[q % 2][:, :], wts[m][:, k, i], inT[m][:, k],
                                                 start=k == 0, stop=k == KD - 1)
                            last.then_inc(psum, 1)

                    def spread(q):
                        m, i = ITEMS[q]
                        if i == SHARED[m]:
                            weights_turned(m)
                            pe.wait_ge(wT_ready, m + 1)
                        n = 3 * (E1, E2)[m]
                        if n_routed(q) > 1:
                            pe.wait_ge(hid_ready, n_routed(q) - 1)
                        pe.matmul(WB[:, :], pick[0:n, m, i - SHARED[m]], wT[0:n, :], start=True,
                                  stop=True).then_inc(weight_psum, 1)

                    def project_down(q):
                        m, i = ITEMS[q]
                        if routed(q):
                            pe.wait_ge(hid_ready, n_routed(q))
                        else:
                            pe.wait_ge(mult_up, q + 1)
                        if m == 1 and i == 0:
                            pe.wait_ge(inT_act, 2)
                            pe.wait_ge(inT_dve, 2)
                        for k in range(KD):
                            last = pe.matmul(YB[k][:, :], down[m][:, i, k * P:(k + 1) * P], hid[:, q % 3],
                                             start=i == 0, stop=i == NI[m] - 1)
                        last.then_inc(hid_used, 1)

                    for m in range(2):
                        first = 0 if m == 0 else N1
                        router(m)
                        for q in range(first, first + NI[m]):
                            project(q)
                            if routed(q):
                                spread(q)
                            if q > first:
                                project_down(q - 1)
                        project_down(first + NI[m] - 1)
                    pe.wait_ge(inT_act, 3)
                    pe.wait_ge(inT_dve, 3)
                    for half_of in range(2):
                        for tt in range(2):
                            t = 2 * half_of + tt
                            for k in range(KD):
                                last = pe.transpose(GB[half_of][:, tt * D + k * P:tt * D + (k + 1) * P],
                                                    outT[:, k, t * P:(t + 1) * P], ident[:])
                        last.then_inc(turned, 1)

                @block.scalar
                def _(act):
                    act.wait_ge(turned, 1)
                    act.copy(inT[0][:, 0], GB[0][:, :]).then_inc(inT_act, 1)

                    def exps(m):
                        act.wait_ge(shifted, m + 1)
                        n = (E1, E2)[m]
                        act.activation(ex[:, :, 0:n], lg[:, :, 0:n], ACT.Exp, scale=(1.0, -1.0)[m]).then_inc(exps_ready, 1)

                    for q, (m, i) in enumerate(ITEMS):
                        if i == 0:
                            exps(m)
                        act.wait_ge(gate_psum, q + 1)
                        if q >= 2:
                            act.wait_ge(mult_up, q - 1)
                        if m == 0:
                            act.copy(act_g[:, q % 2], GB[q % 2][:, :]).then_inc(gate_active, 1)
                        else:
                            act.activation(act_g[:, q % 2], GB[q % 2][:, :], ACT.Silu).then_inc(gate_active, 1)
                        if i == NI[m] - 1:
                            act.wait_ge(hid_used, q + 1)
                            act.copy((inT[1], outT)[m][:, 0], YB[0][:, :]).then_inc(inT_act, 1)

                @block.vector
                def _(dve):
                    link = Chain(dve, dve_chain)
                    dve.wait_ge(x_in, 32)
                    dve.tensor_copy(condb[:], cond_now[:].broadcast_to([DH, P])).then_inc(condb_ready, 1)
                    dve.wait_ge(turned, 2)
                    dve.tensor_copy(inT[0][:, 1], GB[1][:, :]).then_inc(inT_dve, 1)

                    def route(m):
                        n = (E1, E2)[m]
                        rows = TT
                        dve.wait_ge(logits_psum, m + 1)
                        psum = MB[:, 0:TT * n].rearrange("p (t e) -> p t e", e=n)
                        l, e, s = lg[:, :, 0:n], ex[:, :, 0:n], sc[:, :, 0:n]
                        chosen, wn = sel[:, :, 0:n], w[:, :, 0:n]
                        spread_rows = lambda v: v.unsqueeze(2).broadcast_to([P, TT, n])
                        if m == 0:
                            link(dve.tensor_scalar(l, psum, 0.5, None, ALU.mult))
                            link(dve.tensor_reduce(mx[:], l, AX.X, ALU.max))
                            dve.tensor_tensor(l, l, spread_rows(mx[:]), ALU.subtract).then_inc(shifted, 1)
                            dve.wait_ge(exps_ready, 1)
                            link(dve.tensor_reduce(wsum[:], e, AX.X, ALU.add))
                            link(dve.reciprocal(wsum[:], wsum[:]))
                            link(dve.tensor_tensor(s, e, spread_rows(wsum[:]), ALU.mult))
                            rank_below(dve, link, chosen, s, lower, gt, ge, TT, n, 2)
                        else:
                            dve.tensor_copy(l, psum).then_inc(shifted, 1)
                            dve.wait_ge(exps_ready, 2)
                            link(dve.tensor_scalar(e, e, 1.0, None, ALU.add))
                            link(dve.reciprocal(s, e))
                            link(dve.tensor_tensor(sbias[:], s, cb[:].unsqueeze(1).broadcast_to([P, TT, E2]), ALU.add))
                            in_groups = lambda v: v.rearrange("p t (g e) -> p (t g) e", g=G2)
                            rank_below(dve, link, in_groups(chosen), in_groups(sbias[:]), lower, gt, ge, TT * G2,
                                       E2 // G2, 2)
                            link(dve.tensor_tensor(rest[:], sbias[:], chosen, ALU.mult))
                            link(dve.tensor_reduce(gsum[:].rearrange("p t g -> p (t g)"), in_groups(rest[:]), AX.X, ALU.add))
                            rank_below(dve, link, gsel[:], gsum[:], lower, gt, ge, TT, G2, 2)
                            link(dve.tensor_scalar(goff[:], gsel[:], 1.0e30, -1.0e30, ALU.mult, ALU.add))
                            of_group = lambda v: v.rearrange("p t g -> p (t g)").unsqueeze(2).broadcast_to(
                                [P, TT * G2, E2 // G2])
                            link(dve.tensor_tensor(in_groups(sbias[:]), in_groups(sbias[:]), of_group(gsel[:]), ALU.mult))
                            link(dve.tensor_tensor(in_groups(sbias[:]), in_groups(sbias[:]), of_group(goff[:]), ALU.add))
                            rank_below(dve, link, chosen, sbias[:], lower, gt, ge, TT, n, 4)
                        link(dve.tensor_tensor(wn, s, chosen, ALU.mult))
                        link(dve.tensor_reduce(wsum[:], wn, AX.X, ALU.add))
                        link(dve.tensor_scalar(wsum[:], wsum[:], 1e-20, None, ALU.add))
                        link(dve.reciprocal(wsum[:], wsum[:]))
                        link(dve.tensor_tensor(wn, wn, spread_rows(wsum[:]), ALU.mult))
                        r = rest[:, :, 0:n]
                        link(dve.tensor_copy(parts[:, :, 0:n], wn))
                        link(dve.tensor_tensor(r, wn, parts[:, :, 0:n], ALU.subtract))
                        link(dve.tensor_copy(parts[:, :, n:2 * n], r))
                        link(dve.tensor_tensor(r, r, parts[:, :, n:2 * n], ALU.subtract))
                        dve.tensor_copy(parts[:, :, 2 * n:3 * n], r).then_inc(parts_ready, 1)

                    def take_weights(m):
                        n = 3 * (E1, E2)[m]
                        dve.wait_ge(wT_psum, m + 1)
                        if m == 1:
                            dve.wait_ge(weight_psum, E1)
                        dve.tensor_copy(wT[0:n, :], MB16[0:n, 0:L]).then_inc(wT_ready, 1)

                    for q, (m, i) in enumerate(ITEMS):
                        if i == 0:
                            route(m)
                        if i == SHARED[m]:
                            take_weights(m)
                        ag, h = act_g[:, q % 2], hid[:, q % 3]
                        dve.wait_ge(gate_active, q + 1)
                        if q >= 3:
                            dve.wait_ge(hid_used, q - 2)
                        if m == 0:
                            link(dve.scalar_tensor_tensor(out=ag, in0=ag, scalar=0.01, in1=ag, op0=ALU.mult, op1=ALU.max))
                        dve.wait_ge(up_psum, q + 1)
                        if routed(q):
                            dve.tensor_tensor(h, ag, UB[q % 2][:, :], ALU.mult).then_inc(mult_up, 1)
                            dve.wait_ge(mult_up, q + 1)
                            dve.wait_ge(weight_psum, n_routed(q))
                            dve.tensor_tensor(h, h, WB[:, :], ALU.mult).then_inc(hid_ready, 1)
                        else:
                            dve.tensor_tensor(h, ag, UB[q % 2][:, :], ALU.mult).then_inc(mult_up, 1)
                        if i == NI[m] - 1:
                            dve.wait_ge(hid_used, q + 1)
                            dve.tensor_copy((inT[1], outT)[m][:, 1], YB[1][:, :]).then_inc(inT_dve, 1)
                    for half_of in range(2):
                        ts = slice(2 * half_of, 2 * half_of + 2)
                        dve.wait_ge(turned, 3 + half_of)
                        dve.tensor_tensor(res[:, ts].rearrange("p t d -> p (t d)"), GB[half_of][:, :],
                                          x1[:, ts].rearrange("p t d -> p (t d)"), ALU.add).then_inc(res_ready, 1)
            clear(nc, sems)


def bass_adaln(nc, a, out, scratch):
    bias_phase(nc, a, scratch["bias_rows"])
    attention_phase(nc, a, scratch["bias_rows"], scratch["hT"])
    delta_inputs_phase(nc, a, scratch["hT"], scratch["xg"], scratch["qk"], scratch["vb"], scratch["gates"],
                       scratch["low"])
    inverse_phase(nc, a, scratch["low"], scratch["inv"])
    delta_rule_phase(nc, a, scratch["xg"], scratch["qk"], scratch["vb"], scratch["gates"], scratch["inv"],
                     scratch["x1"])
    mixtures_phase(nc, a, scratch["x1"], out)


def kernel(**inputs):
    import numpy as _np
    import concourse.bacc as _bacc
    from concourse import mybir as _mybir
    from concourse.bass_utils import run_bass_kernel_spmd as _run

    names = [n for n in inputs if n != "mask_BxS_bf1"]
    arrays = {n: _np.ascontiguousarray(inputs[n]) for n in names}
    for n in ("L0_cond_g_norm", "L0_cond_g_out"):
        arrays[n] = _np.ascontiguousarray(arrays[n].reshape(-1, P).T)
    arrays["mask"] = _np.ascontiguousarray(inputs["mask_BxS_bf1"]).view(_np.uint8)
    arrays["c_ident"] = _np.eye(P, dtype=_np.float32)
    arrays["c_turn"] = _np.ascontiguousarray(arrays["c_ident"][::-1])
    arrays["c_pos"] = (L - 1 - _np.arange(L).reshape(TT, P).T).astype(_np.float32)
    arrays["c_lower"] = _np.ascontiguousarray(_np.broadcast_to(_np.tril(_np.ones((E2, E2), _np.float32), -1), (P, E2, E2)))
    pick = _np.zeros((3 * E2, 2, 8, P), _np.float32)
    for s in range(3):
        for i in range(8):
            pick[E1 * s + i, 0, i, :] = 1
            for e in range(2):
                pick[E2 * s + 2 * i + e, 1, i, M2 * e:M2 * (e + 1)] = 1
    arrays["c_pick"] = pick
    arrays["c_cond"] = _np.ascontiguousarray(inputs["cond_64"][:, :, None])
    arrays["conv"] = _np.ascontiguousarray(_np.stack([inputs[f"L0_attn_conv_{n}"] for n in "qkv"])
                                           .reshape(3, KD, P, 4).transpose(2, 0, 1, 3))
    arrays["L0_attn_frac_conv_w"] = _np.ascontiguousarray(
        inputs["L0_attn_frac_conv_w"].reshape(4, KD, P, 2).transpose(2, 1, 0, 3))
    angle = _np.arange(L)[:, None] * (1.0 / 10000.0 ** (_np.arange(0, DH, 2) / DH))[None, :]
    for n, f in (("c_cos", _np.cos), ("c_sin", _np.sin)):
        arrays[n] = _np.ascontiguousarray(f(angle).astype(_np.float32).reshape(TT, P, -1).transpose(1, 0, 2))
    at = _np.arange(P)
    same = at[:, None] // CH == at[None, :] // CH
    arrays["c_causal"] = (same & (at[:, None] <= at[None, :])).astype(_np.float32)
    arrays["c_strict"] = -(at[:, None] % CH > _np.arange(CH)[None, :]).astype(_np.float32)
    arrays["c_chunk_of"] = ((at[:, None] // CH == _np.arange(NC4)[None, :]) / CH).astype(_np.float32)
    arrays["c_eye32"] = _np.ascontiguousarray(_np.broadcast_to(_np.eye(CH, dtype=_np.float32), (P, CH, CH)))
    gates = _np.concatenate([inputs[f"L0_attn_{n}"] for n in ("Wb", "Wgamma", "frac_gate_w")], axis=1)
    arrays["gates"] = _np.ascontiguousarray(gates.reshape(KD, P, -1).transpose(1, 0, 2))
    for n in ("L0_cond2_wt", "L0_ffn_router_w"):
        arrays[n] = _np.ascontiguousarray(arrays[n].T.reshape(KD, P, -1).transpose(1, 0, 2))
    arrays["L0_cond2_wg"] = _np.ascontiguousarray(arrays["L0_cond2_wg"].T)
    for n in ("gate", "up", "down"):
        n = f"L0_ffn_shared_{n}_w"
        arrays[n] = _np.ascontiguousarray(arrays[n].T)
    nc = _bacc.Bacc("TRN2", target_bir_lowering=False, num_devices=1)
    a = {}
    fed = {}
    for n, v in arrays.items():
        a[n] = nc.dram_tensor(f"in_{n}", v.shape, _mybir.dt.from_np(v.dtype), kind="ExternalInput").ap()
        fed[f"in_{n}"] = v
    out = nc.dram_tensor("out", [B, L, D], _mybir.dt.float32, kind="ExternalOutput").ap()
    shapes = {"bias_rows": [NH, BIAS_W + 1], "hT": [B, P, KD, L], "xg": [B, P, TT * D], "qk": [B, P, TT * 2 * D],
              "vb": [B, P, TT * D], "gates": [B, P, TT * (2 * H2 + 1)], "low": [B, TT, H2, NC4, CH, CH],
              "inv": [B, TT, H2, NC4, CH, CH], "x1": [B, L, D]}
    scratch = {n: nc.dram_tensor(f"s_{n}", shape, _mybir.dt.float32, kind="Internal").ap() for n, shape in shapes.items()}
    bass_adaln(nc, a, out, scratch)
    r = _run(nc, [fed], core_ids=[0])
    return r.results[0]["out"]
```

```python
from contextlib import ExitStack

import numpy as np
import concourse.bass as bass
from concourse import mybir

F32 = mybir.dt.float32
BF16 = mybir.dt.bfloat16
ALU = mybir.AluOpType
ACT = mybir.ActivationFunctionType
AX = mybir.AxisListType

P = 128
B, L, D = 8, 512, 256
KD = D // P
TT = L // P
NH, DH = 16, 64
QT = NH // 2
QW = NH * DH
SCALE = 8.0
NEG = float(-np.finfo(np.float32).max)
MASKED = -1.0e30
BIAS_W = L + P - 1

H2, CH, NC4 = 4, 32, 4
NCH = L // CH
E1, M1 = 8, 128
S1 = 256
E2, M2 = 16, 64
S2W = 512
G2 = 4


class Chain:

    def __init__(self, eng, sem):
        self.eng, self.sem, self.n = eng, sem, 0

    def __call__(self, ins):
        self.n += 1
        ins.then_inc(self.sem, 1)
        self.eng.wait_ge(self.sem, self.n)


def clear(nc, sems):
    with nc.Block() as block:
        @block.sync
        def _(sp):
            for s in sems:
                sp.sem_clear(s)


def space(nc, ctx, prefix):
    sems = []

    def sb(name, shape, dt=F32):
        return ctx.enter_context(nc.sbuf_tensor(f"{prefix}_{name}", shape, dt))

    def bank(name, dt=F32):
        return ctx.enter_context(nc.psum_tensor(f"{prefix}_{name}", [P, 2048 // (2 if dt == BF16 else 4)], dt))

    def sem(name):
        s = ctx.enter_context(nc.semaphore(f"{prefix}_{name}"))
        sems.append(s)
        return s

    return sb, bank, sem, sems


def row(ap, n):
    return bass.AP(tensor=ap.tensor, offset=ap.offset, ap=[[0, P], [1, n]])


def bias_phase(nc, a, bias_rows):
    with ExitStack() as ctx:
        sb, bank, sem, sems = space(nc, ctx, "r")
        pos = sb("pos", [P, TT])
        ident = sb("ident", [P, P])
        w0, b0, g0, b1, g1 = (sb(n, [P, D]) for n in ("w0", "b0", "g0", "b1", "g1"))
        w1 = sb("w1", [P, KD, D])
        w2 = sb("w2", [P, KD, NH])
        b2 = sb("b2", [NH, 1])
        h = sb("h", [P, TT, D])
        hn = sb("hn", [P, TT, D])
        hT = sb("hT", [P, KD, L])
        stats = sb("stats", [P, TT, 6])
        mv = sb("mv", [P, TT, 2])
        ve = sb("ve", [P, TT])
        half = sb("half", [P, TT])
        rstd = sb("rstd", [P, TT])
        rows = sb("rows", [NH, BIAS_W + 1])
        ps = [bank(f"ps{i}") for i in range(4)]

        loaded = sem("loaded")
        half_ready = sem("half_ready")
        var_ready = sem("var_ready")
        rstd_ready = sem("rstd_ready")
        h_normed = sem("h_normed")
        h_active = sem("h_active")
        hT_psum = sem("hT_psum")
        hT_ready = sem("hT_ready")
        prod_psum = sem("prod_psum")
        rows_ready = sem("rows_ready")
        rows_out = sem("rows_out")
        dve_chain = sem("dve_chain")

        with nc.Block() as block:
            @block.sync
            def _(sp):
                loads = [(pos[:], a["c_pos"]), (ident[:], a["c_ident"]), (w0[:], row(a["L0_cond_w0"], D)),
                         (b0[:], row(a["L0_cond_b0"], D)), (g0[:], row(a["L0_cond_g0"], D)),
                         (b1[:], row(a["L0_cond_b1"], D)), (g1[:], row(a["L0_cond_g1"], D)),
                         (w1[:], a["L0_cond_w1"].rearrange("(k p) n -> p k n", p=P)),
                         (w2[:], a["L0_cond_w2"].rearrange("(k p) n -> p k n", p=P)),
                         (b2[:], a["L0_cond_b2"].rearrange("(n o) -> n o", o=1))]
                for dst, src in loads:
                    sp.dma_start(dst, src).then_inc(loaded, 16)
                sp.wait_ge(rows_ready, 1)
                sp.dma_start(bias_rows[:, :], rows[:, :]).then_inc(rows_out, 16)
                sp.wait_ge(rows_out, 16)

            N_LOADS = 160

            @block.gpsimd
            def _(pool):
                pool.memset(half[:], -0.5).then_inc(half_ready, 1)
                pool.wait_ge(half_ready, 1)
                for layer in range(2):
                    pool.wait_ge(var_ready, layer + 1)
                    pool.tensor_tensor(rstd[:], ve[:], half[:], ALU.pow).then_inc(rstd_ready, 1)

            @block.vector
            def _(dve):
                link = Chain(dve, dve_chain)
                link(dve.memset(rows[:, L:], NEG))
                dve.wait_ge(loaded, N_LOADS)
                for layer in range(2):
                    gain = (g0, g1)[layer]
                    if layer == 0:
                        for t in range(TT):
                            last = dve.scalar_tensor_tensor(out=h[:, t], in0=w0[:], scalar=pos[:, t:t + 1],
                                                            in1=b0[:], op0=ALU.mult, op1=ALU.add)
                        link(last)
                    else:
                        for t in range(TT):
                            dve.wait_ge(prod_psum, t + 1)
                            last = dve.tensor_tensor(h[:, t], ps[t][:, 0:D], b1[:], ALU.add)
                        link(last)
                    for t in range(TT):
                        last = dve.bn_stats(stats[:, t], h[:, t])
                    link(last)
                    for t in range(TT):
                        last = dve.bn_aggr(mv[:, t], stats[:, t])
                    link(last)
                    dve.tensor_scalar(ve[:], mv[:, :, 1], 1e-5, None, ALU.add).then_inc(var_ready, 1)
                    dve.wait_ge(rstd_ready, layer + 1)
                    for t in range(TT):
                        last = dve.tensor_scalar(hn[:, t], h[:, t], mv[:, t, 0:1], rstd[:, t:t + 1],
                                                 ALU.subtract, ALU.mult)
                    link(last)
                    for t in range(TT):
                        last = dve.tensor_tensor(hn[:, t], hn[:, t], gain[:], ALU.mult)
                    last.then_inc(h_normed, 1)
                    for k in range(KD):
                        dve.wait_ge(hT_psum, KD * layer + k + 1)
                        dve.tensor_copy(hT[:, k], ps[k][:, :]).then_inc(hT_ready, 1)
                dve.wait_ge(prod_psum, TT + 1)
                dve.tensor_scalar(rows[:, 0:L], ps[2][0:NH, :], b2[:, 0:1], None, ALU.add).then_inc(rows_ready, 1)

            @block.scalar
            def _(act):
                for layer in range(2):
                    act.wait_ge(h_normed, layer + 1)
                    act.activation(hn[:], hn[:], ACT.Silu).then_inc(h_active, 1)

            @block.tensor
            def _(pe):
                pe.wait_ge(loaded, N_LOADS)
                for layer in range(2):
                    pe.wait_ge(h_active, layer + 1)
                    for k in range(KD):
                        for t in range(TT):
                            last = pe.transpose(ps[k][:, t * P:(t + 1) * P], hn[:, t, k * P:(k + 1) * P], ident[:])
                        last.then_inc(hT_psum, 1)
                    pe.wait_ge(hT_ready, KD * (layer + 1))
                    if layer == 0:
                        for t in range(TT):
                            for k in range(KD):
                                last = pe.matmul(ps[t][:, 0:D], hT[:, k, t * P:(t + 1) * P], w1[:, k],
                                                 start=k == 0, stop=k == KD - 1)
                            last.then_inc(prod_psum, 1)
                    else:
                        for k in range(KD):
                            last = pe.matmul(ps[2][0:NH, :], w2[:, k], hT[:, k], start=k == 0, stop=k == KD - 1)
                        last.then_inc(prod_psum, 1)
        clear(nc, sems)


def attention_phase(nc, a, bias_rows, hT_dram):
    QK_LAG, PV_LAG, S_SLOTS, PT_SLOTS = 3, 5, 5, 3
    F32R = mybir.dt.float32r
    with ExitStack() as ctx:
        sb, bank, sem, sems = space(nc, ctx, "a")
        ident = sb("ident", [P, P])
        turn = sb("turn", [P, P])
        w_in = sb("w_in", [P, QW + 2 * DH])
        wqkv = [sb(f"wqkv{i}", [P, KD, QW + 2 * DH], F32R) for i in range(2)]
        wout = sb("wout", [P, QT, D])
        bias = sb("bias", [P, NH, L])
        gn = sb("gn", [P, KD])
        go = sb("go", [P, KD])
        kscale = sb("kscale", [P, 3])
        nullf = sb("nullf", [P, 1])
        nullk = [sb(f"nullk{i}", [P, 2], F32R) for i in range(2)]
        nullv = sb("nullv", [P, DH])
        nullb = sb("nullb", [P, NH])
        nkrow = sb("nkrow", [1, 3 * DH])
        half = sb("half", [P, NH + 2])
        ones = sb("ones", [1, P], BF16)
        mask_in = sb("mask_in", [1, L], mybir.dt.uint8)
        mask_row = sb("mask_row", [1, L], BF16)

        x = sb("x", [P, TT, D])
        stats = sb("stats", [P, 6])
        mv = sb("mv", [P, 2])
        ve = sb("ve", [P, 1])
        rstd = sb("rstd", [P, 1])
        xn = sb("xn", [P, D])
        xnT = [sb(f"xnT{i}", [P, KD, P], F32R) for i in range(2)]
        qraw = sb("qraw", [P, NH + 1, DH])
        sq = sb("sq", [P, NH + 1, DH])
        ss = sb("ss", [P, NH + 1])
        rr = sb("rr", [P, NH + 1])
        qn = sb("qn", [P, NH, DH])
        kn = sb("kn", [P, 2, DH])
        qs = sb("qs", [P, NH, 2, DH], F32R)
        qT = sb("qT", [P, 2, NH, P], F32R)
        kf = sb("kf", [P, P])
        kT = [sb(f"kT{i}", [P, L], F32R) for i in range(2)]
        v = sb("v", [P, TT, DH])
        k_next = [sb(f"k_next{i}", [P, P], F32R) for i in range(2)]
        v_next = sb("v_next", [P, DH])
        nsn = sb("nsn", [P, 2, NH])
        S = sb("S", [P, S_SLOTS, L])
        PT = sb("PT", [P, PT_SLOTS, L])
        nm = sb("nm", [P, 2, NH])
        den = sb("den", [P, 2, NH])
        dn = sb("dn", [P, 2, NH // 2])
        pn = sb("pn", [P, 2, NH // 2])
        dent = sb("dent", [P, 2, NH // 2])
        rden = sb("rden", [P, 2, NH // 2])
        pnr = sb("pnr", [P, 2, NH // 2])
        onull = sb("onull", [P, NH, DH])
        o = sb("o", [P, NH, DH])
        oT = sb("oT", [P, QT, P])
        stats2 = sb("stats2", [P, 6])
        mv2 = sb("mv2", [P, 2])
        ve2 = sb("ve2", [P, 1])
        rstd2 = sb("rstd2", [P, 1])
        hn = sb("hn", [P, D])
        hT = sb("hT", [P, TT, KD, P])

        SB = [bank(f"S{i}") for i in range(2)]
        TB = [bank(f"T{i}") for i in range(2)]
        OB = [bank(f"O{i}") for i in range(2)]
        FB = [bank(f"F{i}") for i in range(2)]

        loaded = sem("loaded")
        w_loaded = sem("w_loaded")
        wout_loaded = sem("wout_loaded")
        w_split = sem("w_split")
        prep = sem("prep")
        prep_psum = sem("prep_psum")
        bias_psum = sem("bias_psum")
        bias_act = sem("bias_act")
        bias_dve = sem("bias_dve")
        dve_chain = sem("dve_chain")
        pool_chain = sem("pool_chain")

        with nc.Block() as block:
            N_LOADS = 14

            @block.sync
            def _(sp):
                toeplitz = bass.AP(tensor=bias_rows.tensor, offset=0, ap=[[1, P], [BIAS_W + 1, NH], [1, L]])
                loads = [(turn[:], a["c_turn"]), (bias[:], toeplitz), (ident[:], a["c_ident"]),
                         (gn[:], a["L0_cond_g_norm"]), (go[:], a["L0_cond_g_out"]),
                         (kscale[0:DH, 0:1], a["L0_cond_q_scale"].rearrange("(n o) -> n o", o=1)),
                         (kscale[DH:P, 0:1], a["L0_cond_q_scale"].rearrange("(n o) -> n o", o=1)),
                         (kscale[0:DH, 1:2], a["L0_cond_k_scale"].rearrange("(n o) -> n o", o=1)),
                         (kscale[DH:P, 1:2], a["L0_cond_k_scale"].rearrange("(n o) -> n o", o=1)),
                         (nullv[:], row(a["cond_64"][1, :], DH)),
                         (nullb[:], row(a["L0_cond_null_attn_bias"], NH)),
                         (nkrow[:, 0:DH], a["cond_64"][0:1, :]),
                         (x[:], a["x"][0].rearrange("(t p) d -> p t d", p=P)),
                         (mask_in[:], a["mask"][0:1, :])]
                assert len(loads) == N_LOADS
                for dst, src in loads:
                    sp.dma_start(dst, src).then_inc(loaded, 16)
                for k in range(KD):
                    if k > 0:
                        sp.wait_ge(w_split, k)
                    sp.dma_start(w_in[:, 0:QW], a["L0_cond_Wq"][k * P:(k + 1) * P, :]).then_inc(w_loaded, 16)
                    sp.dma_start(w_in[:, QW:], a["L0_cond_Wkv"][k * P:(k + 1) * P, :]).then_inc(w_loaded, 16)
                sp.dma_start(wout[:], a["L0_cond_Wout"].rearrange("(k p) n -> p k n", p=P)).then_inc(wout_loaded, 16)
                sp.wait_ge(wout_loaded, 16)

            @block.gpsimd
            def _(pool):
                for tile in (nsn, nm, pn, rden, onull, o):
                    pool.memset(tile[:], 0.0)
                pool.memset(den[:], 1.0)
                pool.memset(half[:], -0.5).then_inc(pool_chain, 1)
                pool.wait_ge(prep, 1)
                pool.wait_ge(pool_chain, 1)
                pool.tensor_tensor(nkrow[:, 2 * DH + 2:2 * DH + 3], nkrow[:, 2 * DH + 1:2 * DH + 2],
                                   half[0:1, 0:1], ALU.pow).then_inc(pool_chain, 1)

            @block.vector
            def _(dve):
                link = Chain(dve, dve_chain)
                dve.memset(ones[:], 1.0)
                dve.wait_ge(loaded, 16 * N_LOADS)
                link(dve.tensor_scalar(kscale[:, 2:3], kscale[:, 0:1], kscale[:, 1:2], SCALE, ALU.mult, ALU.mult))
                link(dve.tensor_tensor_reduce(nkrow[:, DH:2 * DH], nkrow[:, 0:DH], nkrow[:, 0:DH], 1.0, 0.0,
                                              ALU.mult, ALU.add, nkrow[:, 2 * DH:2 * DH + 1]))
                dve.tensor_scalar(nkrow[:, 2 * DH + 1:2 * DH + 2], nkrow[:, 2 * DH:2 * DH + 1], 1e-24, None,
                                  ALU.max).then_inc(prep, 1)
                dve.wait_ge(pool_chain, 2)
                for half_of in range(2):
                    last = dve.tensor_scalar(S[0:1, 0, half_of * DH:(half_of + 1) * DH], nkrow[:, 0:DH],
                                             nkrow[:, 2 * DH + 2:2 * DH + 3], None, ALU.mult)
                last.then_inc(prep, 1)
                dve.wait_ge(prep_psum, 1)
                link(dve.tensor_scalar(nullf[:], FB[0][:, 0:1], kscale[:, 2:3], None, ALU.mult))
                link(dve.tensor_copy(nullk[0][:], nullf[:].broadcast_to([P, 2])))
                dve.tensor_tensor(nullk[1][:], nullf[:].broadcast_to([P, 2]), nullk[0][:].bitcast(F32), ALU.subtract)
                for h in range(1, NH, 2):
                    dve.wait_ge(bias_psum, h + 1)
                    dve.tensor_copy(bias[:, h], (SB + TB)[h % 4][:, :]).then_inc(bias_dve, 1)
                for k in range(KD):
                    dve.wait_ge(w_loaded, 32 * (k + 1))
                    link(dve.tensor_scalar(w_in[:], w_in[:], gn[:, k:k + 1], None, ALU.mult))
                    link(dve.tensor_copy(wqkv[0][:, k], w_in[:]))
                    dve.tensor_tensor(wqkv[1][:, k], w_in[:], wqkv[0][:, k].bitcast(F32), ALU.subtract)\
                       .then_inc(w_split, 1)

            @block.tensor
            def _(pe):
                pe.wait_ge(loaded, 16 * N_LOADS)
                pe.wait_ge(prep, 2)
                pe.matmul(FB[0][:, 0:1], S[0:1, 0, 0:P], ident[0:1, 0:1], start=True, stop=True).then_inc(prep_psum, 1)
                for n in range(2 * TT):
                    pe.matmul(OB[n // TT][:, n % TT * P:(n % TT + 1) * P], ident[:], ident[:], start=True, stop=True)
                for h in range(NH):
                    if h >= 4:
                        pe.wait_ge((bias_act, bias_dve)[h % 2], (h - 4) // 2 + 1)
                    pe.matmul((SB + TB)[h % 4][:, :], turn[:], bias[:, h], start=True, stop=True).then_inc(bias_psum, 1)

            @block.scalar
            def _(act):
                for h in range(0, NH, 2):
                    act.wait_ge(bias_psum, h + 1)
                    act.copy(bias[:, h], (SB + TB)[h % 4][:, :]).then_inc(bias_act, 1)
        clear(nc, sems)

        names = ["x_first", "x_rest", "mask_read", "mask_in_next", "next_taken", "x_var", "x_rstd", "xn_ready",
                 "xnT_high", "xnT_low", "q_ready", "kv_ready", "sq_ready", "ss_ready", "rr_ready", "qn_ready",
                 "q_high", "q_low", "kn_ready", "qT_act", "qT_dve", "kT_read", "kT_ready", "null_ready",
                 "scores_psum", "scores_ready", "probs_ready", "probsT_psum", "probsT_act", "probsT_dve", "pv_done",
                 "null_diff", "null_probs", "weights_ready", "onull_ready", "o_scaled", "o_ready", "oT_act",
                 "oT_dve", "out_var", "out_rstd", "hn_ready", "hT_ready", "hT_out"]
        s = {n: sem(n) for n in names}
        full = [sem(f"F{i}_filled") for i in range(2)]

        NEXT = {0: ["stat"], 1: ["xn"], 2: ["xT"], 3: ["q0"], 4: ["q1"], 5: ["kv"], 6: ["ss"], 8: ["qn"],
                12: ["qT0", "qT1"], 13: ["qT2"], 14: ["qT3", "kT"], 15: ["null"]}
        LAST = {5: ["weigh1"], 8: ["oT"], 9: ["outp"], 11: ["hn"], 12: ["hT"]}
        OWN = {13: ["weigh0"]}

        def iteration():
            steps = []
            for t in range(TT):
                for h in range(NH):
                    steps.append(("head", NH * t + h))
                    steps += [(n, t) for n in OWN.get(h, [])]
                    steps += [(n, t - 1) for n in LAST.get(h, [])]
                    steps += [(n, t + 1) for n in NEXT.get(h, [])]
            return steps + [("head", NH * TT + i) for i in range(PV_LAG)]

        FILLS = {"xT": 0, "q0": 1, "q1": 0, "kv": 1, "qT0": 0, "qT1": 1, "qT2": 0, "qT3": 1, "kT": 0, "null": 1,
                 "outp": 0, "hT": 1}

        def evac_by_dve(n):
            return n % 4 == 3

        def count_dve(n):
            return (n + 1) // 4

        def run(steps, b):
            number, seen = {}, {}
            for name, t in steps:
                seen[name] = seen.get(name, 0) + 1
                number[name, t] = seen[name]

            def done(name, t):
                return number.get((name, t), 0)

            def drained(name, t):
                n = done(name, t)
                return {"xT": [(s["xnT_low"], n)], "q0": [(s["q_ready"], 2 * n - 1)],
                        "q1": [(s["q_ready"], 2 * n)], "kv": [(s["kv_ready"], 2 * n), (s["sq_ready"], 3 * n)],
                        "qT0": [(s["qT_act"], 2 * n - 1)], "qT1": [(s["qT_dve"], 2 * n - 1)],
                        "qT2": [(s["qT_act"], 2 * n)], "qT3": [(s["qT_dve"], 2 * n)],
                        "kT": [(s["kT_read"], n)], "null": [(s["null_ready"], n)],
                        "oT": None, "outp": [(s["hn_ready"], n)], "hT": [(s["hT_ready"], n)]}[name]

            filling, before, held = {}, {}, [[], []]
            for name, t in steps:
                for n in ([0, 1] if name == "oT" else [FILLS[name]] if name in FILLS else []):
                    filling[name, t, n] = len(held[n]) + 1
                    before[name, t, n] = held[n][-1] if held[n] else None
                    held[n].append((name, t))

            heads = [t for name, t in steps if name == "head"]
            with nc.Block() as block:
                @block.sync
                def _(sp):
                    if heads:
                        sp.dma_start(x[:, 0], a["x_next"][bass.ds(b, 1), 0:P, :].rearrange("o p d -> (o p) d"))\
                          .then_inc(s["x_first"], 16)
                        sp.wait_ge(s["mask_read"], 1)
                        sp.dma_start(mask_in[:], a["mask_next"][bass.ds(b, 1), :]).then_inc(s["x_rest"], 16)
                        for t in range(1, TT):
                            sp.wait_ge(s["xn_ready"], t)
                            sp.dma_start(x[:, t], a["x_next"][bass.ds(b, 1), t * P:(t + 1) * P, :].rearrange(
                                "o p d -> (o p) d")).then_inc(s["x_rest"], 16)
                    stores = 0
                    for name, t in steps:
                        if name == "hT":
                            sp.wait_ge(s["hT_ready"], done("hT", t))
                            slot = bass.ds(b if t < 0 else b + 1, 1)
                            at = t % TT
                            sp.dma_start(hT_dram[slot, :, :, at * P:(at + 1) * P].rearrange("o p k n -> (o p) k n"),
                                         hT[:, at]).then_inc(s["hT_out"], 16)
                            stores += 1
                    if stores:
                        sp.wait_ge(s["hT_out"], 16 * stores)
                    if heads:
                        sp.wait_ge(s["x_rest"], 16 * TT)

                def wait_evac(eng, n):
                    if evac_by_dve(n):
                        eng.wait_ge(s["probsT_dve"], count_dve(n))
                    else:
                        eng.wait_ge(s["probsT_act"], n + 1 - count_dve(n))

                @block.tensor
                def _(pe):
                    def fill(name, t, n=None):
                        n = FILLS[name] if n is None else n
                        if before[name, t, n]:
                            step, tile = before[name, t, n]
                            if step == "oT":
                                pe.wait_ge((s["oT_act"], s["oT_dve"])[n], done("oT", tile))
                            else:
                                for sm, value in drained(step, tile):
                                    pe.wait_ge(sm, value)
                        return FB[n]

                    for name, t in steps:
                        if name == "head":
                            n = t
                            if n < NH * TT:
                                tile, h = divmod(n, NH)
                                w = P * (tile + 1)
                                if n == 0:
                                    pe.wait_ge(s["mask_read"], 1)
                                    pe.wait_ge(s["next_taken"], 3)
                                if h == 0 and tile > 0:
                                    pe.wait_ge(s["qT_act"], 2 * done("qT0", tile))
                                    pe.wait_ge(s["qT_dve"], 2 * done("qT1", tile))
                                    pe.wait_ge(s["kT_ready"], done("kT", tile))
                                if n >= 2:
                                    pe.wait_ge(s["scores_ready"], n - 1)
                                o_s = SB[n % 2]
                                pe.matmul(o_s[:, 0:w], ones[:], mask_row[:, 0:w], start=True, stop=False)
                                for i in range(2):
                                    last = pe.matmul(o_s[:, 0:w], qT[:, tile % 2, h], kT[i][:, 0:w],
                                                     start=False, stop=i == 1)
                                last.then_inc(s["scores_psum"], 1)
                            n = t - QK_LAG
                            if 0 <= n < NH * TT:
                                tile = n // NH
                                pe.wait_ge(s["probs_ready"], n + 1)
                                if n >= 2:
                                    wait_evac(pe, n - 2)
                                for j in range(tile + 1):
                                    last = pe.transpose(TB[n % 2][:, j * P:(j + 1) * P],
                                                        S[:, n % S_SLOTS, j * P:(j + 1) * P], ident[:])
                                last.then_inc(s["probsT_psum"], 1)
                            n = t - PV_LAG
                            if 0 <= n < NH * TT:
                                tile, h = divmod(n, NH)
                                wait_evac(pe, n)
                                if h == 0 and tile > 0:
                                    pe.wait_ge(s["o_scaled"], done("weigh0", tile - 1) + done("weigh1", tile - 2))
                                if h == 8:
                                    pe.wait_ge(s["o_scaled"], done("weigh1", tile - 1) + tile)
                                for j in range(tile + 1):
                                    last = pe.matmul(OB[h // 8][:, (h % 8) * DH:(h % 8 + 1) * DH],
                                                     PT[:, n % PT_SLOTS, j * P:(j + 1) * P], v[:, j],
                                                     start=j == 0, stop=j == tile)
                                last.then_inc(s["pv_done"], 1)
                        elif name == "xT":
                            pe.wait_ge(s["xn_ready"], done("xn", t))
                            f = fill(name, t)
                            for k in range(KD):
                                last = pe.transpose(f[:, k * P:(k + 1) * P], xn[:, k * P:(k + 1) * P], ident[:])
                            last.then_inc(full[0], 1)
                        elif name in ("q0", "q1", "kv"):
                            if name == "q0":
                                pe.wait_ge(s["xnT_high"], done("xT", t))
                                pe.wait_ge(s["xnT_low"], done("xT", t))
                            f = fill(name, t)
                            cols = {"q0": slice(0, 512), "q1": slice(512, QW), "kv": slice(QW, QW + 2 * DH)}[name]
                            terms = [(i, j, k) for k in range(KD) for i, j in ((0, 0), (0, 1), (1, 0))]
                            for n, (i, j, k) in enumerate(terms):
                                last = pe.matmul(f[:, 0:cols.stop - cols.start], xnT[i][:, k], wqkv[j][:, k, cols],
                                                 start=n == 0, stop=n == len(terms) - 1)
                            last.then_inc(full[FILLS[name]], 1)
                        elif name in ("qT0", "qT1", "qT2", "qT3"):
                            i = int(name[2])
                            if i % 2 == 0:
                                pe.wait_ge(s["q_high"], 2 * done("qn", t) - 1 + i // 2)
                                pe.wait_ge(s["q_low"], 2 * done("qn", t) - 1 + i // 2)
                            f = fill(name, t)
                            for j in range(4):
                                last = pe.transpose(f[:, j * P:(j + 1) * P],
                                                    qs[:, 4 * i + j].rearrange("p a d -> p (a d)").bitcast(F32), ident[:])
                            last.then_inc(full[FILLS[name]], 1)
                        elif name == "kT":
                            pe.wait_ge(s["kn_ready"], done("qn", t))
                            f = fill(name, t)
                            pe.transpose(f[:, 0:P], kn[:].rearrange("p a d -> p (a d)"), ident[:]).then_inc(full[0], 1)
                        elif name == "null":
                            pe.wait_ge(s["qT_act"], 2 * done("qT0", t))
                            pe.wait_ge(s["qT_dve"], 2 * done("qT1", t))
                            f = fill(name, t)
                            for h in range(NH):
                                for i in range(2):
                                    last = pe.matmul(f[:, 2 * h:2 * h + 2], qT[:, t % 2, h], nullk[i][:],
                                                     start=i == 0, stop=i == 1)
                            last.then_inc(full[1], 1)
                        elif name == "oT":
                            pe.wait_ge(s["o_ready"], done("weigh1", t))
                            for n in range(2):
                                f = fill("oT", t, n)
                                for j in range(4):
                                    i = 4 * n + j
                                    last = pe.transpose(f[:, j * P:(j + 1) * P],
                                                        o[:, 2 * i:2 * i + 2].rearrange("p a d -> p (a d)"), ident[:])
                                last.then_inc(full[n], 1)
                        elif name == "outp":
                            pe.wait_ge(s["oT_act"], done("oT", t))
                            pe.wait_ge(s["oT_dve"], done("oT", t))
                            f = fill(name, t)
                            for i in range(QT):
                                last = pe.matmul(f[:, 0:D], oT[:, i], wout[:, i], start=i == 0, stop=i == QT - 1)
                            last.then_inc(full[0], 1)
                        elif name == "hT":
                            pe.wait_ge(s["hn_ready"], done("hn", t))
                            f = fill(name, t)
                            for k in range(KD):
                                last = pe.transpose(f[:, k * P:(k + 1) * P], hn[:, k * P:(k + 1) * P], ident[:])
                            last.then_inc(full[1], 1)

                @block.vector
                def _(dve):
                    link = Chain(dve, dve_chain)

                    def filled(name, t, n=None):
                        n = FILLS[name] if n is None else n
                        dve.wait_ge(full[n], filling[name, t, n])
                        return FB[n]

                    def weigh(t, i):
                        n = done("weigh0", t) + done("weigh1", t - 1) if i == 0 else done("weigh1", t) + done("weigh0", t)
                        hs = slice(8 * i, 8 * i + 8)
                        c = t % 2
                        if t >= 0:
                            dve.wait_ge(s["scores_ready"], NH * t + 8 * (i + 1))
                        dve.tensor_tensor(dn[:, i], nm[:, c, hs], nsn[:, c, hs], ALU.subtract).then_inc(s["null_diff"], 1)
                        dve.wait_ge(s["null_probs"], n)
                        link(dve.tensor_tensor(dent[:, i], den[:, c, hs], pn[:, i], ALU.add))
                        link(dve.reciprocal(rden[:, i], dent[:, i]))
                        dve.tensor_tensor(pnr[:, i], pn[:, i], rden[:, i], ALU.mult).then_inc(s["weights_ready"], 1)
                        if t >= 0:
                            dve.wait_ge(s["pv_done"], NH * t + 8 * (i + 1))
                        prev = done("oT", t - 1)
                        if prev:
                            dve.wait_ge(full[i], filling["oT", t - 1, i])
                        dve.tensor_tensor(o[:, hs], OB[i][:, :].rearrange("p (h d) -> p h d", d=DH),
                                          rden[:, i].unsqueeze(2).broadcast_to([P, 8, DH]),
                                          ALU.mult).then_inc(s["o_scaled"], 1)

                    if heads:
                        dve.tensor_scalar(mask_row[:], mask_in[:], -MASKED, MASKED, ALU.mult,
                                          ALU.add).then_inc(s["mask_read"], 1)
                        for i in range(2):
                            dve.tensor_copy(kT[i][:, 0:P], k_next[i][:]).then_inc(s["next_taken"], 1)
                        dve.tensor_copy(v[:, 0], v_next[:]).then_inc(s["next_taken"], 1)
                    for name, t in steps:
                        if name == "head":
                            n = t
                            if n < NH * TT:
                                tile, h = divmod(n, NH)
                                w = P * (tile + 1)
                                if h == 0 and tile > 0:
                                    dve.wait_ge(s["null_ready"], done("null", tile))
                                dve.wait_ge(s["scores_psum"], n + 1)
                                if n >= S_SLOTS:
                                    dve.wait_ge(s["probsT_psum"], n - S_SLOTS + 1)
                                dve.tensor_tensor_reduce(S[:, n % S_SLOTS, 0:w], SB[n % 2][:, 0:w],
                                                         bias[:, h, L - w:L], -1.0, nsn[:, tile % 2, h:h + 1],
                                                         ALU.add, ALU.min, nm[:, tile % 2, h:h + 1])\
                                   .then_inc(s["scores_ready"], 1)
                            n = t - QK_LAG
                            if 0 <= n < NH * TT and evac_by_dve(n):
                                dve.wait_ge(s["probsT_psum"], n + 1)
                                if n >= PT_SLOTS:
                                    dve.wait_ge(s["pv_done"], n - PT_SLOTS + 1)
                                w = P * (n // NH + 1)
                                dve.tensor_copy(PT[:, n % PT_SLOTS, 0:w], TB[n % 2][:, 0:w]).then_inc(s["probsT_dve"], 1)
                        elif name == "stat":
                            if t == TT and heads:
                                dve.wait_ge(s["x_first"], 16)
                            if done("stat", t) > 1:
                                dve.wait_ge(s["xn_ready"], done("xn", t - 1))
                            link(dve.bn_stats(stats[:], x[:, t % TT]))
                            link(dve.bn_aggr(mv[:], stats[:]))
                            dve.tensor_scalar(ve[:], mv[:, 1:2], 1e-5, None, ALU.add).then_inc(s["x_var"], 1)
                        elif name == "xn":
                            dve.wait_ge(s["x_rstd"], done("xn", t))
                            if done("xT", t - 1):
                                dve.wait_ge(full[0], filling["xT", t - 1, 0])
                            dve.tensor_scalar(xn[:], x[:, t % TT], mv[:, 0:1], rstd[:], ALU.subtract,
                                              ALU.mult).then_inc(s["xn_ready"], 1)
                        elif name == "xT":
                            dve.wait_ge(s["xnT_high"], done("xT", t))
                            if done("kv", t - 1):
                                dve.wait_ge(full[1], filling["kv", t - 1, 1])
                            dve.tensor_tensor(xnT[1][:].rearrange("p k n -> p (k n)"), FB[0][:, 0:D],
                                              xnT[0][:].rearrange("p k n -> p (k n)").bitcast(F32),
                                              ALU.subtract).then_inc(s["xnT_low"], 1)
                        elif name == "ss":
                            dve.wait_ge(s["sq_ready"], 3 * done("ss", t))
                            if done("rr", t - 1) or done("qn", t - 1):
                                dve.wait_ge(s["rr_ready"], done("qn", t - 1))
                            link(dve.tensor_reduce(ss[:], sq[:], AX.X, ALU.add))
                            dve.tensor_scalar(ss[:], ss[:], 1e-24, None, ALU.max).then_inc(s["ss_ready"], 1)
                        elif name in ("qT1", "qT3"):
                            f = filled(name, t)
                            i = int(name[2])
                            dve.tensor_copy(qT[:, t % 2, 4 * i:4 * i + 4].rearrange("p a n -> p (a n)"), f[:, :])\
                               .then_inc(s["qT_dve"], 1)
                        elif name == "kT":
                            f = filled(name, t)
                            high, low = (k_next[0][:], k_next[1][:]) if t == TT else \
                                (kT[0][:, t * P:(t + 1) * P], kT[1][:, t * P:(t + 1) * P])
                            if done("kT", t - 1):
                                dve.wait_ge(s["kT_ready"], done("kT", t - 1))
                            dve.tensor_scalar(kf[:], f[:, 0:P], kscale[:, 2:3], None, ALU.mult).then_inc(s["kT_read"], 1)
                            dve.wait_ge(s["kT_read"], done("kT", t))
                            link(dve.tensor_copy(high, kf[:]))
                            dve.tensor_tensor(low, kf[:], high.bitcast(F32), ALU.subtract).then_inc(s["kT_ready"], 1)
                        elif name == "null":
                            f = filled(name, t)
                            dve.scalar_tensor_tensor(out=nsn[:, t % 2], in0=f[:, 0:2 * NH:2], scalar=-1.0, in1=nullb[:],
                                                     op0=ALU.mult, op1=ALU.subtract).then_inc(s["null_ready"], 1)
                        elif name in ("weigh0", "weigh1"):
                            weigh(t, int(name[5]))
                        elif name == "oT":
                            f = filled("oT", t, 1)
                            if done("outp", t - 1):
                                dve.wait_ge(full[0], filling["outp", t - 1, 0])
                            dve.tensor_copy(oT[:, 4:8].rearrange("p a n -> p (a n)"), f[:, :]).then_inc(s["oT_dve"], 1)
                        elif name == "outp":
                            f = filled("outp", t)
                            if done("hn", t - 1):
                                dve.wait_ge(s["hn_ready"], done("hn", t - 1))
                            link(dve.bn_stats(stats2[:], f[:, 0:D]))
                            link(dve.bn_aggr(mv2[:], stats2[:]))
                            dve.tensor_scalar(ve2[:], mv2[:, 1:2], 1e-5, None, ALU.add).then_inc(s["out_var"], 1)
                        elif name == "hn":
                            dve.wait_ge(s["out_rstd"], done("hn", t))
                            if done("hT", t - 1):
                                dve.wait_ge(full[1], filling["hT", t - 1, 1])
                            dve.tensor_scalar(hn[:], FB[0][:, 0:D], mv2[:, 0:1], rstd2[:], ALU.subtract,
                                              ALU.mult).then_inc(s["hn_ready"], 1)

                @block.scalar
                def _(act):
                    def filled(name, t, n=None):
                        n = FILLS[name] if n is None else n
                        act.wait_ge(full[n], filling[name, t, n])
                        return FB[n]

                    for name, t in steps:
                        if name == "head":
                            n = t
                            if 0 <= n < NH * TT:
                                tile, h = divmod(n, NH)
                                w = P * (tile + 1)
                                act.wait_ge(s["scores_ready"], n + 1)
                                act.activation(S[:, n % S_SLOTS, 0:w], S[:, n % S_SLOTS, 0:w], ACT.Exp, scale=-1.0,
                                               bias=nm[:, tile % 2, h:h + 1],
                                               accum_out=den[:, tile % 2, h:h + 1]).then_inc(s["probs_ready"], 1)
                            n = t - QK_LAG
                            if 0 <= n < NH * TT and not evac_by_dve(n):
                                act.wait_ge(s["probsT_psum"], n + 1)
                                if n >= PT_SLOTS:
                                    act.wait_ge(s["pv_done"], n - PT_SLOTS + 1)
                                w = P * (n // NH + 1)
                                act.copy(PT[:, n % PT_SLOTS, 0:w], TB[n % 2][:, 0:w]).then_inc(s["probsT_act"], 1)
                        elif name == "xT":
                            f = filled(name, t)
                            if done("kv", t - 1):
                                act.wait_ge(full[1], filling["kv", t - 1, 1])
                            act.copy(xnT[0][:].rearrange("p k n -> p (k n)"), f[:, 0:D]).then_inc(s["xnT_high"], 1)
                        elif name in ("q0", "q1"):
                            i = int(name[1])
                            f = filled(name, t)
                            if i == 0 and done("qn", t - 1):
                                act.wait_ge(s["kn_ready"], done("qn", t - 1))
                                act.wait_ge(s["ss_ready"], done("ss", t - 1))
                            hs = slice(8 * i, 8 * i + 8)
                            act.activation(sq[:, hs].rearrange("p a d -> p (a d)"), f[:, :], ACT.Square)\
                               .then_inc(s["sq_ready"], 1)
                            act.copy(qraw[:, hs].rearrange("p a d -> p (a d)"), f[:, :]).then_inc(s["q_ready"], 1)
                        elif name == "kv":
                            f = filled(name, t)
                            act.activation(sq[:, NH], f[:, 0:DH], ACT.Square).then_inc(s["sq_ready"], 1)
                            act.copy(v_next[:] if t == TT else v[:, t], f[:, DH:2 * DH]).then_inc(s["kv_ready"], 1)
                            act.copy(qraw[:, NH], f[:, 0:DH]).then_inc(s["kv_ready"], 1)
                        elif name == "qn":
                            for i in range(2):
                                hs = slice(8 * i, 8 * i + 8)
                                act.wait_ge(s["qn_ready"], 2 * done("qn", t) - 1 + i)
                                if done("qT3", t - 1):
                                    act.wait_ge(full[1], filling["qT3", t - 1, 1])
                                act.copy(qs[:, hs, 0], qn[:, hs]).then_inc(s["q_high"], 1)
                        elif name in ("qT0", "qT2"):
                            f = filled(name, t)
                            i = int(name[2])
                            act.copy(qT[:, t % 2, 4 * i:4 * i + 4].rearrange("p a n -> p (a n)"), f[:, :])\
                               .then_inc(s["qT_act"], 1)
                        elif name in ("weigh0", "weigh1"):
                            i = int(name[5])
                            n = done("weigh0", t) + (done("weigh1", t - 1) if i == 0 else done("weigh1", t))
                            act.wait_ge(s["null_diff"], n)
                            if n > 2:
                                act.wait_ge(s["weights_ready"], n - 2)
                            act.activation(pn[:, i], dn[:, i], ACT.Exp).then_inc(s["null_probs"], 1)
                        elif name == "oT":
                            f = filled("oT", t, 0)
                            if done("outp", t - 1):
                                act.wait_ge(full[0], filling["outp", t - 1, 0])
                            act.copy(oT[:, 0:4].rearrange("p a n -> p (a n)"), f[:, :]).then_inc(s["oT_act"], 1)
                        elif name == "hT":
                            f = filled(name, t)
                            for k in range(KD):
                                last = act.activation(hT[:, t % TT, k], f[:, k * P:(k + 1) * P], ACT.Copy,
                                                      scale=go[:, k:k + 1])
                            last.then_inc(s["hT_ready"], 1)

                @block.gpsimd
                def _(pool):
                    link = Chain(pool, pool_chain)
                    for name, t in steps:
                        if name == "stat":
                            pool.wait_ge(s["x_var"], done("stat", t))
                            pool.tensor_tensor(rstd[:], ve[:], half[:, 0:1], ALU.pow).then_inc(s["x_rstd"], 1)
                        elif name == "ss":
                            pool.wait_ge(s["ss_ready"], done("ss", t))
                            if done("qn", t - 1):
                                pool.wait_ge(s["kn_ready"], done("qn", t - 1))
                            pool.tensor_tensor(rr[:], ss[:], half[:, 0:NH + 1], ALU.pow).then_inc(s["rr_ready"], 1)
                        elif name == "qn":
                            n = done("qn", t)
                            pool.wait_ge(s["rr_ready"], n)
                            pool.wait_ge(s["q_ready"], 2 * n)
                            pool.wait_ge(s["kv_ready"], 2 * n)

                            def scaled(i):
                                hs = slice(8 * i, 8 * i + 8)
                                pool.tensor_tensor(qn[:, hs], qraw[:, hs], rr[:, hs].unsqueeze(2).broadcast_to([P, 8, DH]),
                                                   ALU.mult).then_inc(s["qn_ready"], 1)

                            if done("kT", t - 1):
                                pool.wait_ge(full[0], filling["kT", t - 1, 0])
                            scaled(0)
                            scaled(1)
                            for i in range(2):
                                hs = slice(8 * i, 8 * i + 8)
                                pool.wait_ge(s["q_high"], 2 * n - 1 + i)
                                if done("qT3", t - 1):
                                    pool.wait_ge(full[1], filling["qT3", t - 1, 1])
                                pool.tensor_tensor(qs[:, hs, 1], qn[:, hs], qs[:, hs, 0].bitcast(F32),
                                                   ALU.subtract).then_inc(s["q_low"], 1)
                            pool.tensor_tensor(kn[:], qraw[:, NH].unsqueeze(1).broadcast_to([P, 2, DH]),
                                               rr[:, NH:NH + 1].unsqueeze(2).broadcast_to([P, 2, DH]),
                                               ALU.mult).then_inc(s["kn_ready"], 1)
                        elif name in ("weigh0", "weigh1"):
                            i = int(name[5])
                            n = done("weigh0", t) + (done("weigh1", t - 1) if i == 0 else done("weigh1", t))
                            hs = slice(8 * i, 8 * i + 8)
                            pool.wait_ge(s["weights_ready"], n)
                            if n > 1:
                                pool.wait_ge(s["onull_ready"], n - 1)
                            pool.tensor_tensor(onull[:, hs], nullv[:].unsqueeze(1).broadcast_to([P, 8, DH]),
                                               pnr[:, i].unsqueeze(2).broadcast_to([P, 8, DH]),
                                               ALU.mult).then_inc(s["onull_ready"], 1)
                            pool.wait_ge(s["onull_ready"], n)
                            pool.wait_ge(s["o_scaled"], n)
                            ins = pool.tensor_tensor(o[:, hs], o[:, hs], onull[:, hs], ALU.add)
                            if i == 1:
                                ins.then_inc(s["o_ready"], 1)
                            else:
                                link(ins)
                        elif name == "outp":
                            pool.wait_ge(s["out_var"], done("outp", t))
                            if done("hn", t - 1):
                                pool.wait_ge(s["hn_ready"], done("hn", t - 1))
                            pool.tensor_tensor(rstd2[:], ve2[:], half[:, 0:1], ALU.pow).then_inc(s["out_rstd"], 1)
            clear(nc, sems)

        run([(n, TT) for names in NEXT.values() for n in names], 0)
        with nc.Fori(0, B) as b:
            run(iteration(), b)
        run([(n, -1) for names in LAST.values() for n in names], B)




def drained_before(order, drained):
    held, out = {}, {}
    for bank, step, n in order:
        out[bank, step, n] = drained(*held[bank]) if bank in held else []
        held[bank] = (step, n)
    return out


def delta_inputs_phase(nc, a, hT_dram, xg_dram, qk_dram, vb_dram, bg_dram, low_dram):
    PAD = 8
    with ExitStack() as ctx:
        sb, bank, sem, sems = space(nc, ctx, "b")
        ident = sb("ident", [P, P])
        wqkv = sb("wqkv", [P, KD, 3 * D])
        wsm = sb("wsm", [P, KD, 2 * H2 + 1])
        smb = sb("smb", [P, 2 * H2 + 1])
        conv = sb("conv", [P, 3, KD, 4])
        frac = sb("frac", [P, KD, 4, 2])
        own = sb("own", [P, KD])
        cos = sb("cos", [P, TT, DH // 2])
        sin = sb("sin", [P, TT, DH // 2])
        rot = sb("rot", [P, H2])
        cm = sb("cm", [P, TT, H2, DH // 2])
        sm = sb("sm", [P, TT, H2, DH // 2])
        omx = sb("omx", [P, H2, DH])
        mixw = sb("mixw", [P, D])
        strict = sb("strict", [P, CH])
        half = sb("half", [P, 8])

        h = sb("h", [P, KD, PAD + L])
        x = sb("x", [P, TT, D])
        proj = sb("proj", [P, 6, 3 + L])
        y = sb("y", [P, 6, L])
        gates_in = sb("gates_in", [P, TT, 2 * H2 + 1])
        gates = sb("gates", [P, TT, 2 * H2 + 1])
        nb = sb("nb", [P, TT, H2, CH])
        fr = sb("fr", [P, KD, L])
        ft = sb("ft", [P, L])
        fsq = sb("fsq", [P, TT, D])
        fss = sb("fss", [P, TT])
        fve = sb("fve", [P, TT])
        frs = sb("frs", [P, TT])
        fsc = sb("fsc", [P, TT])
        z = sb("z", [P, 2, 8, DH])
        zm = sb("zm", [P, 2, 8, DH])
        rb1 = sb("rb1", [P, 2, P])
        rb2 = sb("rb2", [P, 2, P])
        ra1 = sb("ra1", [P, 2, P])
        ra2 = sb("ra2", [P, 2, P])
        r = sb("r", [P, 2, 8, DH])
        rsq = sb("rsq", [P, 8, DH])
        rss = sb("rss", [P, 2, 8])
        rrn = sb("rrn", [P, 2, 8])
        qk = sb("qk", [P, TT, 8, DH])
        vb = sb("vb", [P, TT, H2, DH])
        kT = sb("kT", [P, TT, 2, P])
        low = sb("low", [P, TT, H2, CH])
        xg = sb("xg", [P, TT, D])

        J = [bank(f"J{i}") for i in range(2)]
        X = [bank(f"X{i}") for i in range(2)]
        V = bank("V")
        K = bank("K")
        G = [bank(f"G{i}") for i in range(2)]

        loaded = sem("loaded")
        dve_chain = sem("dve_chain")
        pool_chain = sem("pool_chain")
        rot_ready = sem("rot_ready")

        with nc.Block() as block:
            N_LOADS = 13

            @block.sync
            def _(sp):
                loads = [(ident[:], a["c_ident"]), (conv[:], a["conv"]), (frac[:], a["L0_attn_frac_conv_w"]),
                         (cos[:], a["c_cos"]), (sin[:], a["c_sin"]), (rot[:], row(a["L0_attn_rot_logit"], H2)),
                         (mixw[:], row(a["L0_attn_mixer_norm_w"], D)), (strict[:], a["c_strict"]),
                         (smb[:, 2 * H2:], row(a["L0_attn_frac_gate_b"], 1))]
                for i, n in enumerate(("Wq", "Wk", "Wv")):
                    loads.append((wqkv[:, :, i * D:(i + 1) * D], a[f"L0_attn_{n}"].rearrange("(k p) n -> p k n", p=P)))
                loads.append((wsm[:], a["gates"]))
                assert len(loads) == N_LOADS
                for dst, src in loads:
                    sp.dma_start(dst, src).then_inc(loaded, 16)

            @block.scalar
            def _(act):
                act.wait_ge(loaded, 16 * N_LOADS)
                act.activation(rot[:], rot[:], ACT.Sigmoid).then_inc(rot_ready, 1)

            @block.gpsimd
            def _(pool):
                pool.memset(half[:], -0.5)
                pool.memset(h[:, :, 0:PAD], 0.0)
                pool.memset(proj[:, :, 0:3], 0.0)

            @block.vector
            def _(dve):
                link = Chain(dve, dve_chain)
                dve.memset(smb[:, 0:2 * H2], 0.0)
                dve.wait_ge(loaded, 16 * N_LOADS)
                link(dve.tensor_reduce(own[:], frac[:, :, :, 1], AX.X, ALU.add))
                dve.tensor_scalar(own[:], own[:], 2.0, None, ALU.add)
                dve.wait_ge(rot_ready, 1)
                for t in range(TT):
                    for table, mixed in ((cos, cm), (sin, sm)):
                        dve.tensor_tensor(mixed[:, t], table[:, t].unsqueeze(1).broadcast_to([P, H2, DH // 2]),
                                          rot[:].unsqueeze(2).broadcast_to([P, H2, DH // 2]), ALU.mult)
                dve.tensor_scalar(omx[:], rot[:].unsqueeze(2).broadcast_to([P, H2, DH]), -1.0, 1.0, ALU.mult, ALU.add)
        clear(nc, sems)

        h_in = sem("h_in")
        proj_psum = sem("proj_psum")
        proj_ready = sem("proj_ready")
        conv_ready = sem("conv_ready")
        y_ready = sem("y_ready")
        gates_psum = sem("gates_psum")
        gates_read = sem("gates_read")
        gates_ready = sem("gates_ready")
        nb_ready = sem("nb_ready")
        frac_ready = sem("frac_ready")
        fracT_psum = sem("fracT_psum")
        frac_sums = sem("frac_sums")
        frac_var = sem("frac_var")
        frac_scale = sem("frac_scale")
        xg_ready = sem("xg_ready")
        z_psum = sem("z_psum")
        z_ready = sem("z_ready")
        pool_rot = sem("pool_rot")
        r_ready = sem("r_ready")
        rsq_ready = sem("rsq_ready")
        rss_ready = sem("rss_ready")
        rrn_ready = sem("rrn_ready")
        qk_ready = sem("qk_ready")
        v_psum = sem("v_psum")
        vb_ready = sem("vb_ready")
        kT_psum = sem("kT_psum")
        kT_ready = sem("kT_ready")
        gram_psum = sem("gram_psum")
        low_ready = sem("low_ready")
        stored = sem("stored")

        ORDER = ([("J", i % 2, "proj", i) for i in range(6)] + [("K", 0, "gates", 0)]
                 + [("X", t % 2, "z", t) for t in range(TT)] + [("V", 0, "v", 0), ("V", 0, "v", 1)]
                 + [("J", 0, "frac", 0), ("J", 1, "frac", 1)])
        for t in range(TT):
            ORDER.append(("K", 0, "kT", t))
            if t % 2:
                ORDER += [("G", e, "gram", 2 * (t // 2) + e) for e in range(2)]

        def drained(step, n):
            return {"proj": [(proj_ready, n + 1)], "gates": [(gates_read, 1)], "z": [(z_ready, n + 1)],
                    "v": [(vb_ready, n + 1)], "frac": [(xg_ready, 2 * n + 2)], "kT": [(kT_ready, n + 1)],
                    "gram": [(low_ready, 4 * (n + 1))]}[step]

        before = drained_before([((name, i), step, n) for name, i, step, n in ORDER], drained)
        BANKS = {"J": J, "X": X, "V": [V], "K": [K], "G": G}

        with nc.Fori(0, B) as b:
            with nc.Block() as block:
                @block.sync
                def _(sp):
                    sp.dma_start(h[:, :, PAD:], hT_dram[bass.ds(b + 1, 1), :, :, :].rearrange("o p k n -> (o p) k n")).then_inc(h_in, 16)
                    sp.dma_start(x[:], a["x"][bass.ds(b, 1), :, :].rearrange("o (t p) d -> p (o t) d", p=P)).then_inc(h_in, 16)
                    sp.wait_ge(gates_ready, 1)
                    sp.dma_start(bg_dram[bass.ds(b, 1), :, :].rearrange("o p n -> (o p) n"),
                                 gates[:].rearrange("p t n -> p (t n)")).then_inc(stored, 16)
                    sp.wait_ge(vb_ready, 2)
                    sp.dma_start(vb_dram[bass.ds(b, 1), :, :].rearrange("o p n -> (o p) n"),
                                 vb[:].rearrange("p t h d -> p (t h d)")).then_inc(stored, 16)
                    sp.wait_ge(xg_ready, TT)
                    sp.dma_start(xg_dram[bass.ds(b, 1), :, :].rearrange("o p n -> (o p) n"),
                                 xg[:].rearrange("p t d -> p (t d)")).then_inc(stored, 16)
                    sp.wait_ge(qk_ready, TT)
                    sp.dma_start(qk_dram[bass.ds(b, 1), :, :].rearrange("o p n -> (o p) n"),
                                 qk[:].rearrange("p t h d -> p (t h d)")).then_inc(stored, 16)
                    sp.wait_ge(low_ready, 16)
                    for c in range(NC4):
                        sp.dma_start(low_dram[bass.ds(b, 1), :, :, c].rearrange("o t h i j -> i (o t h) j"),
                                     low[c * CH:(c + 1) * CH].rearrange("p t h j -> p (t h) j")).then_inc(stored, 16)
                    sp.wait_ge(stored, 16 * (4 + NC4))

                @block.tensor
                def _(pe):
                    def fill(name, i, step, n):
                        for s, value in before[(name, i), step, n]:
                            pe.wait_ge(s, value)
                        return BANKS[name][i]

                    pe.wait_ge(h_in, 32)
                    for i in range(6):
                        o = fill("J", i % 2, "proj", i)
                        for k in range(KD):
                            last = pe.matmul(o[:, :], wqkv[:, k, i * P:(i + 1) * P], h[:, k, PAD:],
                                             start=k == 0, stop=k == KD - 1)
                        last.then_inc(proj_psum, 1)
                    o = fill("K", 0, "gates", 0)
                    n = 2 * H2 + 1
                    for t in range(TT):
                        for k in range(KD):
                            last = pe.matmul(o[:, t * n:(t + 1) * n], h[:, k, PAD + t * P:PAD + (t + 1) * P],
                                             wsm[:, k], start=k == 0, stop=k == KD - 1)
                    last.then_inc(gates_psum, 1)
                    for t in range(TT):
                        if t == 0:
                            pe.wait_ge(y_ready, 4)
                        o = fill("X", t % 2, "z", t)
                        for i in range(4):
                            last = pe.transpose(o[:, i * P:(i + 1) * P], y[:, i, t * P:(t + 1) * P], ident[:])
                        last.then_inc(z_psum, 1)
                    pe.wait_ge(y_ready, 6)
                    for g in range(2):
                        o = fill("V", 0, "v", g)
                        for tt in range(2):
                            for i in range(2):
                                t = 2 * g + tt
                                last = pe.transpose(o[:, tt * D + i * P:tt * D + (i + 1) * P],
                                                    y[:, 4 + i, t * P:(t + 1) * P], ident[:])
                        last.then_inc(v_psum, 1)
                    pe.wait_ge(frac_ready, KD)
                    for g in range(2):
                        o = fill("J", g, "frac", g)
                        for tt in range(2):
                            for k in range(KD):
                                t = 2 * g + tt
                                last = pe.transpose(o[:, tt * D + k * P:tt * D + (k + 1) * P],
                                                    fr[:, k, t * P:(t + 1) * P], ident[:])
                        last.then_inc(fracT_psum, 1)
                    for t in range(TT):
                        pe.wait_ge(qk_ready, t + 1)
                        o = fill("K", 0, "kT", t)
                        for i in range(2):
                            last = pe.transpose(o[:, i * P:(i + 1) * P],
                                                qk[:, t, H2 + 2 * i:H2 + 2 * i + 2].rearrange("p a d -> p (a d)"), ident[:])
                        last.then_inc(kT_psum, 1)
                        if t % 2:
                            pe.wait_ge(kT_ready, t + 1)
                            for e in range(2):
                                o = fill("G", e, "gram", 2 * (t // 2) + e)
                                part = slice(e * DH, (e + 1) * DH)
                                for tt in range(2):
                                    for i in range(2):
                                        keys = kT[part, t - 1 + tt, i]
                                        j = 2 * tt + i
                                        last = pe.matmul(o[:, j * P:(j + 1) * P], keys, keys, start=True, stop=True)
                                last.then_inc(gram_psum, 1)

                @block.scalar
                def _(act):
                    for i in range(6):
                        act.wait_ge(proj_psum, i + 1)
                        act.copy(proj[:, i, 3:], J[i % 2][:, :]).then_inc(proj_ready, 1)
                    act.wait_ge(gates_read, 1)
                    act.activation(gates[:], gates_in[:], ACT.Sigmoid).then_inc(gates_ready, 1)
                    for i in range(6):
                        act.wait_ge(conv_ready, i + 1)
                        act.activation(y[:, i], y[:, i], ACT.Silu).then_inc(y_ready, 1)
                    for t in range(TT + 1):
                        if t < TT:
                            act.wait_ge(z_psum, t + 1)
                            if t >= 2:
                                act.wait_ge(r_ready, t - 1)
                                act.wait_ge(pool_rot, t - 1)
                            act.copy(z[:, t % 2].rearrange("p a d -> p (a d)"), X[t % 2][:, :]).then_inc(z_ready, 1)
                        if t > 0:
                            act.wait_ge(r_ready, t)
                            if t > 1:
                                act.wait_ge(rss_ready, t - 1)
                            act.activation(rsq[:], r[:, (t - 1) % 2], ACT.Square).then_inc(rsq_ready, 1)
                    for t in range(TT):
                        act.wait_ge(fracT_psum, t // 2 + 1)
                        act.activation(fsq[:, t], J[t // 2][:, (t % 2) * D:(t % 2 + 1) * D], ACT.Square,
                                       accum_out=fss[:, t:t + 1]).then_inc(frac_sums, 1)
                    for t in range(TT):
                        act.wait_ge(kT_psum, t + 1)
                        act.copy(kT[:, t].rearrange("p a n -> p (a n)"), K[:, 0:2 * P]).then_inc(kT_ready, 1)

                @block.gpsimd
                def _(pool):
                    link = Chain(pool, pool_chain)
                    pool.wait_ge(h_in, 32)
                    for k in range(KD):
                        link(pool.tensor_scalar(fr[:, k], h[:, k, PAD:], own[:, k:k + 1], None, ALU.mult))
                        for i in range(4):
                            dil = 2 ** i
                            link(pool.tensor_scalar(ft[:], h[:, k, PAD - dil:PAD - dil + L], frac[:, k, i, 0:1], None,
                                                    ALU.mult))
                            ins = pool.tensor_tensor(fr[:, k], fr[:, k], ft[:], ALU.add)
                            if i < 3:
                                link(ins)
                        ins.then_inc(frac_ready, 1)
                        pool.wait_ge(frac_ready, k + 1)
                    pool.wait_ge(gates_ready, 1)
                    for t in range(TT):
                        ins = pool.tensor_tensor(nb[:, t], gates[:, t, 0:H2].unsqueeze(2).broadcast_to([P, H2, CH]),
                                                 strict[:].unsqueeze(1).broadcast_to([P, H2, CH]), ALU.mult)
                    ins.then_inc(nb_ready, 1)
                    for t in range(TT + 1):
                        if t < TT:
                            pool.wait_ge(z_ready, t + 1)
                            if t >= 2:
                                pool.wait_ge(r_ready, t - 1)
                            zt = z[:, t % 2].rearrange("p a (d two) -> p two (a d)", two=2)
                            x1, x2 = (zt[:, i].rearrange("p (q n) -> p q n", q=2) for i in range(2))
                            c, s = (m[:, t].rearrange("p h d -> p (h d)").unsqueeze(1).broadcast_to([P, 2, P])
                                    for m in (cm, sm))
                            pool.tensor_tensor(zm[:, t % 2].rearrange("p (q h) d -> p q (h d)", q=2),
                                               z[:, t % 2].rearrange("p (q h) d -> p q (h d)", q=2),
                                               omx[:].rearrange("p h d -> p (h d)").unsqueeze(1).broadcast_to([P, 2, 2 * P]),
                                               ALU.mult)
                            if t > 0:
                                pool.wait_ge(r_ready, t)
                            pool.tensor_tensor(rb1[:], x1, s, ALU.mult)
                            link(pool.tensor_tensor(rb2[:], x2, c, ALU.mult))
                            pool.tensor_tensor(rb1[:], rb1[:], rb2[:], ALU.add).then_inc(pool_rot, 1)
                        if t > 0:
                            pool.wait_ge(rss_ready, t)
                            if t > 2:
                                pool.wait_ge(qk_ready, t - 2)
                            pool.tensor_tensor(rrn[:, (t - 1) % 2], rss[:, (t - 1) % 2], half[:], ALU.pow).then_inc(rrn_ready, 1)
                    pool.wait_ge(frac_var, 1)
                    link(pool.tensor_tensor(frs[:], fve[:], half[:, 0:TT], ALU.pow))
                    pool.tensor_tensor(fsc[:], frs[:], gates[:, :, 2 * H2], ALU.mult).then_inc(frac_scale, 1)

                @block.vector
                def _(dve):
                    link = Chain(dve, dve_chain)

                    def gates_step():
                        dve.wait_ge(gates_psum, 1)
                        n = 2 * H2 + 1
                        dve.tensor_tensor(gates_in[:], K[:, 0:TT * n].rearrange("p (t n) -> p t n", n=n),
                                          smb[:].unsqueeze(1).broadcast_to([P, TT, n]), ALU.add).then_inc(gates_read, 1)

                    for i in range(6):
                        w = conv[:, i // 2, i % 2]
                        dve.wait_ge(proj_ready, i + 1)
                        link(dve.tensor_scalar(y[:, i], proj[:, i, 0:L], w[:, 0:1], None, ALU.mult))
                        for j in range(1, 4):
                            ins = dve.scalar_tensor_tensor(out=y[:, i], in0=proj[:, i, j:j + L], scalar=w[:, j:j + 1],
                                                           in1=y[:, i], op0=ALU.mult, op1=ALU.add)
                            if j < 3:
                                link(ins)
                        ins.then_inc(conv_ready, 1)
                        if i == 3:
                            gates_step()
                    for t in range(TT + 1):
                        if t < TT:
                            dve.wait_ge(z_ready, t + 1)
                            if t > 0:
                                dve.wait_ge(r_ready, t)
                            zt = z[:, t % 2].rearrange("p a (d two) -> p two (a d)", two=2)
                            x1, x2 = (zt[:, i].rearrange("p (q n) -> p q n", q=2) for i in range(2))
                            c, s = (m[:, t].rearrange("p h d -> p (h d)").unsqueeze(1).broadcast_to([P, 2, P])
                                    for m in (cm, sm))
                            dve.tensor_tensor(ra1[:], x1, c, ALU.mult)
                            link(dve.tensor_tensor(ra2[:], x2, s, ALU.mult))
                            link(dve.tensor_tensor(ra1[:], ra1[:], ra2[:], ALU.subtract))
                            dve.wait_ge(pool_rot, t + 1)
                            rt, zt = r[:, t % 2], zm[:, t % 2]
                            dve.tensor_tensor(rt[:, :, 0:CH], zt[:, :, 0:CH],
                                              ra1[:].rearrange("p q (h d) -> p (q h) d", d=CH), ALU.add)
                            dve.tensor_tensor(rt[:, :, CH:], zt[:, :, CH:],
                                              rb1[:].rearrange("p q (h d) -> p (q h) d", d=CH), ALU.add).then_inc(r_ready, 1)
                        if t > 0:
                            i = (t - 1) % 2
                            dve.wait_ge(rsq_ready, t)
                            link(dve.tensor_reduce(rss[:, i], rsq[:], AX.X, ALU.add))
                            dve.tensor_scalar(rss[:, i], rss[:, i], 1e-6, None, ALU.add).then_inc(rss_ready, 1)
                            dve.wait_ge(rrn_ready, t)
                            dve.tensor_tensor(qk[:, t - 1], r[:, i], rrn[:, i].unsqueeze(2).broadcast_to([P, 8, DH]),
                                              ALU.mult).then_inc(qk_ready, 1)
                        if t in (2, 3):
                            g = t - 2
                            dve.wait_ge(v_psum, g + 1)
                            dve.wait_ge(gates_ready, 1)
                            for tt in range(2):
                                ins = dve.tensor_tensor(vb[:, 2 * g + tt], V[:, tt * D:(tt + 1) * D].rearrange(
                                    "p (h d) -> p h d", d=DH),
                                    gates[:, 2 * g + tt, 0:H2].unsqueeze(2).broadcast_to([P, H2, DH]), ALU.mult)
                            ins.then_inc(vb_ready, 1)
                    dve.wait_ge(frac_sums, TT)
                    dve.tensor_scalar(fve[:], fss[:], 1.0 / D, 1e-5, ALU.mult, ALU.add).then_inc(frac_var, 1)
                    for n in range(4):
                        g, e = divmod(n, 2)
                        dve.wait_ge(gram_psum, n + 1)
                        dve.wait_ge(nb_ready, 1)
                        for c in range(NC4):
                            part = slice(c * CH, (c + 1) * CH)
                            hs = slice(e, H2, 2)
                            src = G[e][part, :].rearrange("p (t i n) -> p t i n", t=2, i=2)[:, :, :, part]
                            dve.tensor_tensor(low[part, 2 * g:2 * g + 2, hs], src, nb[part, 2 * g:2 * g + 2, hs],
                                              ALU.mult).then_inc(low_ready, 1)
                    dve.wait_ge(frac_scale, 1)
                    for t in range(TT):
                        link(dve.scalar_tensor_tensor(out=xg[:, t], in0=J[t // 2][:, (t % 2) * D:(t % 2 + 1) * D],
                                                      scalar=fsc[:, t:t + 1], in1=mixw[:], op0=ALU.mult, op1=ALU.mult))
                        dve.tensor_tensor(xg[:, t], xg[:, t], x[:, t], ALU.add).then_inc(xg_ready, 1)
            clear(nc, sems)


def inverse_phase(nc, a, low_dram, inv_dram):
    with ExitStack() as ctx:
        sb, bank, sem, sems = space(nc, ctx, "i")
        A = sb("A", [P, NC4, CH, CH])
        AT = sb("AT", [P, NC4, CH, CH])
        prod = sb("prod", [P, NC4, CH * CH])
        upd = sb("upd", [P, NC4, CH])
        eye = sb("eye", [P, CH, CH])
        loaded = sem("loaded")
        turned = sem("turned")
        stored = sem("stored")
        dve_chain = sem("dve_chain")
        pool_chain = sem("pool_chain")

        def substitute(eng, link, cs):
            n = cs.stop - cs.start
            for i in range(1, CH):
                own_row = A[:, cs, i, 0:i].unsqueeze(2).broadcast_to([P, n, i, i])
                above = A[:, cs, 0:i, 0:i].rearrange("p c j k -> p c k j")
                pr = prod[:, cs, 0:i * i].rearrange("p c (k j) -> p c k j", j=i)
                link(eng.tensor_tensor(pr, above, own_row, ALU.mult))
                link(eng.tensor_reduce(upd[:, cs, 0:i], pr, AX.X, ALU.add))
                link(eng.tensor_tensor(A[:, cs, i, 0:i], A[:, cs, i, 0:i], upd[:, cs, 0:i], ALU.add))

        with nc.Block() as block:
            @block.sync
            def _(sp):
                sp.dma_start(A[:], low_dram.rearrange("b t h c i j -> (b t h) c i j")).then_inc(loaded, 16)
                sp.dma_start(eye[:], a["c_eye32"]).then_inc(loaded, 16)
                sp.wait_ge(turned, NC4)
                sp.dma_start(inv_dram.rearrange("b t h c i j -> (b t h) c i j"), AT[:]).then_inc(stored, 16)
                sp.wait_ge(stored, 16)

            @block.vector
            def _(dve):
                link = Chain(dve, dve_chain)
                dve.wait_ge(loaded, 32)
                substitute(dve, link, slice(0, NC4))
                for c in range(NC4):
                    dve.tensor_tensor(AT[:, c], A[:, c].rearrange("p i j -> p j i"), eye[:], ALU.add).then_inc(turned, 1)
        clear(nc, sems)


def delta_rule_phase(nc, a, xg_dram, qk_dram, vb_dram, bg_dram, inv_dram, x1_dram):
    NG = 2 * H2 + 1
    with ExitStack() as ctx:
        sb, bank, sem, sems = space(nc, ctx, "d")
        ident = sb("ident", [P, P])
        causal = sb("causal", [P, P])
        chunk_of = sb("chunk_of", [P, NC4])
        wo = sb("wo", [P, KD, D])
        onw = sb("onw", [P, 1])
        eye = sb("eye", [P, DH])
        half = sb("half", [P, TT * H2])
        qk = sb("qk", [P, TT, 8, DH])
        vk = sb("vk", [P, TT, H2, 2, DH])
        gates = sb("gates", [P, TT, NG])
        xg = sb("xg", [P, TT, D])
        inv = sb("inv", [P, TT, H2, P])
        gx = sb("gx", [P, TT, H2, DH])
        gm = sb("gm", [P, TT, 2, NC4])
        gI = sb("gI", [P, TT, NC4, 2, DH])
        qkT = sb("qkT", [P, TT, 4, P])
        attn = sb("attn", [P, 2, TT, 2, P])
        uw = sb("uw", [P, TT, H2, 2, DH])
        qpT = sb("qpT", [P, TT, 2, P])
        MT = sb("MT", [P, TT, NC4, 2, DH])
        kb_u = sb("kb_u", [P, TT, NC4, 2, DH])
        S = sb("S", [P, NCH + 1, 2, DH])
        osq = sb("osq", [P, 2, TT * 2, DH])
        oss = sb("oss", [P, 2, TT * 2])
        ors = sb("ors", [P, 2, TT * 2])
        on = sb("on", [P, TT, H2, DH])
        onT = sb("onT", [P, KD, L])
        x1 = sb("x1", [P, TT, D])
        R = [bank(f"R{i}") for i in range(8)]

        loaded = sem("loaded")
        dve_chain = sem("dve_chain")
        with nc.Block() as block:
            @block.sync
            def _(sp):
                loads = [(ident[:], a["c_ident"]), (causal[:], a["c_causal"]), (chunk_of[:], a["c_chunk_of"]),
                         (wo[:], a["L0_attn_Wo"].rearrange("(k p) n -> p k n", p=P)),
                         (onw[0:DH], a["L0_attn_o_norm_w"].rearrange("(n o) -> n o", o=1)),
                         (onw[DH:P], a["L0_attn_o_norm_w"].rearrange("(n o) -> n o", o=1)),
                         (eye[0:DH], a["c_ident"][0:DH, 0:DH]), (eye[DH:P], a["c_ident"][0:DH, 0:DH])]
                for dst, src in loads:
                    sp.dma_start(dst, src).then_inc(loaded, 16)

            @block.gpsimd
            def _(pool):
                pool.memset(half[:], -0.5)
                pool.memset(inv[:], 0.0)
                pool.memset(S[:, 0], 0.0)

            @block.vector
            def _(dve):
                dve.wait_ge(loaded, 16 * 8)
                for k in range(KD):
                    dve.tensor_scalar(wo[:, k], wo[:, k], onw[:, 0:1], None, ALU.mult)
        clear(nc, sems)

        rows_in = sem("rows_in")
        inv_in = sem("inv_in")
        kb_ready = sem("kb_ready")
        gx_ready = sem("gx_ready")
        gm_psum = sem("gm_psum")
        gm_ready = sem("gm_ready")
        gI_ready = sem("gI_ready")
        qkT_psum = sem("qkT_psum")
        qkT_ready = sem("qkT_ready")
        attn_psum = sem("attn_psum")
        attn_ready = sem("attn_ready")
        uw_psum = sem("uw_psum")
        uw_ready = sem("uw_ready")
        qp_psum = sem("qp_psum")
        qp_ready = sem("qp_ready")
        step_psum = sem("step_psum")
        MT_ready = sem("MT_ready")
        ku_ready = sem("ku_ready")
        state_psum = [sem(f"state_psum{e}") for e in range(2)]
        state_ready = [sem(f"state_ready{e}") for e in range(2)]
        o_psum = sem("o_psum")
        osq_ready = sem("osq_ready")
        oss_ready = sem("oss_ready")
        ors_ready = sem("ors_ready")
        on_ready = sem("on_ready")
        onT_psum = sem("onT_psum")
        onT_ready = sem("onT_ready")
        core_psum = sem("core_psum")
        x1_ready = sem("x1_ready")
        stored = sem("stored")

        ORDER = [(t % 2, "qkT", t) for t in range(TT)]
        ORDER += [(2 + e, "attn", e) for e in range(2)] + [(t, "uw", t) for t in range(2)]
        ORDER += [(2 + e, "attn", 2 + e) for e in range(2)] + [(t % 2, "uw", t) for t in (2, 3)]
        ORDER += [(4, "gm", 0), (2, "qp", 0), (3, "qp", 1)]
        ORDER += [(4 + c, "step", 4 * g + c) for g in range(2) for c in range(NC4)]
        ORDER += [(e, "o", e) for e in range(2)] + [(2 + e, "state", e) for e in range(2)]
        ORDER += [(4 + k, "onT", k) for k in range(KD)] + [(6 + g, "core", g) for g in range(2)]

        def drained(step, n):
            return {"qkT": [(qkT_ready, n + 1)], "attn": [(attn_ready, n + 1)], "uw": [(uw_ready, n + 1)],
                    "gm": [(gm_ready, 1)], "qp": [(qp_ready, n + 1)],
                    "step": [(MT_ready, n + 1), (ku_ready, n + 1)]}[step]

        before = drained_before(ORDER, drained)

        with nc.Fori(0, B) as b:
            with nc.Block() as block:
                @block.sync
                def _(sp):
                    sp.dma_start(gates[:].rearrange("p t n -> p (t n)"),
                                 bg_dram[bass.ds(b, 1), :, :].rearrange("o p n -> (o p) n")).then_inc(rows_in, 16)
                    sp.dma_start(qk[:].rearrange("p t h d -> p (t h d)"),
                                 qk_dram[bass.ds(b, 1), :, :].rearrange("o p n -> (o p) n")).then_inc(rows_in, 16)
                    sp.dma_start(vk[:, :, :, 0], vb_dram[bass.ds(b, 1), :, :].rearrange(
                        "o p (t h d) -> (o p) t h d", h=H2, d=DH)).then_inc(rows_in, 16)
                    for c in range(NC4):
                        part = slice(c * CH, (c + 1) * CH)
                        sp.dma_start(inv[part, :, :, part].rearrange("p t h i -> p (t h) i"),
                                     inv_dram[bass.ds(b, 1), :, :, c].rearrange("o t h j i -> j (o t h) i")).then_inc(inv_in, 16)
                    sp.dma_start(xg[:].rearrange("p t d -> p (t d)"),
                                 xg_dram[bass.ds(b, 1), :, :].rearrange("o p n -> (o p) n")).then_inc(inv_in, 16)
                    for g in range(2):
                        sp.wait_ge(x1_ready, g + 1)
                        sp.dma_start(x1_dram[bass.ds(b, 1), g * 2 * P:(g + 1) * 2 * P, :].rearrange(
                            "o (t p) d -> p (o t) d", p=P), x1[:, 2 * g:2 * g + 2]).then_inc(stored, 16)
                    sp.wait_ge(stored, 32)

                @block.gpsimd
                def _(pool):
                    pool.wait_ge(rows_in, 48)
                    for t in range(TT):
                        pool.tensor_tensor(vk[:, t, :, 1], qk[:, t, H2:],
                                           gates[:, t, 0:H2].unsqueeze(2).broadcast_to([P, H2, DH]), ALU.mult)\
                            .then_inc(kb_ready, 1)
                    for t in range(TT):
                        ins = pool.tensor_copy(gx[:, t], gates[:, t, H2:2 * H2].unsqueeze(2).broadcast_to([P, H2, DH]))
                    ins.then_inc(gx_ready, 1)
                    pool.wait_ge(gm_ready, 1)
                    for t in range(TT):
                        for c in range(NC4):
                            ins = pool.tensor_tensor(gI[:, t, c], eye[:].unsqueeze(1).broadcast_to([P, 2, DH]),
                                                     gm[:, t, :, c].unsqueeze(2).broadcast_to([P, 2, DH]), ALU.mult)
                        ins.then_inc(gI_ready, 1)
                    pool.wait_ge(oss_ready, 1)
                    pool.tensor_tensor(ors[:].rearrange("p e n -> p (e n)"), oss[:].rearrange("p e n -> p (e n)"),
                                       half[:], ALU.pow).then_inc(ors_ready, 1)

                @block.tensor
                def _(pe):
                    def fill(i, step, n):
                        for s, value in before[i, step, n]:
                            pe.wait_ge(s, value)
                        return R[i]

                    pe.wait_ge(rows_in, 48)
                    for t in range(TT):
                        o = fill(t % 2, "qkT", t)
                        for i in range(4):
                            last = pe.transpose(o[:, i * P:(i + 1) * P],
                                                qk[:, t, 2 * i:2 * i + 2].rearrange("p a d -> p (a d)"), ident[:])
                        last.then_inc(qkT_psum, 1)

                    def attention(g):
                        pe.wait_ge(qkT_ready, 2 * g + 2)
                        for e in range(2):
                            o = fill(2 + e, "attn", 2 * g + e)
                            part = slice(e * DH, (e + 1) * DH)
                            for tt in range(2):
                                for i in range(2):
                                    t, j = 2 * g + tt, 2 * tt + i
                                    last = pe.matmul(o[:, j * P:(j + 1) * P], qkT[part, t, 2 + i], qkT[part, t, i],
                                                     start=True, stop=True)
                            last.then_inc(attn_psum, 1)

                    def solve(t):
                        if t == 0:
                            pe.wait_ge(inv_in, 16 * (NC4 + 1))
                        pe.wait_ge(kb_ready, t + 1)
                        o = fill(t % 2, "uw", t)
                        for h in range(H2):
                            last = pe.matmul(o[:, h * P:(h + 1) * P], inv[:, t, h],
                                             vk[:, t, h].rearrange("p a d -> p (a d)"), start=True, stop=True)
                        last.then_inc(uw_psum, 1)

                    attention(0)
                    solve(0)
                    solve(1)
                    attention(1)
                    solve(2)
                    solve(3)
                    pe.wait_ge(gx_ready, 1)
                    o = fill(4, "gm", 0)
                    for t in range(TT):
                        for i in range(2):
                            j = (2 * t + i) * NC4
                            last = pe.matmul(o[:, j:j + NC4], gx[:, t, 2 * i:2 * i + 2].rearrange("p a d -> p (a d)"),
                                             chunk_of[:], start=True, stop=True)
                    last.then_inc(gm_psum, 1)
                    for g in range(2):
                        pe.wait_ge(uw_ready, 2 * g + 2)
                        pe.wait_ge(attn_ready, 2 * g + 2)
                        o = fill(2 + g, "qp", g)
                        for tt in range(2):
                            for h in range(H2):
                                t, i, e = 2 * g + tt, h // 2, h % 2
                                last = pe.matmul(o[e * DH:(e + 1) * DH, (2 * tt + i) * P:(2 * tt + i + 1) * P],
                                                 uw[:, t, h, 1], attn[:, e, t, i], start=True, stop=True)
                        last.then_inc(qp_psum, 1)
                    for g in range(2):
                        for c in range(NC4):
                            o = fill(4 + c, "step", 4 * g + c)
                            part = slice(c * CH, (c + 1) * CH)
                            for tt in range(2):
                                for h in range(H2):
                                    t, i, e = 2 * g + tt, h // 2, h % 2
                                    keys = qk[part, t, H2 + h]
                                    at = 4 * tt + i
                                    for lhs, rhs, j in ((uw[part, t, h, 1], keys, at), (keys, uw[part, t, h, 0], at + 2)):
                                        last = pe.matmul(o[e * DH:(e + 1) * DH, j * DH:(j + 1) * DH], lhs, rhs,
                                                         start=True, stop=True, tile_position=(c * CH, e * DH))
                            last.then_inc(step_psum, 1)
                    for n in range(NCH):
                        t, c = divmod(n, NC4)
                        for e in range(2):
                            part = slice(e * DH, (e + 1) * DH)
                            if n > 0:
                                pe.wait_ge(state_ready[e], n)
                            if n < NCH - 1:
                                if n == 0:
                                    fill(2 + e, "state", e)
                                pe.wait_ge(MT_ready, 4 * (t // 2) + c + 1)
                                for i in range(2):
                                    last = pe.matmul(R[2 + e][part, i * DH:(i + 1) * DH], MT[part, t, c, i], S[part, n, i],
                                                     start=True, stop=True)
                                last.then_inc(state_psum[e], 1)
                            if n == 0:
                                fill(e, "o", e)
                                pe.wait_ge(qp_ready, 2)
                            for i in range(2):
                                o = R[e][:, (2 * t + i) * DH:(2 * t + i + 1) * DH]
                                if c == 0:
                                    pe.matmul(o, attn[:, e, t, i], uw[:, t, 2 * i + e, 0], start=i == 0, stop=False,
                                              skip_group_check=True)
                            for i in range(2):
                                o = R[e][:, (2 * t + i) * DH:(2 * t + i + 1) * DH]
                                last = pe.matmul(o[c * CH:(c + 1) * CH], qpT[part, t, i, c * CH:(c + 1) * CH], S[part, n, i],
                                                 start=False, stop=c == NC4 - 1, skip_group_check=True,
                                                 tile_position=(e * DH, c * CH))
                            if n == NCH - 1:
                                last.then_inc(o_psum, 1)
                    pe.wait_ge(on_ready, 2)
                    for k in range(KD):
                        o = fill(4 + k, "onT", k)
                        for t in range(TT):
                            last = pe.transpose(o[:, t * P:(t + 1) * P],
                                                on[:, t, 2 * k:2 * k + 2].rearrange("p a d -> p (a d)"), ident[:])
                        last.then_inc(onT_psum, 1)
                    pe.wait_ge(onT_ready, KD)
                    for g in range(2):
                        o = fill(6 + g, "core", g)
                        for tt in range(2):
                            for k in range(KD):
                                t = 2 * g + tt
                                last = pe.matmul(o[:, tt * D:(tt + 1) * D], onT[:, k, t * P:(t + 1) * P], wo[:, k],
                                                 start=k == 0, stop=k == KD - 1)
                        last.then_inc(core_psum, 1)

                @block.scalar
                def _(act):
                    for t in range(TT):
                        act.wait_ge(qkT_psum, t + 1)
                        act.copy(qkT[:, t].rearrange("p a n -> p (a n)"), R[t % 2][:, :]).then_inc(qkT_ready, 1)
                    for t in range(TT):
                        act.wait_ge(uw_psum, t + 1)
                        act.copy(uw[:, t].rearrange("p h a d -> p (h a d)"), R[t % 2][:, :]).then_inc(uw_ready, 1)
                    for n in range(2 * NC4):
                        g, c = divmod(n, NC4)
                        act.wait_ge(step_psum, n + 1)
                        act.wait_ge(MT_ready, n + 1)
                        act.copy(kb_u[:, 2 * g:2 * g + 2, c].rearrange("p t i d -> p t (i d)"),
                                 R[4 + c][:, :].rearrange("p (t s n) -> p t s n", t=2, s=2)[:, :, 1]).then_inc(ku_ready, 1)
                    for e in range(2):
                        act.wait_ge(o_psum, e + 1)
                        act.activation(osq[:, e].rearrange("p n d -> p (n d)"), R[e][:, :], ACT.Square).then_inc(osq_ready, 1)
                    act.wait_ge(onT_psum, 1)
                    act.copy(onT[:, 0], R[4][:, :]).then_inc(onT_ready, 1)

                @block.vector
                def _(dve):
                    link = Chain(dve, dve_chain)

                    def mask(n):
                        g, e = divmod(n, 2)
                        dve.wait_ge(attn_psum, n + 1)
                        dve.tensor_tensor(attn[:, e, 2 * g:2 * g + 2].rearrange("p t i n -> p (t i) n"),
                                          R[2 + e][:, :].rearrange("p (j n) -> p j n", n=P),
                                          causal[:].unsqueeze(1).broadcast_to([P, 4, P]), ALU.mult).then_inc(attn_ready, 1)

                    for n in range(4):
                        mask(n)
                    dve.wait_ge(gm_psum, 1)
                    dve.tensor_copy(gm[:].rearrange("p t i c -> p (t i c)"), R[4][:, 0:TT * 2 * NC4]).then_inc(gm_ready, 1)
                    for g in range(2):
                        dve.wait_ge(qp_psum, g + 1)
                        dve.wait_ge(qkT_ready, TT)
                        dve.scalar_tensor_tensor(out=qpT[:, 2 * g:2 * g + 2].rearrange("p t i n -> p t (i n)"),
                                                 in0=R[2 + g][:, :].rearrange("p (t n) -> p t n", t=2), scalar=-1.0,
                                                 in1=qkT[:, 2 * g:2 * g + 2, 0:2].rearrange("p t i n -> p t (i n)"),
                                                 op0=ALU.mult, op1=ALU.add).then_inc(qp_ready, 1)
                    for n in range(2 * NC4):
                        g, c = divmod(n, NC4)
                        dve.wait_ge(step_psum, n + 1)
                        dve.wait_ge(gI_ready, 2 * g + 2)
                        dve.tensor_tensor(MT[:, 2 * g:2 * g + 2, c].rearrange("p t i d -> p t (i d)"),
                                          gI[:, 2 * g:2 * g + 2, c].rearrange("p t i d -> p t (i d)"),
                                          R[4 + c][:, :].rearrange("p (t s n) -> p t s n", t=2, s=2)[:, :, 0],
                                          ALU.subtract).then_inc(MT_ready, 1)
                    for n in range(NCH - 1):
                        t, c = divmod(n, NC4)
                        for e in range(2):
                            part = slice(e * DH, (e + 1) * DH)
                            dve.wait_ge(state_psum[e], n + 1)
                            dve.wait_ge(ku_ready, 4 * (t // 2) + c + 1)
                            dve.tensor_tensor(S[part, n + 1].rearrange("p i d -> p (i d)"), R[2 + e][part, 0:2 * DH],
                                              kb_u[part, t, c].rearrange("p i d -> p (i d)"), ALU.add)\
                               .then_inc(state_ready[e], 1)
                    dve.wait_ge(osq_ready, 2)
                    link(dve.tensor_reduce(oss[:].rearrange("p e n -> p (e n)"),
                                           osq[:].rearrange("p e n d -> p (e n) d"), AX.X, ALU.add))
                    dve.tensor_scalar(oss[:], oss[:], 1.0 / DH, 1e-5, ALU.mult, ALU.add).then_inc(oss_ready, 1)
                    dve.wait_ge(ors_ready, 1)
                    for e in range(2):
                        dve.tensor_tensor(on[:].rearrange("p t (i e) d -> p (t i) e d", e=2)[:, :, e],
                                          R[e][:, :].rearrange("p (n d) -> p n d", d=DH),
                                          ors[:, e].unsqueeze(2).broadcast_to([P, TT * 2, DH]), ALU.mult).then_inc(on_ready, 1)
                    dve.wait_ge(onT_psum, 2)
                    dve.tensor_copy(onT[:, 1], R[5][:, :]).then_inc(onT_ready, 1)
                    for g in range(2):
                        ts = slice(2 * g, 2 * g + 2)
                        dve.wait_ge(core_psum, g + 1)
                        dve.tensor_tensor(x1[:, ts].rearrange("p t d -> p (t d)"), R[6 + g][:, :],
                                          xg[:, ts].rearrange("p t d -> p (t d)"), ALU.add).then_inc(x1_ready, 1)
            clear(nc, sems)


def rank_below(dve, link, out, vals, lower, gt, ge, n_rows, n, k):
    other = vals.unsqueeze(2).broadcast_to([P, n_rows, n, n])
    own = vals.unsqueeze(3).broadcast_to([P, n_rows, n, n])
    g = gt[:, 0:n_rows * n * n].rearrange("p (r e f) -> p r e f", e=n, f=n)
    q = ge[:, 0:n_rows * n * n].rearrange("p (r e f) -> p r e f", e=n, f=n)
    dve.tensor_tensor(g, other, own, ALU.is_gt)
    link(dve.tensor_tensor(q, other, own, ALU.is_ge))
    link(dve.tensor_tensor(q, q, lower[:, 0:n, 0:n].unsqueeze(1).broadcast_to([P, n_rows, n, n]), ALU.mult))
    link(dve.tensor_tensor(g, g, q, ALU.max))
    link(dve.tensor_reduce(out, g, AX.X, ALU.add))
    link(dve.tensor_scalar(out, out, float(k), None, ALU.is_lt))


def mixtures_phase(nc, a, x1_dram, out):
    with ExitStack() as ctx:
        sb, bank, sem, sems = space(nc, ctx, "m")
        ident = sb("ident", [P, P])
        ident16 = sb("ident16", [P, P], BF16)
        lower = sb("lower", [P, E2, E2])
        pick_in = sb("pick_in", [3 * E2, 2, 8, P])
        pick = sb("pick", [3 * E2, 2, 8, P], BF16)
        wt = sb("wt", [P, KD, E1])
        wg = sb("wg", [DH, E1])
        cond_now = sb("cond_now", [DH, 1])
        condb = sb("condb", [DH, P])
        wr = sb("wr", [P, KD, E2])
        cb = sb("cb", [P, E2])
        N1S, N1 = S1 // P, S1 // P + E1
        N2S, N2 = S2W // P, S2W // P + E2 // 2
        gate = [sb("gate1", [P, KD, N1, P]), sb("gate2", [P, KD, N2, P])]
        up = [sb("up1", [P, KD, N1, P]), sb("up2", [P, KD, N2, P])]
        down = [sb("down1", [P, N1, D]), sb("down2", [P, N2, D])]

        x1 = sb("x1", [P, TT, D])
        inT = [sb("x1T", [P, KD, L]), sb("yT", [P, KD, L])]
        lg = sb("lg", [P, TT, E2])
        mx = sb("mx", [P, TT])
        ex = sb("ex", [P, TT, E2])
        sc = sb("sc", [P, TT, E2])
        sbias = sb("sbias", [P, TT, E2])
        sel = sb("sel", [P, TT, E2])
        gsum = sb("gsum", [P, TT, G2])
        gsel = sb("gsel", [P, TT, G2])
        goff = sb("goff", [P, TT, G2])
        gt = sb("gt", [P, TT * E2 * E2])
        ge = sb("ge", [P, TT * E2 * E2])
        wsum = sb("wsum", [P, TT])
        w = sb("w", [P, TT, E2])
        rest = sb("rest", [P, TT, E2])
        parts = sb("parts", [P, TT, 3 * E2], BF16)
        wT = sb("wT", [3 * E2, L], BF16)
        act_g = sb("act_g", [P, 2, L])
        hid = sb("hid", [P, 3, L])
        outT = sb("outT", [P, KD, L])
        res = sb("res", [P, TT, D])

        GB = [bank(f"G{i}") for i in range(2)]
        UB = [bank(f"U{i}") for i in range(2)]
        YB = [bank(f"Y{i}") for i in range(2)]
        WB = bank("W")
        MB = bank("M")
        MB16 = MB[:, :].bitcast(BF16)

        loaded = sem("loaded")
        dve_chain = sem("dve_chain")

        with nc.Block() as block:
            @block.sync
            def _(sp):
                loads = [(ident[:], a["c_ident"]), (lower[:], a["c_lower"]), (pick_in[:], a["c_pick"]),
                         (wt[:], a["L0_cond2_wt"]), (wg[:], a["L0_cond2_wg"]),
                         (wr[:], a["L0_ffn_router_w"]), (cb[:], row(a["L0_ffn_correction_bias"], E2)),
                         (down[0][:, 0:N1S], a["L0_cond2_sw_down"].rearrange("(i p) n -> p i n", p=P)),
                         (down[0][:, N1S:], a["L0_cond2_w_down"].rearrange("e m n -> m e n")),
                         (down[1][:, 0:N2S], a["L0_ffn_shared_down_w"].rearrange("(i p) n -> p i n", p=P)),
                         (down[1][:, N2S:], a["L0_ffn_down_w"].rearrange("(i e) m n -> (e m) i n", e=2))]
                for k in range(KD):
                    ks = slice(k * P, (k + 1) * P)
                    for dst, shared, own in ((gate, ("L0_cond2_sw_gate", "L0_ffn_shared_gate_w"),
                                              ("L0_cond2_w_gate", "L0_ffn_gate_w")),
                                             (up, ("L0_cond2_sw_up", "L0_ffn_shared_up_w"),
                                              ("L0_cond2_w_up", "L0_ffn_up_w"))):
                        for m, ns in ((0, N1S), (1, N2S)):
                            loads.append((dst[m][:, k, 0:ns].rearrange("p i n -> p (i n)"), a[shared[m]][ks, :]))
                            width = (M1, M2)[m]
                            loads.append((dst[m][:, k, ns:].rearrange("p i n -> p (i n)").rearrange(
                                "p (e m) -> p e m", m=width), a[own[m]][:, ks, :].rearrange("e p m -> p e m")))
                for dst, src in loads:
                    sp.dma_start(dst, src).then_inc(loaded, 16)
                sp.wait_ge(loaded, 16 * len(loads))

            @block.vector
            def _(dve):
                dve.wait_ge(loaded, 16 * 27)
                dve.tensor_copy(ident16[:], ident[:])
                dve.tensor_copy(pick[:], pick_in[:])
        clear(nc, sems)

        x_in = sem("x_in")
        turned = sem("turned")
        inT_act = sem("inT_act")
        inT_dve = sem("inT_dve")
        condb_ready = sem("condb_ready")
        logits_psum = sem("logits_psum")
        logits_read = sem("logits_read")
        shifted = sem("shifted")
        exps_ready = sem("exps_ready")
        parts_ready = sem("parts_ready")
        wT_psum = sem("wT_psum")
        wT_ready = sem("wT_ready")
        gate_psum = sem("gate_psum")
        up_psum = sem("up_psum")
        weight_psum = sem("weight_psum")
        gate_active = sem("gate_active")
        mult_up = sem("mult_up")
        hid_ready = sem("hid_ready")
        hid_used = sem("hid_used")
        y_done = sem("y_done")
        res_ready = sem("res_ready")
        res_out = sem("res_out")

        ITEMS = [(0, i) for i in range(N1)] + [(1, i) for i in range(N2)]
        SHARED = (N1S, N2S)
        NI = (N1, N2)

        def routed(q):
            m, i = ITEMS[q]
            return i >= SHARED[m]

        def n_routed(q):
            return sum(routed(j) for j in range(q + 1))

        with nc.Fori(0, B) as b:
            with nc.Block() as block:
                @block.sync
                def _(sp):
                    sp.dma_start(x1[:], x1_dram[bass.ds(b, 1), :, :].rearrange("o (t p) d -> p (o t) d", p=P)).then_inc(x_in, 16)
                    sp.dma_start(cond_now[:], a["c_cond"][bass.ds(b, 1), :, :].rearrange("o n k -> (o n) k")).then_inc(x_in, 16)
                    for half_of in range(2):
                        sp.wait_ge(res_ready, half_of + 1)
                        ts = slice(2 * half_of, 2 * half_of + 2)
                        sp.dma_start(out[bass.ds(b, 1), half_of * 2 * P:(half_of + 1) * 2 * P, :].rearrange(
                            "o (t p) d -> p (o t) d", p=P), res[:, ts]).then_inc(res_out, 16)
                    sp.wait_ge(res_out, 32)

                @block.tensor
                def _(pe):
                    pe.wait_ge(x_in, 32)
                    for k in range(KD):
                        for t in range(TT):
                            last = pe.transpose(GB[k][:, t * P:(t + 1) * P], x1[:, t, k * P:(k + 1) * P], ident[:])
                        last.then_inc(turned, 1)

                    def router(m):
                        pe.wait_ge(inT_act, m + 1)
                        pe.wait_ge(inT_dve, m + 1)
                        if m == 0:
                            pe.wait_ge(condb_ready, 1)
                        n = (E1, E2)[m]
                        for t in range(TT):
                            o = MB[:, t * n:(t + 1) * n]
                            for k in range(KD):
                                last = pe.matmul(o, inT[m][:, k, t * P:(t + 1) * P], (wt, wr)[m][:, k],
                                                 start=k == 0, stop=m == 1 and k == KD - 1)
                            if m == 0:
                                last = pe.matmul(o, condb[:], wg[:], start=False, stop=True)
                        last.then_inc(logits_psum, 1)

                    def weights_turned(m):
                        pe.wait_ge(parts_ready, m + 1)
                        n = 3 * (E1, E2)[m]
                        for t in range(TT):
                            last = pe.transpose(MB16[0:n, t * P:(t + 1) * P], parts[:, t, 0:n], ident16[:])
                        last.then_inc(wT_psum, 1)

                    def project(q):
                        m, i = ITEMS[q]
                        if q >= 2:
                            pe.wait_ge(gate_active, q - 1)
                            pe.wait_ge(mult_up, q - 1)
                        for dst, wts, psum in ((GB, gate, gate_psum), (UB, up, up_psum)):
                            for k in range(KD):
                                last = pe.matmul(dst[q % 2][:, :], wts[m][:, k, i], inT[m][:, k],
                                                 start=k == 0, stop=k == KD - 1)
                            last.then_inc(psum, 1)

                    def spread(q):
                        m, i = ITEMS[q]
                        if i == SHARED[m]:
                            weights_turned(m)
                            pe.wait_ge(wT_ready, m + 1)
                        n = 3 * (E1, E2)[m]
                        if n_routed(q) > 1:
                            pe.wait_ge(hid_ready, n_routed(q) - 1)
                        pe.matmul(WB[:, :], pick[0:n, m, i - SHARED[m]], wT[0:n, :], start=True,
                                  stop=True).then_inc(weight_psum, 1)

                    def project_down(q):
                        m, i = ITEMS[q]
                        if routed(q):
                            pe.wait_ge(hid_ready, n_routed(q))
                        else:
                            pe.wait_ge(mult_up, q + 1)
                        if m == 1 and i == 0:
                            pe.wait_ge(inT_act, 2)
                            pe.wait_ge(inT_dve, 2)
                        for k in range(KD):
                            last = pe.matmul(YB[k][:, :], down[m][:, i, k * P:(k + 1) * P], hid[:, q % 3],
                                             start=i == 0, stop=i == NI[m] - 1)
                        last.then_inc(hid_used, 1)

                    for m in range(2):
                        first = 0 if m == 0 else N1
                        router(m)
                        for q in range(first, first + NI[m]):
                            project(q)
                            if routed(q):
                                spread(q)
                            if q > first:
                                project_down(q - 1)
                        project_down(first + NI[m] - 1)
                    pe.wait_ge(inT_act, 3)
                    pe.wait_ge(inT_dve, 3)
                    for half_of in range(2):
                        for tt in range(2):
                            t = 2 * half_of + tt
                            for k in range(KD):
                                last = pe.transpose(GB[half_of][:, tt * D + k * P:tt * D + (k + 1) * P],
                                                    outT[:, k, t * P:(t + 1) * P], ident[:])
                        last.then_inc(turned, 1)

                @block.scalar
                def _(act):
                    act.wait_ge(turned, 1)
                    act.copy(inT[0][:, 0], GB[0][:, :]).then_inc(inT_act, 1)

                    def exps(m):
                        act.wait_ge(shifted, m + 1)
                        n = (E1, E2)[m]
                        act.activation(ex[:, :, 0:n], lg[:, :, 0:n], ACT.Exp, scale=(1.0, -1.0)[m]).then_inc(exps_ready, 1)

                    for q, (m, i) in enumerate(ITEMS):
                        if i == 0:
                            exps(m)
                        act.wait_ge(gate_psum, q + 1)
                        if q >= 2:
                            act.wait_ge(mult_up, q - 1)
                        if m == 0:
                            act.copy(act_g[:, q % 2], GB[q % 2][:, :]).then_inc(gate_active, 1)
                        else:
                            act.activation(act_g[:, q % 2], GB[q % 2][:, :], ACT.Silu).then_inc(gate_active, 1)
                        if i == NI[m] - 1:
                            act.wait_ge(hid_used, q + 1)
                            act.copy((inT[1], outT)[m][:, 0], YB[0][:, :]).then_inc(inT_act, 1)

                @block.vector
                def _(dve):
                    link = Chain(dve, dve_chain)
                    dve.wait_ge(x_in, 32)
                    dve.tensor_copy(condb[:], cond_now[:].broadcast_to([DH, P])).then_inc(condb_ready, 1)
                    dve.wait_ge(turned, 2)
                    dve.tensor_copy(inT[0][:, 1], GB[1][:, :]).then_inc(inT_dve, 1)

                    def route(m):
                        n = (E1, E2)[m]
                        rows = TT
                        dve.wait_ge(logits_psum, m + 1)
                        psum = MB[:, 0:TT * n].rearrange("p (t e) -> p t e", e=n)
                        l, e, s = lg[:, :, 0:n], ex[:, :, 0:n], sc[:, :, 0:n]
                        chosen, wn = sel[:, :, 0:n], w[:, :, 0:n]
                        spread_rows = lambda v: v.unsqueeze(2).broadcast_to([P, TT, n])
                        if m == 0:
                            link(dve.tensor_scalar(l, psum, 0.5, None, ALU.mult))
                            link(dve.tensor_reduce(mx[:], l, AX.X, ALU.max))
                            dve.tensor_tensor(l, l, spread_rows(mx[:]), ALU.subtract).then_inc(shifted, 1)
                            dve.wait_ge(exps_ready, 1)
                            link(dve.tensor_reduce(wsum[:], e, AX.X, ALU.add))
                            link(dve.reciprocal(wsum[:], wsum[:]))
                            link(dve.tensor_tensor(s, e, spread_rows(wsum[:]), ALU.mult))
                            rank_below(dve, link, chosen, s, lower, gt, ge, TT, n, 2)
                        else:
                            dve.tensor_copy(l, psum).then_inc(shifted, 1)
                            dve.wait_ge(exps_ready, 2)
                            link(dve.tensor_scalar(e, e, 1.0, None, ALU.add))
                            link(dve.reciprocal(s, e))
                            link(dve.tensor_tensor(sbias[:], s, cb[:].unsqueeze(1).broadcast_to([P, TT, E2]), ALU.add))
                            in_groups = lambda v: v.rearrange("p t (g e) -> p (t g) e", g=G2)
                            rank_below(dve, link, in_groups(chosen), in_groups(sbias[:]), lower, gt, ge, TT * G2,
                                       E2 // G2, 2)
                            link(dve.tensor_tensor(rest[:], sbias[:], chosen, ALU.mult))
                            link(dve.tensor_reduce(gsum[:].rearrange("p t g -> p (t g)"), in_groups(rest[:]), AX.X, ALU.add))
                            rank_below(dve, link, gsel[:], gsum[:], lower, gt, ge, TT, G2, 2)
                            link(dve.tensor_scalar(goff[:], gsel[:], 1.0e30, -1.0e30, ALU.mult, ALU.add))
                            of_group = lambda v: v.rearrange("p t g -> p (t g)").unsqueeze(2).broadcast_to(
                                [P, TT * G2, E2 // G2])
                            link(dve.tensor_tensor(in_groups(sbias[:]), in_groups(sbias[:]), of_group(gsel[:]), ALU.mult))
                            link(dve.tensor_tensor(in_groups(sbias[:]), in_groups(sbias[:]), of_group(goff[:]), ALU.add))
                            rank_below(dve, link, chosen, sbias[:], lower, gt, ge, TT, n, 4)
                        link(dve.tensor_tensor(wn, s, chosen, ALU.mult))
                        link(dve.tensor_reduce(wsum[:], wn, AX.X, ALU.add))
                        link(dve.tensor_scalar(wsum[:], wsum[:], 1e-20, None, ALU.add))
                        link(dve.reciprocal(wsum[:], wsum[:]))
                        link(dve.tensor_tensor(wn, wn, spread_rows(wsum[:]), ALU.mult))
                        r = rest[:, :, 0:n]
                        link(dve.tensor_copy(parts[:, :, 0:n], wn))
                        link(dve.tensor_tensor(r, wn, parts[:, :, 0:n], ALU.subtract))
                        link(dve.tensor_copy(parts[:, :, n:2 * n], r))
                        link(dve.tensor_tensor(r, r, parts[:, :, n:2 * n], ALU.subtract))
                        dve.tensor_copy(parts[:, :, 2 * n:3 * n], r).then_inc(parts_ready, 1)

                    def take_weights(m):
                        n = 3 * (E1, E2)[m]
                        dve.wait_ge(wT_psum, m + 1)
                        if m == 1:
                            dve.wait_ge(weight_psum, E1)
                        dve.tensor_copy(wT[0:n, :], MB16[0:n, 0:L]).then_inc(wT_ready, 1)

                    for q, (m, i) in enumerate(ITEMS):
                        if i == 0:
                            route(m)
                        if i == SHARED[m]:
                            take_weights(m)
                        ag, h = act_g[:, q % 2], hid[:, q % 3]
                        dve.wait_ge(gate_active, q + 1)
                        if q >= 3:
                            dve.wait_ge(hid_used, q - 2)
                        if m == 0:
                            link(dve.scalar_tensor_tensor(out=ag, in0=ag, scalar=0.01, in1=ag, op0=ALU.mult, op1=ALU.max))
                        dve.wait_ge(up_psum, q + 1)
                        if routed(q):
                            dve.tensor_tensor(h, ag, UB[q % 2][:, :], ALU.mult).then_inc(mult_up, 1)
                            dve.wait_ge(mult_up, q + 1)
                            dve.wait_ge(weight_psum, n_routed(q))
                            dve.tensor_tensor(h, h, WB[:, :], ALU.mult).then_inc(hid_ready, 1)
                        else:
                            dve.tensor_tensor(h, ag, UB[q % 2][:, :], ALU.mult).then_inc(mult_up, 1)
                        if i == NI[m] - 1:
                            dve.wait_ge(hid_used, q + 1)
                            dve.tensor_copy((inT[1], outT)[m][:, 1], YB[1][:, :]).then_inc(inT_dve, 1)
                    for half_of in range(2):
                        ts = slice(2 * half_of, 2 * half_of + 2)
                        dve.wait_ge(turned, 3 + half_of)
                        dve.tensor_tensor(res[:, ts].rearrange("p t d -> p (t d)"), GB[half_of][:, :],
                                          x1[:, ts].rearrange("p t d -> p (t d)"), ALU.add).then_inc(res_ready, 1)
            clear(nc, sems)


def bass_adaln(nc, a, out, scratch):
    bias_phase(nc, a, scratch["bias_rows"])
    attention_phase(nc, a, scratch["bias_rows"], scratch["hT"])
    delta_inputs_phase(nc, a, scratch["hT"], scratch["xg"], scratch["qk"], scratch["vb"], scratch["gates"],
                       scratch["low"])
    inverse_phase(nc, a, scratch["low"], scratch["inv"])
    delta_rule_phase(nc, a, scratch["xg"], scratch["qk"], scratch["vb"], scratch["gates"], scratch["inv"],
                     scratch["x1"])
    mixtures_phase(nc, a, scratch["x1"], out)


def kernel(**inputs):
    import numpy as _np
    import concourse.bacc as _bacc
    from concourse import mybir as _mybir
    from concourse.bass_utils import run_bass_kernel_spmd as _run

    names = [n for n in inputs if n != "mask_BxS_bf1"]
    arrays = {n: _np.ascontiguousarray(inputs[n]) for n in names}
    for n in ("L0_cond_g_norm", "L0_cond_g_out"):
        arrays[n] = _np.ascontiguousarray(arrays[n].reshape(-1, P).T)
    arrays["mask"] = _np.ascontiguousarray(inputs["mask_BxS_bf1"]).view(_np.uint8)
    for n in ("x", "mask"):
        arrays[f"{n}_next"] = _np.concatenate([arrays[n][1:], arrays[n][:1]])
    arrays["c_ident"] = _np.eye(P, dtype=_np.float32)
    arrays["c_turn"] = _np.ascontiguousarray(arrays["c_ident"][::-1])
    arrays["c_pos"] = (L - 1 - _np.arange(L).reshape(TT, P).T).astype(_np.float32)
    arrays["c_lower"] = _np.ascontiguousarray(_np.broadcast_to(_np.tril(_np.ones((E2, E2), _np.float32), -1), (P, E2, E2)))
    pick = _np.zeros((3 * E2, 2, 8, P), _np.float32)
    for s in range(3):
        for i in range(8):
            pick[E1 * s + i, 0, i, :] = 1
            for e in range(2):
                pick[E2 * s + 2 * i + e, 1, i, M2 * e:M2 * (e + 1)] = 1
    arrays["c_pick"] = pick
    arrays["c_cond"] = _np.ascontiguousarray(inputs["cond_64"][:, :, None])
    arrays["conv"] = _np.ascontiguousarray(_np.stack([inputs[f"L0_attn_conv_{n}"] for n in "qkv"])
                                           .reshape(3, KD, P, 4).transpose(2, 0, 1, 3))
    arrays["L0_attn_frac_conv_w"] = _np.ascontiguousarray(
        inputs["L0_attn_frac_conv_w"].reshape(4, KD, P, 2).transpose(2, 1, 0, 3))
    angle = _np.arange(L)[:, None] * (1.0 / 10000.0 ** (_np.arange(0, DH, 2) / DH))[None, :]
    for n, f in (("c_cos", _np.cos), ("c_sin", _np.sin)):
        arrays[n] = _np.ascontiguousarray(f(angle).astype(_np.float32).reshape(TT, P, -1).transpose(1, 0, 2))
    at = _np.arange(P)
    same = at[:, None] // CH == at[None, :] // CH
    arrays["c_causal"] = (same & (at[:, None] <= at[None, :])).astype(_np.float32)
    arrays["c_strict"] = -(at[:, None] % CH > _np.arange(CH)[None, :]).astype(_np.float32)
    arrays["c_chunk_of"] = ((at[:, None] // CH == _np.arange(NC4)[None, :]) / CH).astype(_np.float32)
    arrays["c_eye32"] = _np.ascontiguousarray(_np.broadcast_to(_np.eye(CH, dtype=_np.float32), (P, CH, CH)))
    gates = _np.concatenate([inputs[f"L0_attn_{n}"] for n in ("Wb", "Wgamma", "frac_gate_w")], axis=1)
    arrays["gates"] = _np.ascontiguousarray(gates.reshape(KD, P, -1).transpose(1, 0, 2))
    for n in ("L0_cond2_wt", "L0_ffn_router_w"):
        arrays[n] = _np.ascontiguousarray(arrays[n].T.reshape(KD, P, -1).transpose(1, 0, 2))
    arrays["L0_cond2_wg"] = _np.ascontiguousarray(arrays["L0_cond2_wg"].T)
    for n in ("gate", "up", "down"):
        n = f"L0_ffn_shared_{n}_w"
        arrays[n] = _np.ascontiguousarray(arrays[n].T)
    nc = _bacc.Bacc("TRN2", target_bir_lowering=False, num_devices=1)
    a = {}
    fed = {}
    for n, v in arrays.items():
        a[n] = nc.dram_tensor(f"in_{n}", v.shape, _mybir.dt.from_np(v.dtype), kind="ExternalInput").ap()
        fed[f"in_{n}"] = v
    out = nc.dram_tensor("out", [B, L, D], _mybir.dt.float32, kind="ExternalOutput").ap()
    shapes = {"bias_rows": [NH, BIAS_W + 1], "hT": [B + 1, P, KD, L], "xg": [B, P, TT * D], "qk": [B, P, TT * 2 * D],
              "vb": [B, P, TT * D], "gates": [B, P, TT * (2 * H2 + 1)], "low": [B, TT, H2, NC4, CH, CH],
              "inv": [B, TT, H2, NC4, CH, CH], "x1": [B, L, D]}
    scratch = {n: nc.dram_tensor(f"s_{n}", shape, _mybir.dt.float32, kind="Internal").ap() for n, shape in shapes.items()}
    bass_adaln(nc, a, out, scratch)
    r = _run(nc, [fed], core_ids=[0])
    return r.results[0]["out"]
```

```python
from contextlib import ExitStack

import numpy as np
import concourse.bass as bass
from concourse import mybir

F32 = mybir.dt.float32
BF16 = mybir.dt.bfloat16
ALU = mybir.AluOpType
ACT = mybir.ActivationFunctionType
AX = mybir.AxisListType

P = 128
B, L, D = 8, 512, 256
KD = D // P
TT = L // P
NH, DH = 16, 64
QT = NH // 2
QW = NH * DH
SCALE = 8.0
NEG = float(-np.finfo(np.float32).max)
MASKED = -1.0e30
BIAS_W = L + P - 1

H2, CH, NC4 = 4, 32, 4
NCH = L // CH
E1, M1 = 8, 128
S1 = 256
E2, M2 = 16, 64
S2W = 512
G2 = 4


class Chain:

    def __init__(self, eng, sem):
        self.eng, self.sem, self.n = eng, sem, 0

    def __call__(self, ins):
        self.n += 1
        ins.then_inc(self.sem, 1)
        self.eng.wait_ge(self.sem, self.n)


def clear(nc, sems):
    with nc.Block() as block:
        @block.sync
        def _(sp):
            for s in sems:
                sp.sem_clear(s)


def space(nc, ctx, prefix):
    sems = []

    def sb(name, shape, dt=F32):
        return ctx.enter_context(nc.sbuf_tensor(f"{prefix}_{name}", shape, dt))

    def bank(name, dt=F32):
        return ctx.enter_context(nc.psum_tensor(f"{prefix}_{name}", [P, 2048 // (2 if dt == BF16 else 4)], dt))

    def sem(name):
        s = ctx.enter_context(nc.semaphore(f"{prefix}_{name}"))
        sems.append(s)
        return s

    return sb, bank, sem, sems


def row(ap, n):
    return bass.AP(tensor=ap.tensor, offset=ap.offset, ap=[[0, P], [1, n]])


def bias_phase(nc, a, bias_rows):
    with ExitStack() as ctx:
        sb, bank, sem, sems = space(nc, ctx, "r")
        pos = sb("pos", [P, TT])
        ident = sb("ident", [P, P])
        w0, b0, g0, b1, g1 = (sb(n, [P, D]) for n in ("w0", "b0", "g0", "b1", "g1"))
        w1 = sb("w1", [P, KD, D])
        w2 = sb("w2", [P, KD, NH])
        b2 = sb("b2", [NH, 1])
        h = sb("h", [P, TT, D])
        hn = sb("hn", [P, TT, D])
        hT = sb("hT", [P, KD, L])
        stats = sb("stats", [P, TT, 6])
        mv = sb("mv", [P, TT, 2])
        ve = sb("ve", [P, TT])
        half = sb("half", [P, TT])
        rstd = sb("rstd", [P, TT])
        rows = sb("rows", [NH, BIAS_W + 1])
        ps = [bank(f"ps{i}") for i in range(4)]

        loaded = sem("loaded")
        half_ready = sem("half_ready")
        var_ready = sem("var_ready")
        rstd_ready = sem("rstd_ready")
        h_normed = sem("h_normed")
        h_active = sem("h_active")
        hT_psum = sem("hT_psum")
        hT_ready = sem("hT_ready")
        prod_psum = sem("prod_psum")
        rows_ready = sem("rows_ready")
        rows_out = sem("rows_out")
        dve_chain = sem("dve_chain")

        with nc.Block() as block:
            @block.sync
            def _(sp):
                loads = [(pos[:], a["c_pos"]), (ident[:], a["c_ident"]), (w0[:], row(a["L0_cond_w0"], D)),
                         (b0[:], row(a["L0_cond_b0"], D)), (g0[:], row(a["L0_cond_g0"], D)),
                         (b1[:], row(a["L0_cond_b1"], D)), (g1[:], row(a["L0_cond_g1"], D)),
                         (w1[:], a["L0_cond_w1"].rearrange("(k p) n -> p k n", p=P)),
                         (w2[:], a["L0_cond_w2"].rearrange("(k p) n -> p k n", p=P)),
                         (b2[:], a["L0_cond_b2"].rearrange("(n o) -> n o", o=1))]
                for dst, src in loads:
                    sp.dma_start(dst, src).then_inc(loaded, 16)
                sp.wait_ge(rows_ready, 1)
                sp.dma_start(bias_rows[:, :], rows[:, :]).then_inc(rows_out, 16)
                sp.wait_ge(rows_out, 16)

            N_LOADS = 160

            @block.gpsimd
            def _(pool):
                pool.memset(half[:], -0.5).then_inc(half_ready, 1)
                pool.wait_ge(half_ready, 1)
                for layer in range(2):
                    pool.wait_ge(var_ready, layer + 1)
                    pool.tensor_tensor(rstd[:], ve[:], half[:], ALU.pow).then_inc(rstd_ready, 1)

            @block.vector
            def _(dve):
                link = Chain(dve, dve_chain)
                link(dve.memset(rows[:, L:], NEG))
                dve.wait_ge(loaded, N_LOADS)
                for layer in range(2):
                    gain = (g0, g1)[layer]
                    if layer == 0:
                        for t in range(TT):
                            last = dve.scalar_tensor_tensor(out=h[:, t], in0=w0[:], scalar=pos[:, t:t + 1],
                                                            in1=b0[:], op0=ALU.mult, op1=ALU.add)
                        link(last)
                    else:
                        for t in range(TT):
                            dve.wait_ge(prod_psum, t + 1)
                            last = dve.tensor_tensor(h[:, t], ps[t][:, 0:D], b1[:], ALU.add)
                        link(last)
                    for t in range(TT):
                        last = dve.bn_stats(stats[:, t], h[:, t])
                    link(last)
                    for t in range(TT):
                        last = dve.bn_aggr(mv[:, t], stats[:, t])
                    link(last)
                    dve.tensor_scalar(ve[:], mv[:, :, 1], 1e-5, None, ALU.add).then_inc(var_ready, 1)
                    dve.wait_ge(rstd_ready, layer + 1)
                    for t in range(TT):
                        last = dve.tensor_scalar(hn[:, t], h[:, t], mv[:, t, 0:1], rstd[:, t:t + 1],
                                                 ALU.subtract, ALU.mult)
                    link(last)
                    for t in range(TT):
                        last = dve.tensor_tensor(hn[:, t], hn[:, t], gain[:], ALU.mult)
                    last.then_inc(h_normed, 1)
                    for k in range(KD):
                        dve.wait_ge(hT_psum, KD * layer + k + 1)
                        dve.tensor_copy(hT[:, k], ps[k][:, :]).then_inc(hT_ready, 1)
                dve.wait_ge(prod_psum, TT + 1)
                dve.tensor_scalar(rows[:, 0:L], ps[2][0:NH, :], b2[:, 0:1], None, ALU.add).then_inc(rows_ready, 1)

            @block.scalar
            def _(act):
                for layer in range(2):
                    act.wait_ge(h_normed, layer + 1)
                    act.activation(hn[:], hn[:], ACT.Silu).then_inc(h_active, 1)

            @block.tensor
            def _(pe):
                pe.wait_ge(loaded, N_LOADS)
                for layer in range(2):
                    pe.wait_ge(h_active, layer + 1)
                    for k in range(KD):
                        for t in range(TT):
                            last = pe.transpose(ps[k][:, t * P:(t + 1) * P], hn[:, t, k * P:(k + 1) * P], ident[:])
                        last.then_inc(hT_psum, 1)
                    pe.wait_ge(hT_ready, KD * (layer + 1))
                    if layer == 0:
                        for t in range(TT):
                            for k in range(KD):
                                last = pe.matmul(ps[t][:, 0:D], hT[:, k, t * P:(t + 1) * P], w1[:, k],
                                                 start=k == 0, stop=k == KD - 1)
                            last.then_inc(prod_psum, 1)
                    else:
                        for k in range(KD):
                            last = pe.matmul(ps[2][0:NH, :], w2[:, k], hT[:, k], start=k == 0, stop=k == KD - 1)
                        last.then_inc(prod_psum, 1)
        clear(nc, sems)


def attention_phase(nc, a, bias_rows, hT_dram):
    QK_LAG, PV_LAG, S_SLOTS, PT_SLOTS = 2, 4, 5, 3
    F32R = mybir.dt.float32r
    with ExitStack() as ctx:
        sb, bank, sem, sems = space(nc, ctx, "a")
        ident = sb("ident", [P, P])
        turn = sb("turn", [P, P])
        QKVN = QW + 2 * DH + NH
        w_in = sb("w_in", [P, QKVN])
        wqkv = [sb(f"wqkv{i}", [P, KD, QKVN], F32R) for i in range(2)]
        wout = sb("wout", [P, QT, D])
        bias = sb("bias", [P, NH, L])
        gn = sb("gn", [P, KD])
        go = sb("go", [P, KD])
        kscale = sb("kscale", [P, 3])
        nullk = sb("nullk", [P, DH])
        nulln = sb("nulln", [P, 2])
        scales = sb("scales", [P, 2, DH])
        nullv = sb("nullv", [P, DH])
        nullb = sb("nullb", [P, NH])
        half = sb("half", [P, NH + 2])
        ones = sb("ones", [1, P], BF16)
        mask_in = sb("mask_in", [1, L], mybir.dt.uint8)
        mask_row = sb("mask_row", [1, L], BF16)

        x = sb("x", [P, TT, D])
        stats = sb("stats", [P, 6])
        mv = sb("mv", [P, 2])
        ve = sb("ve", [P, 1])
        rstd = sb("rstd", [P, 1])
        xn = sb("xn", [P, D])
        xnT = [sb(f"xnT{i}", [P, KD, P], F32R) for i in range(2)]
        qraw = sb("qraw", [P, NH + 1, DH])
        sq = sb("sq", [P, NH + 1, DH])
        ss = sb("ss", [P, NH + 1])
        rr = sb("rr", [P, NH + 1])
        qn = sb("qn", [P, NH, DH])
        kn = sb("kn", [P, 2, DH])
        qs = sb("qs", [P, NH, 2, DH], F32R)
        qT = sb("qT", [P, 2, NH, P], F32R)
        kf = sb("kf", [P, P])
        kT = [sb(f"kT{i}", [P, L], F32R) for i in range(2)]
        v = sb("v", [P, TT, DH])
        k_next = [sb(f"k_next{i}", [P, P], F32R) for i in range(2)]
        v_next = sb("v_next", [P, DH])
        nraw = sb("nraw", [P, NH])
        nsn = sb("nsn", [P, 2, NH])
        S = sb("S", [P, S_SLOTS, L])
        PT = sb("PT", [P, PT_SLOTS, L])
        nm = sb("nm", [P, 2, NH])
        den = sb("den", [P, 2, NH])
        dn = sb("dn", [P, 2, NH // 2])
        pn = sb("pn", [P, 2, NH // 2])
        dent = sb("dent", [P, 2, NH // 2])
        rden = sb("rden", [P, 2, NH // 2])
        pnr = sb("pnr", [P, 2, NH // 2])
        onull = sb("onull", [P, NH // 2, DH])
        o = sb("o", [P, NH, DH])
        oT = sb("oT", [P, QT, P])
        stats2 = sb("stats2", [P, 6])
        mv2 = sb("mv2", [P, 2])
        ve2 = sb("ve2", [P, 1])
        rstd2 = sb("rstd2", [P, 1])
        hn = sb("hn", [P, D])
        hT = sb("hT", [P, TT, KD, P])

        SB = [bank(f"S{i}") for i in range(2)]
        TB = [bank(f"T{i}") for i in range(2)]
        OB = [bank(f"O{i}") for i in range(2)]
        FB = [bank(f"F{i}") for i in range(2)]

        loaded = sem("loaded")
        w_loaded = sem("w_loaded")
        wout_loaded = sem("wout_loaded")
        w_split = sem("w_split")
        BIAS_LOADS = 4
        bias_loaded = [sem(f"bias_loaded{i}") for i in range(BIAS_LOADS)]
        prep = sem("prep")
        bias_psum = sem("bias_psum")
        bias_act = sem("bias_act")
        dve_chain = sem("dve_chain")
        pool_chain = sem("pool_chain")

        with nc.Block() as block:
            N_LOADS = 15

            @block.sync
            def _(sp):
                loads = [(gn[:], a["L0_cond_g_norm"]), (go[:], a["L0_cond_g_out"]),
                         (turn[:], a["c_turn"]), (ident[:], a["c_ident"]),
                         (kscale[0:DH, 0:1], a["L0_cond_q_scale"].rearrange("(n o) -> n o", o=1)),
                         (kscale[DH:P, 0:1], a["L0_cond_q_scale"].rearrange("(n o) -> n o", o=1)),
                         (kscale[0:DH, 1:2], a["L0_cond_k_scale"].rearrange("(n o) -> n o", o=1)),
                         (kscale[DH:P, 1:2], a["L0_cond_k_scale"].rearrange("(n o) -> n o", o=1)),
                         (nullv[:], row(a["cond_64"][1, :], DH)),
                         (nullb[:], row(a["L0_cond_null_attn_bias"], NH)),
                         (nullk[:], row(a["cond_64"][0, :], DH)),
                         (scales[:, 0], row(a["L0_cond_q_scale"], DH)),
                         (scales[:, 1], row(a["L0_cond_k_scale"], DH)),
                         (x[:], a["x"][0].rearrange("(t p) d -> p t d", p=P)),
                         (mask_in[:], a["mask"][0:1, :])]
                assert len(loads) == N_LOADS

                def load_weights(k):
                    sp.dma_start(w_in[:, 0:QW], a["L0_cond_Wq"][k * P:(k + 1) * P, :]).then_inc(w_loaded, 16)
                    sp.dma_start(w_in[:, QW:QW + 2 * DH], a["L0_cond_Wkv"][k * P:(k + 1) * P, :]).then_inc(w_loaded, 16)

                load_weights(0)
                for dst, src in loads:
                    sp.dma_start(dst, src).then_inc(loaded, 16)
                for k in range(1, KD):
                    sp.wait_ge(w_split, k)
                    load_weights(k)
                sp.dma_start(wout[:], a["L0_cond_Wout"].rearrange("(k p) n -> p k n", p=P)).then_inc(wout_loaded, 16)
                sp.wait_ge(wout_loaded, 16)

            @block.gpsimd
            def _(pool):
                for tile in (nsn, nm, o):
                    pool.memset(tile[:], 0.0)
                pool.memset(den[:], 1.0)
                pool.memset(half[:], -0.5).then_inc(pool_chain, 1)
                pool.wait_ge(prep, 1)
                pool.wait_ge(pool_chain, 1)
                pool.tensor_tensor(nulln[:, 1:2], nulln[:, 0:1], half[:, 0:1], ALU.pow).then_inc(pool_chain, 1)

            @block.vector
            def _(dve):
                link = Chain(dve, dve_chain)
                dve.memset(ones[:], 1.0)
                dve.wait_ge(loaded, 16 * N_LOADS)
                link(dve.tensor_scalar(kscale[:, 2:3], kscale[:, 0:1], kscale[:, 1:2], SCALE, ALU.mult, ALU.mult))
                link(dve.tensor_tensor(sq[:, 0], nullk[:], nullk[:], ALU.mult))
                link(dve.tensor_reduce(nulln[:, 0:1], sq[:, 0], AX.X, ALU.add))
                dve.tensor_scalar(nulln[:, 0:1], nulln[:, 0:1], 1e-24, None, ALU.max).then_inc(prep, 1)
                dve.wait_ge(pool_chain, 2)
                dve.wait_ge(prep, 1)
                link(dve.tensor_scalar(nullk[:], nullk[:], nulln[:, 1:2], SCALE, ALU.mult, ALU.mult))
                for i in range(2):
                    link(dve.tensor_tensor(nullk[:], nullk[:], scales[:, i], ALU.mult))
                for k in range(KD):
                    dve.wait_ge(w_loaded, 32 * (k + 1))
                    link(dve.tensor_tensor(qn[:], w_in[:, 0:QW].rearrange("p (h d) -> p h d", d=DH),
                                           nullk[:].unsqueeze(1).broadcast_to([P, NH, DH]), ALU.mult))
                    link(dve.tensor_reduce(w_in[:, QW + 2 * DH:], qn[:], AX.X, ALU.add))
                    link(dve.tensor_scalar(w_in[:], w_in[:], gn[:, k:k + 1], None, ALU.mult))
                    link(dve.tensor_copy(wqkv[0][:, k], w_in[:]))
                    dve.tensor_tensor(wqkv[1][:, k], w_in[:], wqkv[0][:, k].bitcast(F32), ALU.subtract)\
                       .then_inc(w_split, 1)

            @block.tensor
            def _(pe):
                pe.wait_ge(loaded, 16 * N_LOADS)
                for n in range(2 * TT):
                    pe.matmul(OB[n // TT][:, n % TT * P:(n % TT + 1) * P], ident[:], ident[:], start=True, stop=True)
                for h in range(NH):
                    if h % (NH // BIAS_LOADS) == 0:
                        pe.wait_ge(bias_loaded[h // (NH // BIAS_LOADS)], 16)
                    if h >= 4:
                        pe.wait_ge(bias_act, h - 3)
                    pe.matmul((SB + TB)[h % 4][:, :], turn[:], bias[:, h], start=True, stop=True).then_inc(bias_psum, 1)

            @block.scalar
            def _(act):
                for i in range(BIAS_LOADS):
                    n = NH // BIAS_LOADS
                    toeplitz = bass.AP(tensor=bias_rows.tensor, offset=i * n * (BIAS_W + 1),
                                       ap=[[1, P], [BIAS_W + 1, n], [1, L]])
                    act.dma_start(bias[:, i * n:(i + 1) * n], toeplitz).then_inc(bias_loaded[i], 16)
                for h in range(NH):
                    act.wait_ge(bias_psum, h + 1)
                    act.copy(bias[:, h], (SB + TB)[h % 4][:, :]).then_inc(bias_act, 1)
        clear(nc, sems)

        names = ["x_first", "x_rest", "mask_read", "next_taken", "x_var", "x_rstd", "xn_ready",
                 "xnT_high", "xnT_low", "q_ready", "kv_ready", "sq_ready", "ss_ready", "rr_ready", "qn_ready",
                 "q_high", "q_low", "kn_ready", "qT_act", "qT_dve", "kT_read", "kT_ready", "null_ready",
                 "scores_psum", "scores_ready", "probs_ready", "probsT_psum", "probsT_act", "probsT_dve", "pv_done",
                 "null_diff", "null_probs", "weights_ready", "onull_ready", "o_scaled", "o_ready", "oT_act",
                 "oT_dve", "out_var", "out_rstd", "hn_ready", "hT_ready", "hT_out"]
        s = {n: sem(n) for n in names}
        full = [sem(f"F{i}_filled") for i in range(2)]

        FRONT = {"stat": -5, "xn": -3, "xT": -2, "q0": 0, "q1": 1, "kv": 2, "ss": 3, "qn": 4, "kT": 7,
                 "null": 10, "qs0": 8, "qs1": 9, "qT0": 12, "qT1": 12, "qT2": 13, "qT3": 14}
        FRONT_1 = {"stat": 0, "xn": 1, "xT": 2, "q0": 4, "q1": 4, "kv": 4, "ss": 5, "qn": 6, "kT": 14,
                   "null": 15, "qs0": 11, "qs1": 12, "qT0": 13, "qT1": 14, "qT2": 14, "qT3": 15}
        BACK = {"diff1": 0, "weigh1": 4, "oT": 6, "outp": 9, "hn": 11, "hT": 13}

        def iteration():
            behind = {}
            for t in range(TT):
                behind.setdefault(NH * t + 10, []).append(("diff0", t))
                behind.setdefault(NH * t + 13, []).append(("weigh0", t))
                for n, h in BACK.items():
                    behind.setdefault(NH * t + h, []).append((n, t - 1))
            for t in range(1, TT + 1):
                for n, h in ({**FRONT, **FRONT_1} if t == 1 else FRONT).items():
                    behind.setdefault(NH * (t - 1) + h, []).append((n, t))
            steps = []
            for n in range(NH * TT):
                steps += [("head", n)] + behind.get(n, [])
            return steps + [("head", NH * TT + i) for i in range(PV_LAG)]

        FILLS = {"xT": 0, "q0": 1, "q1": 0, "kv": 1, "qT0": 0, "qT1": 1, "qT2": 0, "qT3": 1, "kT": 0,
                 "outp": 0, "hT": 1}

        def evac_by_dve(n):
            return n % 4 == 3

        def count_dve(n):
            return (n + 1) // 4

        def run(steps, b):
            number, seen = {}, {}
            for name, t in steps:
                seen[name] = seen.get(name, 0) + 1
                number[name, t] = seen[name]

            def done(name, t):
                return number.get((name, t), 0)

            def drained(name, t):
                n = done(name, t)
                return {"xT": [(s["xnT_low"], n)], "q0": [(s["q_ready"], 2 * n - 1)],
                        "q1": [(s["q_ready"], 2 * n)], "kv": [(s["kv_ready"], 3 * n), (s["sq_ready"], 3 * n)],
                        "qT0": [(s["qT_act"], 2 * n - 1)], "qT1": [(s["qT_dve"], 2 * n - 1)],
                        "qT2": [(s["qT_act"], 2 * n)], "qT3": [(s["qT_dve"], 2 * n)],
                        "kT": [(s["kT_read"], n)],
                        "oT": None, "outp": [(s["hn_ready"], n)], "hT": [(s["hT_ready"], n)]}[name]

            filling, before, held = {}, {}, [[], []]
            for name, t in steps:
                for n in ([0, 1] if name == "oT" else [FILLS[name]] if name in FILLS else []):
                    filling[name, t, n] = len(held[n]) + 1
                    before[name, t, n] = held[n][-1] if held[n] else None
                    held[n].append((name, t))

            heads = [t for name, t in steps if name == "head"]
            with nc.Block() as block:
                @block.sync
                def _(sp):
                    if heads:
                        sp.dma_start(x[:, 0], a["x_next"][bass.ds(b, 1), 0:P, :].rearrange("o p d -> (o p) d"))\
                          .then_inc(s["x_first"], 16)
                        sp.wait_ge(s["mask_read"], 1)
                        sp.dma_start(mask_in[:], a["mask_next"][bass.ds(b, 1), :]).then_inc(s["x_rest"], 16)
                        for t in range(1, TT):
                            sp.wait_ge(s["xn_ready"], t)
                            sp.dma_start(x[:, t], a["x_next"][bass.ds(b, 1), t * P:(t + 1) * P, :].rearrange(
                                "o p d -> (o p) d")).then_inc(s["x_rest"], 16)
                    stores = 0
                    for name, t in steps:
                        if name == "hT":
                            sp.wait_ge(s["hT_ready"], done("hT", t))
                            slot = bass.ds(b if t < 0 else b + 1, 1)
                            at = t % TT
                            sp.dma_start(hT_dram[slot, :, :, at * P:(at + 1) * P].rearrange("o p k n -> (o p) k n"),
                                         hT[:, at]).then_inc(s["hT_out"], 16)
                            stores += 1
                    if stores:
                        sp.wait_ge(s["hT_out"], 16 * stores)
                    if heads:
                        sp.wait_ge(s["x_rest"], 16 * TT)

                def wait_evac(eng, n):
                    if evac_by_dve(n):
                        eng.wait_ge(s["probsT_dve"], count_dve(n))
                    else:
                        eng.wait_ge(s["probsT_act"], n + 1 - count_dve(n))

                @block.tensor
                def _(pe):
                    def fill(name, t, n=None):
                        n = FILLS[name] if n is None else n
                        if before[name, t, n]:
                            step, tile = before[name, t, n]
                            if step == "oT":
                                pe.wait_ge((s["oT_act"], s["oT_dve"])[n], done("oT", tile))
                            else:
                                for sm, value in drained(step, tile):
                                    pe.wait_ge(sm, value)
                        return FB[n]

                    for name, t in steps:
                        if name == "head":
                            n = t
                            if n < NH * TT:
                                tile, h = divmod(n, NH)
                                w = P * (tile + 1)
                                if n == 0:
                                    pe.wait_ge(s["mask_read"], 1)
                                    pe.wait_ge(s["next_taken"], 3)
                                if h == 0 and tile > 0:
                                    pe.wait_ge(s["qT_act"], 2 * done("qT0", tile))
                                    pe.wait_ge(s["qT_dve"], 2 * done("qT1", tile))
                                    pe.wait_ge(s["kT_ready"], done("kT", tile))
                                if n >= 2:
                                    pe.wait_ge(s["scores_ready"], n - 1)
                                o_s = SB[n % 2]
                                pe.matmul(o_s[:, 0:w], ones[:], mask_row[:, 0:w], start=True, stop=False)
                                for i in range(2):
                                    last = pe.matmul(o_s[:, 0:w], qT[:, tile % 2, h], kT[i][:, 0:w],
                                                     start=False, stop=i == 1)
                                last.then_inc(s["scores_psum"], 1)
                            n = t - QK_LAG
                            if 0 <= n < NH * TT:
                                tile = n // NH
                                pe.wait_ge(s["probs_ready"], n + 1)
                                if n >= 2:
                                    wait_evac(pe, n - 2)
                                for j in range(tile + 1):
                                    last = pe.transpose(TB[n % 2][:, j * P:(j + 1) * P],
                                                        S[:, n % S_SLOTS, j * P:(j + 1) * P], ident[:])
                                last.then_inc(s["probsT_psum"], 1)
                            n = t - PV_LAG
                            if 0 <= n < NH * TT:
                                tile, h = divmod(n, NH)
                                wait_evac(pe, n)
                                if h == 0 and tile > 0:
                                    pe.wait_ge(s["o_scaled"], done("weigh0", tile - 1) + done("weigh1", tile - 2))
                                if h == 8:
                                    pe.wait_ge(s["o_scaled"], done("weigh1", tile - 1) + tile)
                                for j in range(tile + 1):
                                    last = pe.matmul(OB[h // 8][:, (h % 8) * DH:(h % 8 + 1) * DH],
                                                     PT[:, n % PT_SLOTS, j * P:(j + 1) * P], v[:, j],
                                                     start=j == 0, stop=j == tile)
                                last.then_inc(s["pv_done"], 1)
                        elif name == "xT":
                            pe.wait_ge(s["xn_ready"], done("xn", t))
                            f = fill(name, t)
                            for k in range(KD):
                                last = pe.transpose(f[:, k * P:(k + 1) * P], xn[:, k * P:(k + 1) * P], ident[:])
                            last.then_inc(full[0], 1)
                        elif name in ("q0", "q1", "kv"):
                            if name == "q0":
                                pe.wait_ge(s["xnT_high"], done("xT", t))
                                pe.wait_ge(s["xnT_low"], done("xT", t))
                            f = fill(name, t)
                            cols = {"q0": slice(0, 512), "q1": slice(512, QW), "kv": slice(QW, QKVN)}[name]
                            terms = [(i, j, k) for k in range(KD) for i, j in ((0, 0), (0, 1), (1, 0))]
                            for n, (i, j, k) in enumerate(terms):
                                last = pe.matmul(f[:, 0:cols.stop - cols.start], xnT[i][:, k], wqkv[j][:, k, cols],
                                                 start=n == 0, stop=n == len(terms) - 1)
                            last.then_inc(full[FILLS[name]], 1)
                        elif name in ("qT0", "qT1", "qT2", "qT3"):
                            i = int(name[2])
                            if i % 2 == 0:
                                pe.wait_ge(s["q_high"], 2 * done("qn", t) - 1 + i // 2)
                                pe.wait_ge(s["q_low"], 2 * done("qn", t) - 1 + i // 2)
                            f = fill(name, t)
                            for j in range(4):
                                last = pe.transpose(f[:, j * P:(j + 1) * P],
                                                    qs[:, 4 * i + j].rearrange("p a d -> p (a d)").bitcast(F32), ident[:])
                            last.then_inc(full[FILLS[name]], 1)
                        elif name == "kT":
                            pe.wait_ge(s["kn_ready"], done("qn", t))
                            f = fill(name, t)
                            pe.transpose(f[:, 0:P], kn[:].rearrange("p a d -> p (a d)"), ident[:]).then_inc(full[0], 1)
                        elif name == "oT":
                            pe.wait_ge(s["o_ready"], done("weigh1", t))
                            for n in range(2):
                                f = fill("oT", t, n)
                                for j in range(4):
                                    i = 4 * n + j
                                    last = pe.transpose(f[:, j * P:(j + 1) * P],
                                                        o[:, 2 * i:2 * i + 2].rearrange("p a d -> p (a d)"), ident[:])
                                last.then_inc(full[n], 1)
                        elif name == "outp":
                            pe.wait_ge(s["oT_act"], done("oT", t))
                            pe.wait_ge(s["oT_dve"], done("oT", t))
                            f = fill(name, t)
                            for i in range(QT):
                                last = pe.matmul(f[:, 0:D], oT[:, i], wout[:, i], start=i == 0, stop=i == QT - 1)
                            last.then_inc(full[0], 1)
                        elif name == "hT":
                            pe.wait_ge(s["hn_ready"], done("hn", t))
                            f = fill(name, t)
                            for k in range(KD):
                                last = pe.transpose(f[:, k * P:(k + 1) * P], hn[:, k * P:(k + 1) * P], ident[:])
                            last.then_inc(full[1], 1)

                @block.vector
                def _(dve):
                    link = Chain(dve, dve_chain)

                    def filled(name, t, n=None):
                        n = FILLS[name] if n is None else n
                        dve.wait_ge(full[n], filling[name, t, n])
                        return FB[n]

                    def weigh(t, i):
                        n = done("weigh0", t) + done("weigh1", t - 1) if i == 0 else done("weigh1", t) + done("weigh0", t)
                        hs = slice(8 * i, 8 * i + 8)
                        c = t % 2
                        dve.wait_ge(s["null_probs"], n)
                        link(dve.tensor_tensor(dent[:, i], den[:, c, hs], pn[:, i], ALU.add))
                        link(dve.reciprocal(rden[:, i], dent[:, i]))
                        dve.tensor_tensor(pnr[:, i], pn[:, i], rden[:, i], ALU.mult).then_inc(s["weights_ready"], 1)
                        if t >= 0:
                            dve.wait_ge(s["pv_done"], NH * t + 8 * (i + 1))
                        prev = done("oT", t - 1)
                        if prev:
                            dve.wait_ge(full[i], filling["oT", t - 1, i])
                        dve.tensor_tensor(o[:, hs], OB[i][:, :].rearrange("p (h d) -> p h d", d=DH),
                                          rden[:, i].unsqueeze(2).broadcast_to([P, 8, DH]),
                                          ALU.mult).then_inc(s["o_scaled"], 1)
                        dve.wait_ge(s["weights_ready"], n)
                        dve.tensor_tensor(onull[:], nullv[:].unsqueeze(1).broadcast_to([P, 8, DH]),
                                          pnr[:, i].unsqueeze(2).broadcast_to([P, 8, DH]),
                                          ALU.mult).then_inc(s["onull_ready"], 1)
                        dve.wait_ge(s["onull_ready"], n)
                        dve.wait_ge(s["o_scaled"], n)
                        ins = dve.tensor_tensor(o[:, hs], o[:, hs], onull[:], ALU.add)
                        if i == 1:
                            ins.then_inc(s["o_ready"], 1)
                        else:
                            link(ins)

                    if heads:
                        dve.tensor_scalar(mask_row[:], mask_in[:], -MASKED, MASKED, ALU.mult,
                                          ALU.add).then_inc(s["mask_read"], 1)
                        for i in range(2):
                            dve.tensor_copy(kT[i][:, 0:P], k_next[i][:]).then_inc(s["next_taken"], 1)
                        dve.tensor_copy(v[:, 0], v_next[:]).then_inc(s["next_taken"], 1)
                    for name, t in steps:
                        if name == "head":
                            n = t
                            if n < NH * TT:
                                tile, h = divmod(n, NH)
                                w = P * (tile + 1)
                                if h == 0 and tile > 0:
                                    dve.wait_ge(s["null_ready"], done("null", tile))
                                dve.wait_ge(s["scores_psum"], n + 1)
                                if n >= S_SLOTS:
                                    dve.wait_ge(s["probsT_psum"], n - S_SLOTS + 1)
                                dve.tensor_tensor_reduce(S[:, n % S_SLOTS, 0:w], SB[n % 2][:, 0:w],
                                                         bias[:, h, L - w:L], -1.0, nsn[:, tile % 2, h:h + 1],
                                                         ALU.add, ALU.min, nm[:, tile % 2, h:h + 1])\
                                   .then_inc(s["scores_ready"], 1)
                            n = t - QK_LAG
                            if 0 <= n < NH * TT and evac_by_dve(n):
                                dve.wait_ge(s["probsT_psum"], n + 1)
                                if n >= PT_SLOTS:
                                    dve.wait_ge(s["pv_done"], n - PT_SLOTS + 1)
                                w = P * (n // NH + 1)
                                dve.tensor_copy(PT[:, n % PT_SLOTS, 0:w], TB[n % 2][:, 0:w]).then_inc(s["probsT_dve"], 1)
                        elif name == "stat":
                            if t == TT and heads:
                                dve.wait_ge(s["x_first"], 16)
                            if done("stat", t) > 1:
                                dve.wait_ge(s["xn_ready"], done("xn", t - 1))
                            link(dve.bn_stats(stats[:], x[:, t % TT]))
                            link(dve.bn_aggr(mv[:], stats[:]))
                            dve.tensor_scalar(ve[:], mv[:, 1:2], 1e-5, None, ALU.add).then_inc(s["x_var"], 1)
                        elif name == "xn":
                            dve.wait_ge(s["x_rstd"], done("xn", t))
                            if done("xT", t - 1):
                                dve.wait_ge(full[0], filling["xT", t - 1, 0])
                            dve.tensor_scalar(xn[:], x[:, t % TT], mv[:, 0:1], rstd[:], ALU.subtract,
                                              ALU.mult).then_inc(s["xn_ready"], 1)
                        elif name == "xT":
                            dve.wait_ge(s["xnT_high"], done("xT", t))
                            if done("kv", t - 1):
                                dve.wait_ge(full[1], filling["kv", t - 1, 1])
                            dve.tensor_tensor(xnT[1][:].rearrange("p k n -> p (k n)"), FB[0][:, 0:D],
                                              xnT[0][:].rearrange("p k n -> p (k n)").bitcast(F32),
                                              ALU.subtract).then_inc(s["xnT_low"], 1)
                        elif name == "ss":
                            dve.wait_ge(s["sq_ready"], 3 * done("ss", t))
                            if done("rr", t - 1) or done("qn", t - 1):
                                dve.wait_ge(s["rr_ready"], done("qn", t - 1))
                            link(dve.tensor_reduce(ss[:], sq[:], AX.X, ALU.add))
                            dve.tensor_scalar(ss[:], ss[:], 1e-24, None, ALU.max).then_inc(s["ss_ready"], 1)
                        elif name in ("qT1", "qT3"):
                            f = filled(name, t)
                            i = int(name[2])
                            dve.tensor_copy(qT[:, t % 2, 4 * i:4 * i + 4].rearrange("p a n -> p (a n)"), f[:, :])\
                               .then_inc(s["qT_dve"], 1)
                        elif name == "kT":
                            f = filled(name, t)
                            high, low = (k_next[0][:], k_next[1][:]) if t == TT else \
                                (kT[0][:, t * P:(t + 1) * P], kT[1][:, t * P:(t + 1) * P])
                            if done("kT", t - 1):
                                dve.wait_ge(s["kT_ready"], done("kT", t - 1))
                            dve.tensor_scalar(kf[:], f[:, 0:P], kscale[:, 2:3], None, ALU.mult).then_inc(s["kT_read"], 1)
                            dve.wait_ge(s["kT_read"], done("kT", t))
                            link(dve.tensor_copy(high, kf[:]))
                            dve.tensor_tensor(low, kf[:], high.bitcast(F32), ALU.subtract).then_inc(s["kT_ready"], 1)
                        elif name == "null":
                            dve.wait_ge(s["rr_ready"], done("ss", t))
                            link(dve.tensor_tensor(nsn[:, t % 2], nraw[:], rr[:, 0:NH], ALU.mult))
                            dve.scalar_tensor_tensor(out=nsn[:, t % 2], in0=nsn[:, t % 2], scalar=-1.0, in1=nullb[:],
                                                     op0=ALU.mult, op1=ALU.subtract).then_inc(s["null_ready"], 1)
                        elif name in ("diff0", "diff1"):
                            i, c = int(name[4]), t % 2
                            hs = slice(8 * i, 8 * i + 8)
                            if t >= 0:
                                dve.wait_ge(s["scores_ready"], NH * t + 8 * (i + 1))
                            dve.tensor_tensor(dn[:, i], nm[:, c, hs], nsn[:, c, hs],
                                              ALU.subtract).then_inc(s["null_diff"], 1)
                        elif name in ("weigh0", "weigh1"):
                            weigh(t, int(name[5]))
                        elif name == "oT":
                            f = filled("oT", t, 1)
                            if done("outp", t - 1):
                                dve.wait_ge(full[0], filling["outp", t - 1, 0])
                            dve.tensor_copy(oT[:, 4:8].rearrange("p a n -> p (a n)"), f[:, :]).then_inc(s["oT_dve"], 1)
                        elif name == "outp":
                            f = filled("outp", t)
                            if done("hn", t - 1):
                                dve.wait_ge(s["hn_ready"], done("hn", t - 1))
                            link(dve.bn_stats(stats2[:], f[:, 0:D]))
                            link(dve.bn_aggr(mv2[:], stats2[:]))
                            dve.tensor_scalar(ve2[:], mv2[:, 1:2], 1e-5, None, ALU.add).then_inc(s["out_var"], 1)
                        elif name == "hn":
                            dve.wait_ge(s["out_rstd"], done("hn", t))
                            if done("hT", t - 1):
                                dve.wait_ge(full[1], filling["hT", t - 1, 1])
                            dve.tensor_scalar(hn[:], FB[0][:, 0:D], mv2[:, 0:1], rstd2[:], ALU.subtract,
                                              ALU.mult).then_inc(s["hn_ready"], 1)

                @block.scalar
                def _(act):
                    def filled(name, t, n=None):
                        n = FILLS[name] if n is None else n
                        act.wait_ge(full[n], filling[name, t, n])
                        return FB[n]

                    for name, t in steps:
                        if name == "head":
                            n = t
                            if 0 <= n < NH * TT:
                                tile, h = divmod(n, NH)
                                w = P * (tile + 1)
                                act.wait_ge(s["scores_ready"], n + 1)
                                act.activation(S[:, n % S_SLOTS, 0:w], S[:, n % S_SLOTS, 0:w], ACT.Exp, scale=-1.0,
                                               bias=nm[:, tile % 2, h:h + 1],
                                               accum_out=den[:, tile % 2, h:h + 1]).then_inc(s["probs_ready"], 1)
                            n = t - QK_LAG
                            if 0 <= n < NH * TT and not evac_by_dve(n):
                                act.wait_ge(s["probsT_psum"], n + 1)
                                if n >= PT_SLOTS:
                                    act.wait_ge(s["pv_done"], n - PT_SLOTS + 1)
                                w = P * (n // NH + 1)
                                act.copy(PT[:, n % PT_SLOTS, 0:w], TB[n % 2][:, 0:w]).then_inc(s["probsT_act"], 1)
                        elif name == "xT":
                            f = filled(name, t)
                            if done("kv", t - 1):
                                act.wait_ge(full[1], filling["kv", t - 1, 1])
                            act.copy(xnT[0][:].rearrange("p k n -> p (k n)"), f[:, 0:D]).then_inc(s["xnT_high"], 1)
                        elif name in ("q0", "q1"):
                            i = int(name[1])
                            f = filled(name, t)
                            if i == 0 and done("qn", t - 1):
                                act.wait_ge(s["kn_ready"], done("qn", t - 1))
                                act.wait_ge(s["qn_ready"], 2 * done("qn", t - 1))
                                act.wait_ge(s["ss_ready"], done("ss", t - 1))
                                act.wait_ge(s["null_ready"], done("null", t - 1))
                            hs = slice(8 * i, 8 * i + 8)
                            act.activation(sq[:, hs].rearrange("p a d -> p (a d)"), f[:, :], ACT.Square)\
                               .then_inc(s["sq_ready"], 1)
                            act.copy(qraw[:, hs].rearrange("p a d -> p (a d)"), f[:, :]).then_inc(s["q_ready"], 1)
                        elif name == "kv":
                            f = filled(name, t)
                            act.activation(sq[:, NH], f[:, 0:DH], ACT.Square).then_inc(s["sq_ready"], 1)
                            act.copy(v_next[:] if t == TT else v[:, t], f[:, DH:2 * DH]).then_inc(s["kv_ready"], 1)
                            act.copy(nraw[:], f[:, 2 * DH:2 * DH + NH]).then_inc(s["kv_ready"], 1)
                            act.copy(qraw[:, NH], f[:, 0:DH]).then_inc(s["kv_ready"], 1)
                        elif name in ("qs0", "qs1"):
                            i = int(name[2])
                            hs = slice(8 * i, 8 * i + 8)
                            act.wait_ge(s["qn_ready"], 2 * done("qn", t) - 1 + i)
                            if done("qT3", t - 1):
                                act.wait_ge(full[1], filling["qT3", t - 1, 1])
                            act.copy(qs[:, hs, 0], qn[:, hs]).then_inc(s["q_high"], 1)
                        elif name in ("qT0", "qT2"):
                            f = filled(name, t)
                            i = int(name[2])
                            act.copy(qT[:, t % 2, 4 * i:4 * i + 4].rearrange("p a n -> p (a n)"), f[:, :])\
                               .then_inc(s["qT_act"], 1)
                        elif name in ("diff0", "diff1"):
                            i = int(name[4])
                            n = done("diff0", t) + (done("diff1", t - 1) if i == 0 else done("diff1", t))
                            act.wait_ge(s["null_diff"], n)
                            if n > 2:
                                act.wait_ge(s["weights_ready"], n - 2)
                            act.activation(pn[:, i], dn[:, i], ACT.Exp).then_inc(s["null_probs"], 1)
                        elif name == "oT":
                            f = filled("oT", t, 0)
                            if done("outp", t - 1):
                                act.wait_ge(full[0], filling["outp", t - 1, 0])
                            act.copy(oT[:, 0:4].rearrange("p a n -> p (a n)"), f[:, :]).then_inc(s["oT_act"], 1)
                        elif name == "hT":
                            f = filled(name, t)
                            for k in range(KD):
                                last = act.activation(hT[:, t % TT, k], f[:, k * P:(k + 1) * P], ACT.Copy,
                                                      scale=go[:, k:k + 1])
                            last.then_inc(s["hT_ready"], 1)

                @block.gpsimd
                def _(pool):
                    link = Chain(pool, pool_chain)
                    for name, t in steps:
                        if name == "stat":
                            pool.wait_ge(s["x_var"], done("stat", t))
                            pool.tensor_tensor(rstd[:], ve[:], half[:, 0:1], ALU.pow).then_inc(s["x_rstd"], 1)
                        elif name == "ss":
                            pool.wait_ge(s["ss_ready"], done("ss", t))
                            if done("qn", t - 1):
                                pool.wait_ge(s["qn_ready"], 2 * done("qn", t - 1))
                                pool.wait_ge(s["null_ready"], done("null", t - 1))
                            pool.tensor_tensor(rr[:], ss[:], half[:, 0:NH + 1], ALU.pow).then_inc(s["rr_ready"], 1)
                        elif name == "qn":
                            n = done("qn", t)
                            pool.wait_ge(s["rr_ready"], n)
                            pool.wait_ge(s["q_ready"], 2 * n)
                            pool.wait_ge(s["kv_ready"], 3 * n)

                            def scaled(i):
                                hs = slice(8 * i, 8 * i + 8)
                                pool.tensor_tensor(qn[:, hs], qraw[:, hs], rr[:, hs].unsqueeze(2).broadcast_to([P, 8, DH]),
                                                   ALU.mult).then_inc(s["qn_ready"], 1)

                            if done("kT", t - 1):
                                pool.wait_ge(full[0], filling["kT", t - 1, 0])
                            pool.tensor_tensor(kn[:], qraw[:, NH].unsqueeze(1).broadcast_to([P, 2, DH]),
                                               rr[:, NH:NH + 1].unsqueeze(2).broadcast_to([P, 2, DH]),
                                               ALU.mult).then_inc(s["kn_ready"], 1)
                            scaled(0)
                            scaled(1)
                        elif name in ("qs0", "qs1"):
                            i = int(name[2])
                            hs = slice(8 * i, 8 * i + 8)
                            pool.wait_ge(s["q_high"], 2 * done("qn", t) - 1 + i)
                            if done("qT3", t - 1):
                                pool.wait_ge(full[1], filling["qT3", t - 1, 1])
                            pool.tensor_tensor(qs[:, hs, 1], qn[:, hs], qs[:, hs, 0].bitcast(F32),
                                               ALU.subtract).then_inc(s["q_low"], 1)
                        elif name == "outp":
                            pool.wait_ge(s["out_var"], done("outp", t))
                            if done("hn", t - 1):
                                pool.wait_ge(s["hn_ready"], done("hn", t - 1))
                            pool.tensor_tensor(rstd2[:], ve2[:], half[:, 0:1], ALU.pow).then_inc(s["out_rstd"], 1)
            clear(nc, sems)

        run([(n, TT) for n in FRONT], 0)
        with nc.Fori(0, B) as b:
            run(iteration(), b)
        run([(n, -1) for n in BACK], B)




def drained_before(order, drained):
    held, out = {}, {}
    for bank, step, n in order:
        out[bank, step, n] = drained(*held[bank]) if bank in held else []
        held[bank] = (step, n)
    return out


def delta_inputs_phase(nc, a, hT_dram, xg_dram, qk_dram, vb_dram, bg_dram, low_dram):
    PAD = 8
    with ExitStack() as ctx:
        sb, bank, sem, sems = space(nc, ctx, "b")
        ident = sb("ident", [P, P])
        wqkv = sb("wqkv", [P, KD, 3 * D])
        wsm = sb("wsm", [P, KD, 2 * H2 + 1])
        smb = sb("smb", [P, 2 * H2 + 1])
        conv = sb("conv", [P, 3, KD, 4])
        frac = sb("frac", [P, KD, 4, 2])
        own = sb("own", [P, KD])
        diag = sb("diag", [P, KD, 5, P])
        cos = sb("cos", [P, TT, DH // 2])
        sin = sb("sin", [P, TT, DH // 2])
        rot = sb("rot", [P, H2])
        cm = sb("cm", [P, TT, H2, DH // 2])
        sm = sb("sm", [P, TT, H2, DH // 2])
        omx = sb("omx", [P, H2])
        mixw = sb("mixw", [P, D])
        strict = sb("strict", [P, CH])
        half = sb("half", [P, 8])

        h = sb("h", [P, KD, PAD + L])
        x = sb("x", [P, TT, D])
        proj = sb("proj", [P, 6, 3 + L])
        y = sb("y", [P, 6, L])
        gates_in = sb("gates_in", [P, TT, 2 * H2 + 1])
        gates = sb("gates", [P, TT, 2 * H2 + 1])
        nb = sb("nb", [P, TT, H2, CH])
        fsq = sb("fsq", [P, TT, D])
        fss = sb("fss", [P, TT])
        fve = sb("fve", [P, TT])
        frs = sb("frs", [P, TT])
        fsc = sb("fsc", [P, TT])
        z = sb("z", [P, 2, 8, DH])
        zm = sb("zm", [P, 2, 8, DH])
        rb1 = sb("rb1", [P, 2, P])
        rb2 = sb("rb2", [P, 2, P])
        ra1 = sb("ra1", [P, 2, P])
        ra2 = sb("ra2", [P, 2, P])
        r = sb("r", [P, 2, 8, DH])
        rsq = sb("rsq", [P, 8, DH])
        rss = sb("rss", [P, 2, 8])
        rrn = sb("rrn", [P, 2, 8])
        qk = sb("qk", [P, TT, 8, DH])
        vb = sb("vb", [P, TT, H2, DH])
        kT = sb("kT", [P, TT, 2, P])
        low = sb("low", [P, TT, H2, CH])
        xg = sb("xg", [P, TT, D])

        J = [bank(f"J{i}") for i in range(2)]
        X = [bank(f"X{i}") for i in range(2)]
        V = bank("V")
        K = bank("K")
        G = [bank(f"G{i}") for i in range(2)]

        loaded = sem("loaded")
        dve_chain = sem("dve_chain")
        pool_chain = sem("pool_chain")
        rot_ready = sem("rot_ready")

        with nc.Block() as block:
            N_LOADS = 14

            @block.sync
            def _(sp):
                loads = [(ident[:], a["c_ident"]), (conv[:], a["conv"]), (frac[:], a["L0_attn_frac_conv_w"]),
                         (cos[:], a["c_cos"]), (sin[:], a["c_sin"]), (rot[:], row(a["L0_attn_rot_logit"], H2)),
                         (mixw[:], row(a["L0_attn_mixer_norm_w"], D)), (strict[:], a["c_strict"]),
                         (smb[:, 2 * H2:], row(a["L0_attn_frac_gate_b"], 1))]
                for i, n in enumerate(("Wq", "Wk", "Wv")):
                    loads.append((wqkv[:, :, i * D:(i + 1) * D], a[f"L0_attn_{n}"].rearrange("(k p) n -> p k n", p=P)))
                loads.append((wsm[:], a["gates"]))
                loads.append((h[:, :, PAD:], hT_dram[1, :, :, :]))
                assert len(loads) == N_LOADS
                for dst, src in loads:
                    sp.dma_start(dst, src).then_inc(loaded, 16)

            @block.scalar
            def _(act):
                act.wait_ge(loaded, 16 * N_LOADS)
                act.activation(rot[:], rot[:], ACT.Sigmoid).then_inc(rot_ready, 1)

            @block.gpsimd
            def _(pool):
                pool.memset(half[:], -0.5)
                pool.memset(h[:, :, 0:PAD], 0.0)
                pool.memset(proj[:, :, 0:3], 0.0)

            @block.vector
            def _(dve):
                link = Chain(dve, dve_chain)
                dve.memset(smb[:, 0:2 * H2], 0.0)
                dve.wait_ge(loaded, 16 * N_LOADS)
                link(dve.tensor_reduce(own[:], frac[:, :, :, 1], AX.X, ALU.add))
                link(dve.tensor_scalar(own[:], own[:], 2.0, None, ALU.add))
                for k in range(KD):
                    for i in range(5):
                        w = own[:, k:k + 1] if i == 4 else frac[:, k, i, 0:1]
                        dve.tensor_scalar(diag[:, k, i], ident[:], w, None, ALU.mult)
                dve.wait_ge(rot_ready, 1)
                for t in range(TT):
                    for table, mixed in ((cos, cm), (sin, sm)):
                        dve.tensor_tensor(mixed[:, t], table[:, t].unsqueeze(1).broadcast_to([P, H2, DH // 2]),
                                          rot[:].unsqueeze(2).broadcast_to([P, H2, DH // 2]), ALU.mult)
                dve.tensor_scalar(omx[:], rot[:], -1.0, 1.0, ALU.mult, ALU.add)
        clear(nc, sems)

        h_in = sem("h_in")
        x_in = sem("x_in")
        proj_psum = sem("proj_psum")
        proj_ready = sem("proj_ready")
        conv_ready = sem("conv_ready")
        y_ready = sem("y_ready")
        gates_psum = sem("gates_psum")
        gates_read = sem("gates_read")
        gates_ready = sem("gates_ready")
        nb_ready = sem("nb_ready")
        mixer_psum = sem("mixer_psum")
        frac_sums = sem("frac_sums")
        frac_var = sem("frac_var")
        frac_scale = sem("frac_scale")
        xg_ready = sem("xg_ready")
        z_psum = sem("z_psum")
        z_ready = sem("z_ready")
        zm_ready = sem("zm_ready")
        pool_rot = sem("pool_rot")
        r_ready = sem("r_ready")
        rsq_ready = sem("rsq_ready")
        rss_ready = sem("rss_ready")
        rrn_ready = sem("rrn_ready")
        qk_ready = sem("qk_ready")
        v_psum = sem("v_psum")
        vb_ready = sem("vb_ready")
        kT_psum = sem("kT_psum")
        kT_ready = sem("kT_ready")
        gram_psum = sem("gram_psum")
        low_ready = sem("low_ready")
        stored = sem("stored")

        ORDER = ([("J", i % 2, "proj", i) for i in range(6)] + [("K", 0, "gates", 0)]
                 + [("X", t % 2, "z", t) for t in range(TT)] + [("V", 0, "v", 0), ("V", 0, "v", 1)]
                 + [("J", 0, "frac", 0), ("J", 1, "frac", 1)])
        for t in range(TT):
            ORDER.append(("K", 0, "kT", t))
            if t % 2:
                ORDER += [("G", e, "gram", 2 * (t // 2) + e) for e in range(2)]

        def drained(step, n):
            return {"proj": [(proj_ready, n + 1)], "gates": [(gates_read, 1)], "z": [(zm_ready, n + 1)],
                    "v": [(vb_ready, n + 1)], "frac": [(xg_ready, 2 * n + 2)], "kT": [(kT_ready, n + 1)],
                    "gram": [(low_ready, 4 * (n + 1))]}[step]

        before = drained_before([((name, i), step, n) for name, i, step, n in ORDER], drained)
        BANKS = {"J": J, "X": X, "V": [V], "K": [K], "G": G}

        def batch(b, ahead):
            with nc.Block() as block:
                @block.sync
                def _(sp):
                    sp.dma_start(x[:], a["x"][bass.ds(b, 1), :, :].rearrange("o (t p) d -> p (o t) d", p=P)).then_inc(x_in, 16)
                    sp.wait_ge(gates_ready, 1)
                    sp.dma_start(bg_dram[bass.ds(b, 1), :, :].rearrange("o p n -> (o p) n"),
                                 gates[:].rearrange("p t n -> p (t n)")).then_inc(stored, 16)
                    if ahead:
                        sp.wait_ge(mixer_psum, 2)
                        sp.dma_start(h[:, :, PAD:], hT_dram[bass.ds(b + 2, 1), :, :, :].rearrange(
                            "o p k n -> (o p) k n")).then_inc(h_in, 16)
                    sp.wait_ge(vb_ready, 2)
                    sp.dma_start(vb_dram[bass.ds(b, 1), :, :].rearrange("o p n -> (o p) n"),
                                 vb[:].rearrange("p t h d -> p (t h d)")).then_inc(stored, 16)
                    sp.wait_ge(qk_ready, TT)
                    sp.dma_start(qk_dram[bass.ds(b, 1), :, :].rearrange("o p n -> (o p) n"),
                                 qk[:].rearrange("p t h d -> p (t h d)")).then_inc(stored, 16)
                    sp.wait_ge(low_ready, 16)
                    for c in range(NC4):
                        sp.dma_start(low_dram[bass.ds(b, 1), :, :, c].rearrange("o t h i j -> i (o t h) j"),
                                     low[c * CH:(c + 1) * CH].rearrange("p t h j -> p (t h) j")).then_inc(stored, 16)
                    sp.wait_ge(xg_ready, TT)
                    sp.dma_start(xg_dram[bass.ds(b, 1), :, :].rearrange("o p n -> (o p) n"),
                                 xg[:].rearrange("p t d -> p (t d)")).then_inc(stored, 16)
                    sp.wait_ge(stored, 16 * (4 + NC4))
                    if ahead:
                        sp.wait_ge(h_in, 16)

                @block.tensor
                def _(pe):
                    def fill(name, i, step, n):
                        for s, value in before[(name, i), step, n]:
                            pe.wait_ge(s, value)
                        return BANKS[name][i]

                    for i in range(6):
                        o = fill("J", i % 2, "proj", i)
                        for k in range(KD):
                            last = pe.matmul(o[:, :], wqkv[:, k, i * P:(i + 1) * P], h[:, k, PAD:],
                                             start=k == 0, stop=k == KD - 1)
                        last.then_inc(proj_psum, 1)
                    o = fill("K", 0, "gates", 0)
                    n = 2 * H2 + 1
                    for t in range(TT):
                        for k in range(KD):
                            last = pe.matmul(o[:, t * n:(t + 1) * n], h[:, k, PAD + t * P:PAD + (t + 1) * P],
                                             wsm[:, k], start=k == 0, stop=k == KD - 1)
                    last.then_inc(gates_psum, 1)

                    def mixer(g):
                        o = fill("J", g, "frac", g)
                        for tt in range(2):
                            for k in range(KD):
                                at = PAD + (2 * g + tt) * P
                                for i in range(5):
                                    back = 0 if i == 4 else 2 ** i
                                    last = pe.matmul(o[:, tt * D + k * P:tt * D + (k + 1) * P],
                                                     h[:, k, at - back:at - back + P], diag[:, k, i],
                                                     start=i == 0, stop=i == 4)
                        last.then_inc(mixer_psum, 1)

                    mixer(0)
                    for t in range(TT):
                        if t == 0:
                            pe.wait_ge(y_ready, 4)
                        o = fill("X", t % 2, "z", t)
                        for i in range(4):
                            last = pe.transpose(o[:, i * P:(i + 1) * P], y[:, i, t * P:(t + 1) * P], ident[:])
                        last.then_inc(z_psum, 1)
                    pe.wait_ge(y_ready, 6)
                    for g in range(2):
                        o = fill("V", 0, "v", g)
                        for tt in range(2):
                            for i in range(2):
                                t = 2 * g + tt
                                last = pe.transpose(o[:, tt * D + i * P:tt * D + (i + 1) * P],
                                                    y[:, 4 + i, t * P:(t + 1) * P], ident[:])
                        last.then_inc(v_psum, 1)
                    mixer(1)
                    for t in range(TT):
                        pe.wait_ge(qk_ready, t + 1)
                        o = fill("K", 0, "kT", t)
                        for i in range(2):
                            last = pe.transpose(o[:, i * P:(i + 1) * P],
                                                qk[:, t, H2 + 2 * i:H2 + 2 * i + 2].rearrange("p a d -> p (a d)"), ident[:])
                        last.then_inc(kT_psum, 1)
                        if t % 2:
                            pe.wait_ge(kT_ready, t + 1)
                            for e in range(2):
                                o = fill("G", e, "gram", 2 * (t // 2) + e)
                                part = slice(e * DH, (e + 1) * DH)
                                for tt in range(2):
                                    for i in range(2):
                                        keys = kT[part, t - 1 + tt, i]
                                        j = 2 * tt + i
                                        last = pe.matmul(o[:, j * P:(j + 1) * P], keys, keys, start=True, stop=True)
                                last.then_inc(gram_psum, 1)

                @block.scalar
                def _(act):
                    for i in range(6):
                        act.wait_ge(proj_psum, i + 1)
                        act.copy(proj[:, i, 3:], J[i % 2][:, :]).then_inc(proj_ready, 1)
                    act.wait_ge(gates_read, 1)
                    act.activation(gates[:], gates_in[:], ACT.Sigmoid).then_inc(gates_ready, 1)
                    for i in range(6):
                        act.wait_ge(conv_ready, i + 1)
                        act.activation(y[:, i], y[:, i], ACT.Silu).then_inc(y_ready, 1)
                    for t in range(TT + 1):
                        if t < TT:
                            act.wait_ge(z_psum, t + 1)
                            if t >= 2:
                                act.wait_ge(r_ready, t - 1)
                                act.wait_ge(pool_rot, t - 1)
                            act.copy(z[:, t % 2].rearrange("p a d -> p (a d)"), X[t % 2][:, :]).then_inc(z_ready, 1)
                            for i in range(H2):
                                last = act.activation(zm[:, t % 2].rearrange("p (q h) d -> p q h d", q=2)[:, :, i],
                                                      X[t % 2][:, :].rearrange("p (q h d) -> p q h d", q=2, d=DH)[:, :, i],
                                                      ACT.Copy, scale=omx[:, i:i + 1])
                            last.then_inc(zm_ready, 1)
                        if t > 0:
                            act.wait_ge(r_ready, t)
                            if t > 1:
                                act.wait_ge(rss_ready, t - 1)
                            act.activation(rsq[:], r[:, (t - 1) % 2], ACT.Square).then_inc(rsq_ready, 1)
                    for t in range(TT):
                        act.wait_ge(mixer_psum, t // 2 + 1)
                        act.activation(fsq[:, t], J[t // 2][:, (t % 2) * D:(t % 2 + 1) * D], ACT.Square,
                                       accum_out=fss[:, t:t + 1]).then_inc(frac_sums, 1)
                    for t in range(TT):
                        act.wait_ge(kT_psum, t + 1)
                        act.copy(kT[:, t].rearrange("p a n -> p (a n)"), K[:, 0:2 * P]).then_inc(kT_ready, 1)

                @block.gpsimd
                def _(pool):
                    link = Chain(pool, pool_chain)
                    pool.wait_ge(gates_ready, 1)
                    for t in range(TT):
                        ins = pool.tensor_tensor(nb[:, t], gates[:, t, 0:H2].unsqueeze(2).broadcast_to([P, H2, CH]),
                                                 strict[:].unsqueeze(1).broadcast_to([P, H2, CH]), ALU.mult)
                    ins.then_inc(nb_ready, 1)
                    for t in range(TT + 1):
                        if t < TT:
                            pool.wait_ge(z_ready, t + 1)
                            if t >= 2:
                                pool.wait_ge(r_ready, t - 1)
                            zt = z[:, t % 2].rearrange("p a (d two) -> p two (a d)", two=2)
                            x1, x2 = (zt[:, i].rearrange("p (q n) -> p q n", q=2) for i in range(2))
                            c, s = (m[:, t].rearrange("p h d -> p (h d)").unsqueeze(1).broadcast_to([P, 2, P])
                                    for m in (cm, sm))
                            if t > 0:
                                pool.wait_ge(r_ready, t)
                            pool.tensor_tensor(rb1[:], x1, s, ALU.mult)
                            link(pool.tensor_tensor(rb2[:], x2, c, ALU.mult))
                            pool.tensor_tensor(rb1[:], rb1[:], rb2[:], ALU.add).then_inc(pool_rot, 1)
                        if t > 0:
                            pool.wait_ge(rss_ready, t)
                            if t > 2:
                                pool.wait_ge(qk_ready, t - 2)
                            pool.tensor_tensor(rrn[:, (t - 1) % 2], rss[:, (t - 1) % 2], half[:], ALU.pow).then_inc(rrn_ready, 1)
                    pool.wait_ge(frac_var, 1)
                    link(pool.tensor_tensor(frs[:], fve[:], half[:, 0:TT], ALU.pow))
                    pool.tensor_tensor(fsc[:], frs[:], gates[:, :, 2 * H2], ALU.mult).then_inc(frac_scale, 1)

                @block.vector
                def _(dve):
                    link = Chain(dve, dve_chain)

                    def gates_step():
                        dve.wait_ge(gates_psum, 1)
                        n = 2 * H2 + 1
                        dve.tensor_tensor(gates_in[:], K[:, 0:TT * n].rearrange("p (t n) -> p t n", n=n),
                                          smb[:].unsqueeze(1).broadcast_to([P, TT, n]), ALU.add).then_inc(gates_read, 1)

                    for i in range(6):
                        w = conv[:, i // 2, i % 2]
                        dve.wait_ge(proj_ready, i + 1)
                        link(dve.tensor_scalar(y[:, i], proj[:, i, 0:L], w[:, 0:1], None, ALU.mult))
                        for j in range(1, 4):
                            ins = dve.scalar_tensor_tensor(out=y[:, i], in0=proj[:, i, j:j + L], scalar=w[:, j:j + 1],
                                                           in1=y[:, i], op0=ALU.mult, op1=ALU.add)
                            if j < 3:
                                link(ins)
                        ins.then_inc(conv_ready, 1)
                        if i == 3:
                            gates_step()
                    for t in range(TT + 1):
                        if t < TT:
                            dve.wait_ge(z_ready, t + 1)
                            if t > 0:
                                dve.wait_ge(r_ready, t)
                            zt = z[:, t % 2].rearrange("p a (d two) -> p two (a d)", two=2)
                            x1, x2 = (zt[:, i].rearrange("p (q n) -> p q n", q=2) for i in range(2))
                            c, s = (m[:, t].rearrange("p h d -> p (h d)").unsqueeze(1).broadcast_to([P, 2, P])
                                    for m in (cm, sm))
                            dve.tensor_tensor(ra1[:], x1, c, ALU.mult)
                            link(dve.tensor_tensor(ra2[:], x2, s, ALU.mult))
                            link(dve.tensor_tensor(ra1[:], ra1[:], ra2[:], ALU.subtract))
                            dve.wait_ge(pool_rot, t + 1)
                            dve.wait_ge(zm_ready, t + 1)
                            rt, zt = r[:, t % 2], zm[:, t % 2]
                            dve.tensor_tensor(rt[:, :, 0:CH], zt[:, :, 0:CH],
                                              ra1[:].rearrange("p q (h d) -> p (q h) d", d=CH), ALU.add)
                            dve.tensor_tensor(rt[:, :, CH:], zt[:, :, CH:],
                                              rb1[:].rearrange("p q (h d) -> p (q h) d", d=CH), ALU.add).then_inc(r_ready, 1)
                        if t > 0:
                            i = (t - 1) % 2
                            dve.wait_ge(rsq_ready, t)
                            link(dve.tensor_reduce(rss[:, i], rsq[:], AX.X, ALU.add))
                            dve.tensor_scalar(rss[:, i], rss[:, i], 1e-6, None, ALU.add).then_inc(rss_ready, 1)
                            dve.wait_ge(rrn_ready, t)
                            dve.tensor_tensor(qk[:, t - 1], r[:, i], rrn[:, i].unsqueeze(2).broadcast_to([P, 8, DH]),
                                              ALU.mult).then_inc(qk_ready, 1)
                        if t in (2, 3):
                            g = t - 2
                            dve.wait_ge(v_psum, g + 1)
                            dve.wait_ge(gates_ready, 1)
                            for tt in range(2):
                                ins = dve.tensor_tensor(vb[:, 2 * g + tt], V[:, tt * D:(tt + 1) * D].rearrange(
                                    "p (h d) -> p h d", d=DH),
                                    gates[:, 2 * g + tt, 0:H2].unsqueeze(2).broadcast_to([P, H2, DH]), ALU.mult)
                            ins.then_inc(vb_ready, 1)
                    dve.wait_ge(frac_sums, TT)
                    dve.tensor_scalar(fve[:], fss[:], 1.0 / D, 1e-5, ALU.mult, ALU.add).then_inc(frac_var, 1)
                    for n in range(4):
                        g, e = divmod(n, 2)
                        dve.wait_ge(gram_psum, n + 1)
                        dve.wait_ge(nb_ready, 1)
                        for c in range(NC4):
                            part = slice(c * CH, (c + 1) * CH)
                            hs = slice(e, H2, 2)
                            src = G[e][part, :].rearrange("p (t i n) -> p t i n", t=2, i=2)[:, :, :, part]
                            dve.tensor_tensor(low[part, 2 * g:2 * g + 2, hs], src, nb[part, 2 * g:2 * g + 2, hs],
                                              ALU.mult).then_inc(low_ready, 1)
                    dve.wait_ge(frac_scale, 1)
                    dve.wait_ge(x_in, 16)
                    for t in range(TT):
                        link(dve.scalar_tensor_tensor(out=xg[:, t], in0=J[t // 2][:, (t % 2) * D:(t % 2 + 1) * D],
                                                      scalar=fsc[:, t:t + 1], in1=mixw[:], op0=ALU.mult, op1=ALU.mult))
                        dve.tensor_tensor(xg[:, t], xg[:, t], x[:, t], ALU.add).then_inc(xg_ready, 1)
            clear(nc, sems)

        with nc.Fori(0, B - 1) as b:
            batch(b, True)
        batch(B - 1, False)


def inverse_phase(nc, a, low_dram, inv_dram):
    with ExitStack() as ctx:
        sb, bank, sem, sems = space(nc, ctx, "i")
        A = sb("A", [P, NC4, CH, CH])
        AT = sb("AT", [P, NC4, CH, CH])
        prod = sb("prod", [P, NC4, CH * CH // 4])
        eye = sb("eye", [P, CH, CH])
        loaded = sem("loaded")
        turned = sem("turned")
        stored = sem("stored")
        dve_chain = sem("dve_chain")
        pool_chain = sem("pool_chain")

        def substitute(eng, link, cs):
            n = cs.stop - cs.start
            for i in range(1, CH - 1):
                below = CH - 1 - i
                weight = A[:, cs, i + 1:, i].unsqueeze(3).broadcast_to([P, n, below, i])
                complete = A[:, cs, i, 0:i].unsqueeze(2).broadcast_to([P, n, below, i])
                pr = prod[:, cs, 0:below * i].rearrange("p c (r k) -> p c r k", k=i)
                link(eng.tensor_tensor(pr, complete, weight, ALU.mult))
                rows = A[:, cs, i + 1:, 0:i]
                link(eng.tensor_tensor(rows, rows, pr, ALU.add))

        with nc.Block() as block:
            @block.sync
            def _(sp):
                sp.dma_start(A[:], low_dram.rearrange("b t h c i j -> (b t h) c i j")).then_inc(loaded, 16)
                sp.dma_start(eye[:], a["c_eye32"]).then_inc(loaded, 16)
                sp.wait_ge(turned, NC4)
                sp.dma_start(inv_dram.rearrange("b t h c i j -> (b t h) c i j"), AT[:]).then_inc(stored, 16)
                sp.wait_ge(stored, 16)

            @block.gpsimd
            def _(pool):
                link = Chain(pool, pool_chain)
                pool.wait_ge(loaded, 32)
                substitute(pool, link, slice(NC4 - 1, NC4))

            @block.vector
            def _(dve):
                link = Chain(dve, dve_chain)
                dve.wait_ge(loaded, 32)
                substitute(dve, link, slice(0, NC4 - 1))
                dve.wait_ge(pool_chain, 2 * (CH - 2))
                for c in range(NC4):
                    dve.tensor_tensor(AT[:, c], A[:, c].rearrange("p i j -> p j i"), eye[:], ALU.add).then_inc(turned, 1)
        clear(nc, sems)


def delta_rule_phase(nc, a, xg_dram, qk_dram, vb_dram, bg_dram, inv_dram, x1_dram):
    NG = 2 * H2 + 1
    with ExitStack() as ctx:
        sb, bank, sem, sems = space(nc, ctx, "d")
        ident = sb("ident", [P, P])
        causal = sb("causal", [P, P])
        chunk_of = sb("chunk_of", [P, NC4])
        wo = sb("wo", [P, KD, D])
        onw = sb("onw", [P, 1])
        eye = sb("eye", [P, DH])
        half = sb("half", [P, TT * H2])
        qk = sb("qk", [P, TT, 8, DH])
        vk = sb("vk", [P, TT, H2, 2, DH])
        gates = sb("gates", [P, TT, NG])
        xg = sb("xg", [P, TT, D])
        inv = sb("inv", [P, TT, H2, P])
        gx = sb("gx", [P, TT, H2, DH])
        gm = sb("gm", [P, TT, 2, NC4])
        gI = sb("gI", [P, TT, NC4, 2, DH])
        qkT = sb("qkT", [P, TT, 4, P])
        attn = sb("attn", [P, 2, TT, 2, P])
        uw = sb("uw", [P, TT, H2, 2, DH])
        qpT = sb("qpT", [P, TT, 2, P])
        MT = sb("MT", [P, TT, NC4, 2, DH])
        kb_u = sb("kb_u", [P, TT, NC4, 2, DH])
        S = sb("S", [P, NCH + 1, 2, DH])
        osq = sb("osq", [P, 2, TT * 2, DH])
        oss = sb("oss", [P, 2, TT * 2])
        ors = sb("ors", [P, 2, TT * 2])
        on = sb("on", [P, TT, H2, DH])
        onT = sb("onT", [P, KD, L])
        x1 = sb("x1", [P, TT, D])
        R = [bank(f"R{i}") for i in range(8)]

        loaded = sem("loaded")
        dve_chain = sem("dve_chain")
        with nc.Block() as block:
            @block.sync
            def _(sp):
                loads = [(ident[:], a["c_ident"]), (causal[:], a["c_causal"]), (chunk_of[:], a["c_chunk_of"]),
                         (wo[:], a["L0_attn_Wo"].rearrange("(k p) n -> p k n", p=P)),
                         (onw[0:DH], a["L0_attn_o_norm_w"].rearrange("(n o) -> n o", o=1)),
                         (onw[DH:P], a["L0_attn_o_norm_w"].rearrange("(n o) -> n o", o=1)),
                         (eye[0:DH], a["c_ident"][0:DH, 0:DH]), (eye[DH:P], a["c_ident"][0:DH, 0:DH])]
                for dst, src in loads:
                    sp.dma_start(dst, src).then_inc(loaded, 16)

            @block.gpsimd
            def _(pool):
                pool.memset(half[:], -0.5)
                pool.memset(inv[:], 0.0)
                pool.memset(S[:, 0], 0.0)

            @block.vector
            def _(dve):
                dve.wait_ge(loaded, 16 * 8)
                for k in range(KD):
                    dve.tensor_scalar(wo[:, k], wo[:, k], onw[:, 0:1], None, ALU.mult)
        clear(nc, sems)

        rows_in = sem("rows_in")
        xg_in = sem("xg_in")
        kb_ready = sem("kb_ready")
        gx_ready = sem("gx_ready")
        gm_psum = sem("gm_psum")
        gm_ready = sem("gm_ready")
        gI_ready = sem("gI_ready")
        qkT_psum = sem("qkT_psum")
        qkT_ready = sem("qkT_ready")
        attn_psum = sem("attn_psum")
        attn_ready = sem("attn_ready")
        uw_psum = sem("uw_psum")
        uw_ready = sem("uw_ready")
        qp_psum = sem("qp_psum")
        qp_ready = sem("qp_ready")
        step_psum = sem("step_psum")
        MT_ready = sem("MT_ready")
        ku_ready = sem("ku_ready")
        state_psum = [sem(f"state_psum{e}") for e in range(2)]
        state_ready = [sem(f"state_ready{e}") for e in range(2)]
        o_psum = sem("o_psum")
        osq_ready = sem("osq_ready")
        oss_ready = sem("oss_ready")
        ors_ready = sem("ors_ready")
        on_ready = sem("on_ready")
        onT_psum = sem("onT_psum")
        onT_ready = sem("onT_ready")
        core_psum = sem("core_psum")
        x1_ready = sem("x1_ready")
        stored = sem("stored")

        ORDER = [(t % 2, "qkT", t) for t in range(TT)]
        ORDER += [(2 + e, "attn", e) for e in range(2)] + [(t, "uw", t) for t in range(2)]
        ORDER += [(2 + e, "attn", 2 + e) for e in range(2)] + [(t % 2, "uw", t) for t in (2, 3)]
        ORDER += [(4, "gm", 0), (2, "qp", 0), (3, "qp", 1)]
        ORDER += [(4 + c, "step", 4 * g + c) for g in range(2) for c in range(NC4)]
        ORDER += [(e, "o", e) for e in range(2)] + [(2 + e, "state", e) for e in range(2)]
        ORDER += [(4 + k, "onT", k) for k in range(KD)] + [(6 + g, "core", g) for g in range(2)]

        def drained(step, n):
            return {"qkT": [(qkT_ready, n + 1)], "attn": [(attn_ready, n + 1)], "uw": [(uw_ready, n + 1)],
                    "gm": [(gm_ready, 1)], "qp": [(qp_ready, n + 1)],
                    "step": [(MT_ready, n + 1), (ku_ready, n + 1)]}[step]

        before = drained_before(ORDER, drained)

        N_IN = 3 + NC4

        def load(b, sp, wait_gates, wait_values, wait_rows):
            wait_gates()
            sp.dma_start(gates[:].rearrange("p t n -> p (t n)"),
                         bg_dram[bass.ds(b, 1), :, :].rearrange("o p n -> (o p) n")).then_inc(rows_in, 16)
            wait_values()
            sp.dma_start(vk[:, :, :, 0], vb_dram[bass.ds(b, 1), :, :].rearrange(
                "o p (t h d) -> (o p) t h d", h=H2, d=DH)).then_inc(rows_in, 16)
            for c in range(NC4):
                part = slice(c * CH, (c + 1) * CH)
                sp.dma_start(inv[part, :, :, part].rearrange("p t h i -> p (t h) i"),
                             inv_dram[bass.ds(b, 1), :, :, c].rearrange("o t h j i -> j (o t h) i")).then_inc(rows_in, 16)
            wait_rows()
            sp.dma_start(qk[:].rearrange("p t h d -> p (t h d)"),
                         qk_dram[bass.ds(b, 1), :, :].rearrange("o p n -> (o p) n")).then_inc(rows_in, 16)

        with nc.Block() as block:
            @block.sync
            def _(sp):
                load(0, sp, lambda: None, lambda: None, lambda: None)
                sp.wait_ge(rows_in, 16 * N_IN)
        clear(nc, sems)

        def batch(b, ahead):
            with nc.Block() as block:
                @block.sync
                def _(sp):
                    sp.dma_start(xg[:].rearrange("p t d -> p (t d)"),
                                 xg_dram[bass.ds(b, 1), :, :].rearrange("o p n -> (o p) n")).then_inc(xg_in, 16)
                    if ahead:
                        def gates_used():
                            sp.wait_ge(kb_ready, TT)
                            sp.wait_ge(gx_ready, 1)

                        load(b + 1, sp, gates_used, lambda: sp.wait_ge(uw_psum, TT),
                             lambda: sp.wait_ge(step_psum, 2 * NC4))
                    for g in range(2):
                        sp.wait_ge(x1_ready, g + 1)
                        sp.dma_start(x1_dram[bass.ds(b, 1), g * 2 * P:(g + 1) * 2 * P, :].rearrange(
                            "o (t p) d -> p (o t) d", p=P), x1[:, 2 * g:2 * g + 2]).then_inc(stored, 16)
                    sp.wait_ge(stored, 32)
                    if ahead:
                        sp.wait_ge(rows_in, 16 * N_IN)

                @block.gpsimd
                def _(pool):
                    for t in range(TT):
                        pool.tensor_tensor(vk[:, t, :, 1], qk[:, t, H2:],
                                           gates[:, t, 0:H2].unsqueeze(2).broadcast_to([P, H2, DH]), ALU.mult)\
                            .then_inc(kb_ready, 1)
                    for t in range(TT):
                        ins = pool.tensor_copy(gx[:, t], gates[:, t, H2:2 * H2].unsqueeze(2).broadcast_to([P, H2, DH]))
                    ins.then_inc(gx_ready, 1)
                    pool.wait_ge(gm_ready, 1)
                    for t in range(TT):
                        for c in range(NC4):
                            ins = pool.tensor_tensor(gI[:, t, c], eye[:].unsqueeze(1).broadcast_to([P, 2, DH]),
                                                     gm[:, t, :, c].unsqueeze(2).broadcast_to([P, 2, DH]), ALU.mult)
                        ins.then_inc(gI_ready, 1)
                    pool.wait_ge(oss_ready, 1)
                    pool.tensor_tensor(ors[:].rearrange("p e n -> p (e n)"), oss[:].rearrange("p e n -> p (e n)"),
                                       half[:], ALU.pow).then_inc(ors_ready, 1)

                @block.tensor
                def _(pe):
                    def fill(i, step, n):
                        for s, value in before[i, step, n]:
                            pe.wait_ge(s, value)
                        return R[i]

                    for t in range(TT):
                        o = fill(t % 2, "qkT", t)
                        for i in range(4):
                            last = pe.transpose(o[:, i * P:(i + 1) * P],
                                                qk[:, t, 2 * i:2 * i + 2].rearrange("p a d -> p (a d)"), ident[:])
                        last.then_inc(qkT_psum, 1)

                    def attention(g):
                        pe.wait_ge(qkT_ready, 2 * g + 2)
                        for e in range(2):
                            o = fill(2 + e, "attn", 2 * g + e)
                            part = slice(e * DH, (e + 1) * DH)
                            for tt in range(2):
                                for i in range(2):
                                    t, j = 2 * g + tt, 2 * tt + i
                                    last = pe.matmul(o[:, j * P:(j + 1) * P], qkT[part, t, 2 + i], qkT[part, t, i],
                                                     start=True, stop=True)
                            last.then_inc(attn_psum, 1)

                    def solve(t):
                        pe.wait_ge(kb_ready, t + 1)
                        o = fill(t % 2, "uw", t)
                        for h in range(H2):
                            last = pe.matmul(o[:, h * P:(h + 1) * P], inv[:, t, h],
                                             vk[:, t, h].rearrange("p a d -> p (a d)"), start=True, stop=True)
                        last.then_inc(uw_psum, 1)

                    attention(0)
                    solve(0)
                    solve(1)
                    attention(1)
                    solve(2)
                    solve(3)
                    pe.wait_ge(gx_ready, 1)
                    o = fill(4, "gm", 0)
                    for t in range(TT):
                        for i in range(2):
                            j = (2 * t + i) * NC4
                            last = pe.matmul(o[:, j:j + NC4], gx[:, t, 2 * i:2 * i + 2].rearrange("p a d -> p (a d)"),
                                             chunk_of[:], start=True, stop=True)
                    last.then_inc(gm_psum, 1)
                    for g in range(2):
                        pe.wait_ge(uw_ready, 2 * g + 2)
                        pe.wait_ge(attn_ready, 2 * g + 2)
                        o = fill(2 + g, "qp", g)
                        for tt in range(2):
                            for h in range(H2):
                                t, i, e = 2 * g + tt, h // 2, h % 2
                                last = pe.matmul(o[e * DH:(e + 1) * DH, (2 * tt + i) * P:(2 * tt + i + 1) * P],
                                                 uw[:, t, h, 1], attn[:, e, t, i], start=True, stop=True)
                        last.then_inc(qp_psum, 1)

                    def step(g, c):
                        o = fill(4 + c, "step", 4 * g + c)
                        part = slice(c * CH, (c + 1) * CH)
                        for tt in range(2):
                            for h in range(H2):
                                t, i, e = 2 * g + tt, h // 2, h % 2
                                keys = qk[part, t, H2 + h]
                                at = 4 * tt + i
                                for lhs, rhs, j in ((uw[part, t, h, 1], keys, at), (keys, uw[part, t, h, 0], at + 2)):
                                    last = pe.matmul(o[e * DH:(e + 1) * DH, j * DH:(j + 1) * DH], lhs, rhs,
                                                     start=True, stop=True, tile_position=(c * CH, e * DH))
                        last.then_inc(step_psum, 1)

                    for c in range(NC4):
                        step(0, c)
                    for n in range(NCH):
                        t, c = divmod(n, NC4)
                        for e in range(2):
                            part = slice(e * DH, (e + 1) * DH)
                            if n > 0:
                                pe.wait_ge(state_ready[e], n)
                            if n < NCH - 1:
                                if n == 0:
                                    fill(2 + e, "state", e)
                                pe.wait_ge(MT_ready, 4 * (t // 2) + c + 1)
                                for i in range(2):
                                    last = pe.matmul(R[2 + e][part, i * DH:(i + 1) * DH], MT[part, t, c, i], S[part, n, i],
                                                     start=True, stop=True)
                                last.then_inc(state_psum[e], 1)
                            if n == 0:
                                fill(e, "o", e)
                                pe.wait_ge(qp_ready, 2)
                            for i in range(2):
                                o = R[e][:, (2 * t + i) * DH:(2 * t + i + 1) * DH]
                                if c == 0:
                                    pe.matmul(o, attn[:, e, t, i], uw[:, t, 2 * i + e, 0], start=i == 0, stop=False,
                                              skip_group_check=True)
                            for i in range(2):
                                o = R[e][:, (2 * t + i) * DH:(2 * t + i + 1) * DH]
                                last = pe.matmul(o[c * CH:(c + 1) * CH], qpT[part, t, i, c * CH:(c + 1) * CH], S[part, n, i],
                                                 start=False, stop=c == NC4 - 1, skip_group_check=True,
                                                 tile_position=(e * DH, c * CH))
                            if n == NCH - 1:
                                last.then_inc(o_psum, 1)
                        if n < NC4:
                            step(1, n)
                    pe.wait_ge(on_ready, 2)
                    for k in range(KD):
                        o = fill(4 + k, "onT", k)
                        for t in range(TT):
                            last = pe.transpose(o[:, t * P:(t + 1) * P],
                                                on[:, t, 2 * k:2 * k + 2].rearrange("p a d -> p (a d)"), ident[:])
                        last.then_inc(onT_psum, 1)
                    pe.wait_ge(onT_ready, KD)
                    for g in range(2):
                        o = fill(6 + g, "core", g)
                        for tt in range(2):
                            for k in range(KD):
                                t = 2 * g + tt
                                last = pe.matmul(o[:, tt * D:(tt + 1) * D], onT[:, k, t * P:(t + 1) * P], wo[:, k],
                                                 start=k == 0, stop=k == KD - 1)
                        last.then_inc(core_psum, 1)

                @block.scalar
                def _(act):
                    for t in range(TT):
                        act.wait_ge(qkT_psum, t + 1)
                        act.copy(qkT[:, t].rearrange("p a n -> p (a n)"), R[t % 2][:, :]).then_inc(qkT_ready, 1)
                    for t in range(TT):
                        act.wait_ge(uw_psum, t + 1)
                        act.copy(uw[:, t].rearrange("p h a d -> p (h a d)"), R[t % 2][:, :]).then_inc(uw_ready, 1)
                    for n in range(2 * NC4):
                        g, c = divmod(n, NC4)
                        act.wait_ge(step_psum, n + 1)
                        act.wait_ge(MT_ready, n + 1)
                        act.copy(kb_u[:, 2 * g:2 * g + 2, c].rearrange("p t i d -> p t (i d)"),
                                 R[4 + c][:, :].rearrange("p (t s n) -> p t s n", t=2, s=2)[:, :, 1]).then_inc(ku_ready, 1)
                    for e in range(2):
                        act.wait_ge(o_psum, e + 1)
                        act.activation(osq[:, e].rearrange("p n d -> p (n d)"), R[e][:, :], ACT.Square).then_inc(osq_ready, 1)
                    act.wait_ge(onT_psum, 1)
                    act.copy(onT[:, 0], R[4][:, :]).then_inc(onT_ready, 1)

                @block.vector
                def _(dve):
                    link = Chain(dve, dve_chain)

                    def mask(n):
                        g, e = divmod(n, 2)
                        dve.wait_ge(attn_psum, n + 1)
                        dve.tensor_tensor(attn[:, e, 2 * g:2 * g + 2].rearrange("p t i n -> p (t i) n"),
                                          R[2 + e][:, :].rearrange("p (j n) -> p j n", n=P),
                                          causal[:].unsqueeze(1).broadcast_to([P, 4, P]), ALU.mult).then_inc(attn_ready, 1)

                    for n in range(4):
                        mask(n)
                    dve.wait_ge(gm_psum, 1)
                    dve.tensor_copy(gm[:].rearrange("p t i c -> p (t i c)"), R[4][:, 0:TT * 2 * NC4]).then_inc(gm_ready, 1)
                    for g in range(2):
                        dve.wait_ge(qp_psum, g + 1)
                        dve.wait_ge(qkT_ready, TT)
                        dve.scalar_tensor_tensor(out=qpT[:, 2 * g:2 * g + 2].rearrange("p t i n -> p t (i n)"),
                                                 in0=R[2 + g][:, :].rearrange("p (t n) -> p t n", t=2), scalar=-1.0,
                                                 in1=qkT[:, 2 * g:2 * g + 2, 0:2].rearrange("p t i n -> p t (i n)"),
                                                 op0=ALU.mult, op1=ALU.add).then_inc(qp_ready, 1)

                    def transition(n):
                        g, c = divmod(n, NC4)
                        dve.wait_ge(step_psum, n + 1)
                        dve.wait_ge(gI_ready, 2 * g + 2)
                        dve.tensor_tensor(MT[:, 2 * g:2 * g + 2, c].rearrange("p t i d -> p t (i d)"),
                                          gI[:, 2 * g:2 * g + 2, c].rearrange("p t i d -> p t (i d)"),
                                          R[4 + c][:, :].rearrange("p (t s n) -> p t s n", t=2, s=2)[:, :, 0],
                                          ALU.subtract).then_inc(MT_ready, 1)
                    for n in range(NC4):
                        transition(n)
                    for n in range(NCH - 1):
                        t, c = divmod(n, NC4)
                        for e in range(2):
                            part = slice(e * DH, (e + 1) * DH)
                            dve.wait_ge(state_psum[e], n + 1)
                            dve.wait_ge(ku_ready, 4 * (t // 2) + c + 1)
                            dve.tensor_tensor(S[part, n + 1].rearrange("p i d -> p (i d)"), R[2 + e][part, 0:2 * DH],
                                              kb_u[part, t, c].rearrange("p i d -> p (i d)"), ALU.add)\
                               .then_inc(state_ready[e], 1)
                        if n < NC4:
                            transition(NC4 + n)
                    dve.wait_ge(osq_ready, 2)
                    link(dve.tensor_reduce(oss[:].rearrange("p e n -> p (e n)"),
                                           osq[:].rearrange("p e n d -> p (e n) d"), AX.X, ALU.add))
                    dve.tensor_scalar(oss[:], oss[:], 1.0 / DH, 1e-5, ALU.mult, ALU.add).then_inc(oss_ready, 1)
                    dve.wait_ge(ors_ready, 1)
                    for e in range(2):
                        dve.tensor_tensor(on[:].rearrange("p t (i e) d -> p (t i) e d", e=2)[:, :, e],
                                          R[e][:, :].rearrange("p (n d) -> p n d", d=DH),
                                          ors[:, e].unsqueeze(2).broadcast_to([P, TT * 2, DH]), ALU.mult).then_inc(on_ready, 1)
                    dve.wait_ge(onT_psum, 2)
                    dve.tensor_copy(onT[:, 1], R[5][:, :]).then_inc(onT_ready, 1)
                    dve.wait_ge(xg_in, 16)
                    for g in range(2):
                        ts = slice(2 * g, 2 * g + 2)
                        dve.wait_ge(core_psum, g + 1)
                        dve.tensor_tensor(x1[:, ts].rearrange("p t d -> p (t d)"), R[6 + g][:, :],
                                          xg[:, ts].rearrange("p t d -> p (t d)"), ALU.add).then_inc(x1_ready, 1)
            clear(nc, sems)

        with nc.Fori(0, B - 1) as b:
            batch(b, True)
        batch(B - 1, False)


def rank_below(dve, link, out, vals, lower, gt, ge, n_rows, n, k):
    other = vals.unsqueeze(2).broadcast_to([P, n_rows, n, n])
    own = vals.unsqueeze(3).broadcast_to([P, n_rows, n, n])
    g = gt[:, 0:n_rows * n * n].rearrange("p (r e f) -> p r e f", e=n, f=n)
    q = ge[:, 0:n_rows * n * n].rearrange("p (r e f) -> p r e f", e=n, f=n)
    dve.tensor_tensor(g, other, own, ALU.is_gt)
    link(dve.tensor_tensor(q, other, own, ALU.is_ge))
    link(dve.tensor_tensor(q, q, lower[:, 0:n, 0:n].unsqueeze(1).broadcast_to([P, n_rows, n, n]), ALU.mult))
    link(dve.tensor_tensor(g, g, q, ALU.max))
    link(dve.tensor_reduce(out, g, AX.X, ALU.add))
    link(dve.tensor_scalar(out, out, float(k), None, ALU.is_lt))


def mixtures_phase(nc, a, x1_dram, out):
    F32R = mybir.dt.float32r
    with ExitStack() as ctx:
        sb, bank, sem, sems = space(nc, ctx, "m")
        ident = sb("ident", [P, P])
        ident16 = sb("ident16", [P, P], BF16)
        lower = sb("lower", [P, E2, E2])
        pick = sb("pick", [3 * E2, 2, 8, P], BF16)
        N1S, N1 = S1 // P, S1 // P + E1
        N2S, N2 = S2W // P, S2W // P + E2 // 2
        NI = (N1, N2)
        SHARED = (N1S, N2S)
        router_w = [[sb(f"router{m}{j}", [P, KD, (E1, E2)[m]], F32R) for j in range(2)] for m in range(2)]
        gate = [[sb(f"gate{m}{j}", [P, KD, NI[m], P], F32R) for j in range(2)] for m in range(2)]
        up = [[sb(f"up{m}{j}", [P, KD, NI[m], P], F32R) for j in range(2)] for m in range(2)]
        down = [[sb(f"down{m}{j}", [P, NI[m], D], F32R) for j in range(2)] for m in range(2)]
        wg = sb("wg", [DH, E1])
        cb = sb("cb", [P, E2])

        GB = [bank(f"G{i}") for i in range(2)]
        UB = [bank(f"U{i}") for i in range(2)]
        YB = [bank(f"Y{i}") for i in range(2)]
        WB = bank("W")
        MB = bank("M")
        MB16 = MB[:, :].bitcast(BF16)

        N_SMALL = 7
        loaded = sem("loaded")
        dve_chain = sem("dve_chain")

        with ExitStack() as staging:
            STAGES = 3
            stage = staging.enter_context(nc.sbuf_tensor("m_stage", [P, STAGES, max(NI) * P], F32))
            pick_in = staging.enter_context(nc.sbuf_tensor("m_pick_in", [3 * E2, 2, 8, P], F32))
            routers = staging.enter_context(nc.sbuf_tensor("m_routers", [P, KD, E1 + E2], F32))
            stage_in = [sem(f"stage{i}_in") for i in range(STAGES)]
            stage_high = sem("stage_high")
            stage_low = sem("stage_low")
            routers_high = sem("routers_high")

            units = []
            for m in range(2):
                width = (M1, M2)[m]
                names = ({"gate": ("L0_cond2_sw_gate", "L0_cond2_w_gate"), "up": ("L0_cond2_sw_up", "L0_cond2_w_up")},
                         {"gate": ("L0_ffn_shared_gate_w", "L0_ffn_gate_w"), "up": ("L0_ffn_shared_up_w", "L0_ffn_up_w")})[m]
                cut = SHARED[m] * P
                for dst, (shared, own) in ((gate, names["gate"]), (up, names["up"])):
                    for k in range(KD):
                        ks = slice(k * P, (k + 1) * P)
                        units.append(([(0, cut, None, a[shared][ks, :]),
                                       (cut, NI[m] * P, width, a[own][:, ks, :].rearrange("e p m -> p e m"))],
                                      [dst[m][j][:, k].rearrange("p i n -> p (i n)") for j in range(2)]))
                shared = a[("L0_cond2_sw_down", "L0_ffn_shared_down_w")[m]].rearrange("(i p) n -> p i n", p=P)
                own = (a["L0_cond2_w_down"].rearrange("e m n -> m e n"),
                       a["L0_ffn_down_w"].rearrange("(i e) m n -> (e m) i n", e=2))[m]
                for half_of in range(2):
                    i0, i1 = half_of * NI[m] // 2, (half_of + 1) * NI[m] // 2
                    ns = min(max(SHARED[m] - i0, 0), i1 - i0)
                    loads = [(0, ns * D, D, shared[:, i0:i0 + ns])] if ns else []
                    loads.append((ns * D, (i1 - i0) * D, D, own[:, i0 + ns - SHARED[m]:i1 - SHARED[m]]))
                    units.append((loads, [down[m][j][:, i0:i1].rearrange("p i n -> p (i n)") for j in range(2)]))

            def stage_value(u):
                return 16 * sum(len(units[v][0]) for v in range(u % STAGES, u + 1, STAGES))

            with nc.Block() as block:
                @block.sync
                def _(sp):
                    small = [(ident[:], a["c_ident"]), (lower[:], a["c_lower"]), (pick_in[:], a["c_pick"]),
                             (routers[:, :, 0:E1], a["L0_cond2_wt"]), (routers[:, :, E1:], a["L0_ffn_router_w"]),
                             (wg[:], a["L0_cond2_wg"]), (cb[:], row(a["L0_ffn_correction_bias"], E2))]
                    assert len(small) == N_SMALL
                    for dst, src in small:
                        sp.dma_start(dst, src).then_inc(loaded, 16)
                    for u, (loads, _) in enumerate(units):
                        if u >= STAGES:
                            sp.wait_ge(stage_low, u - STAGES + 1)
                        for lo, hi, width, src in loads:
                            dst = stage[:, u % STAGES, lo:hi]
                            if width is not None:
                                dst = dst.rearrange("p (e m) -> p e m", m=width)
                            sp.dma_start(dst, src).then_inc(stage_in[u % STAGES], 16)

                @block.scalar
                def _(act):
                    for u, (_, (high, low)) in enumerate(units):
                        act.wait_ge(stage_in[u % STAGES], stage_value(u))
                        n = high.shape[-1]
                        act.copy(high, stage[:, u % STAGES, 0:n]).then_inc(stage_high, 1)

                @block.vector
                def _(dve):
                    dve.wait_ge(loaded, 16 * N_SMALL)
                    dve.tensor_copy(ident16[:], ident[:])
                    dve.tensor_copy(pick[:], pick_in[:])
                    for m, cols in ((0, slice(0, E1)), (1, slice(E1, E1 + E2))):
                        dve.tensor_copy(router_w[m][0][:], routers[:, :, cols]).then_inc(routers_high, 1)
                        dve.wait_ge(routers_high, m + 1)
                        dve.tensor_tensor(router_w[m][1][:], routers[:, :, cols], router_w[m][0][:].bitcast(F32),
                                          ALU.subtract)
                    for u, (_, (high, low)) in enumerate(units):
                        dve.wait_ge(stage_high, u + 1)
                        n = high.shape[-1]
                        dve.tensor_tensor(low, stage[:, u % STAGES, 0:n], high.bitcast(F32),
                                          ALU.subtract).then_inc(stage_low, 1)
            clear(nc, sems)

        G_SLOTS, H_SLOTS = 3, 2
        cond_now = sb("cond_now", [DH, 1])
        condb = sb("condb", [DH, P])
        x_turn = sb("x_turn", [P, TT, D])
        x1 = sb("x1", [P, TT, D])
        inT = [sb(f"inT{j}", [P, KD, L], F32R) for j in range(2)]
        lg = sb("lg", [P, TT, E2])
        mx = sb("mx", [P, TT])
        ex = sb("ex", [P, TT, E2])
        sc = sb("sc", [P, TT, E2])
        sbias = sb("sbias", [P, TT, E2])
        sel = sb("sel", [P, TT, E2])
        gsum = sb("gsum", [P, TT, G2])
        gsel = sb("gsel", [P, TT, G2])
        goff = sb("goff", [P, TT, G2])
        wsum = sb("wsum", [P, TT])
        w = sb("w", [P, TT, E2])
        rest = sb("rest", [P, TT, E2])
        parts = sb("parts", [P, TT, 3 * E2], BF16)
        wT = sb("wT", [3 * E2, L], BF16)
        hid = sb("hid", [P, G_SLOTS, L])
        hid_part = [sb(f"hid_part{j}", [P, H_SLOTS, L], F32R) for j in range(2)]
        outT = sb("outT", [P, KD, L])
        res = sb("res", [P, TT, D])
        gt = outT[:].rearrange("p k n -> p (k n)")
        ge = res[:].rearrange("p t d -> p (t d)")

        x_in = sem("x_in")
        cond_in = sem("cond_in")
        x_ahead = sem("x_ahead")
        turned = sem("turned")
        rows_back = sem("rows_back")
        in_high = sem("in_high")
        in_low = sem("in_low")
        outT_act = sem("outT_act")
        outT_dve = sem("outT_dve")
        logits_psum = sem("logits_psum")
        shifted = sem("shifted")
        exps_ready = sem("exps_ready")
        parts_ready = sem("parts_ready")
        wT_psum = sem("wT_psum")
        wT_ready = sem("wT_ready")
        gate_psum = sem("gate_psum")
        up_psum = sem("up_psum")
        weight_psum = sem("weight_psum")
        gate_active = sem("gate_active")
        mult_up = sem("mult_up")
        weighted = sem("weighted")
        hid_high = sem("hid_high")
        hid_low = sem("hid_low")
        hid_used = sem("hid_used")
        res_ready = sem("res_ready")
        res_out = sem("res_out")

        ITEMS = [(0, i) for i in range(N1)] + [(1, i) for i in range(N2)]
        NQ = len(ITEMS)
        TERMS = [(i, j, k) for k in range(KD) for i, j in ((0, 0), (0, 1), (1, 0))]

        def routed(q):
            m, i = ITEMS[q]
            return i >= SHARED[m]

        def n_routed(q):
            return sum(routed(j) for j in range(q + 1))

        def turn_rows(pe):
            for k in range(KD):
                for t in range(TT):
                    last = pe.transpose(GB[k][:, t * P:(t + 1) * P], x_turn[:, t, k * P:(k + 1) * P], ident[:])
                last.then_inc(turned, 1)

        def in_highs(act, banks, banks_full=None):
            for k in range(KD):
                if banks_full:
                    act.wait_ge(banks_full, k + 1)
                act.copy(inT[0][:, k], banks[k][:, :]).then_inc(in_high, 1)

        def in_lows(dve, n, banks):
            for k in range(KD):
                dve.wait_ge(in_high, KD * n + k + 1)
                dve.tensor_tensor(inT[1][:, k], banks[k][:, :], inT[0][:, k].bitcast(F32),
                                  ALU.subtract).then_inc(in_low, 1)

        with nc.Block() as block:
            @block.sync
            def _(sp):
                sp.dma_start(x_turn[:], x1_dram[0].rearrange("(t p) d -> p t d", p=P)).then_inc(x_ahead, 16)
                sp.dma_start(cond_now[:], a["c_cond"][0, :, :]).then_inc(cond_in, 16)

            @block.tensor
            def _(pe):
                pe.wait_ge(x_ahead, 16)
                turn_rows(pe)

            @block.scalar
            def _(act):
                in_highs(act, GB, turned)

            @block.vector
            def _(dve):
                in_lows(dve, 0, GB)
                dve.wait_ge(cond_in, 16)
                dve.tensor_copy(condb[:], cond_now[:].broadcast_to([DH, P]))
        clear(nc, sems)

        def batch(b, ahead):
            with nc.Block() as block:
                @block.sync
                def _(sp):
                    sp.dma_start(x1[:], x1_dram[bass.ds(b, 1), :, :].rearrange("o (t p) d -> p (o t) d", p=P)).then_inc(x_in, 16)
                    if ahead:
                        sp.dma_start(x_turn[:], x1_dram[bass.ds(b + 1, 1), :, :].rearrange(
                            "o (t p) d -> p (o t) d", p=P)).then_inc(x_ahead, 16)
                        sp.dma_start(cond_now[:], a["c_cond"][bass.ds(b + 1, 1), :, :].rearrange(
                            "o n k -> (o n) k")).then_inc(cond_in, 16)
                    for half_of in range(2):
                        sp.wait_ge(res_ready, half_of + 1)
                        ts = slice(2 * half_of, 2 * half_of + 2)
                        sp.dma_start(out[bass.ds(b, 1), half_of * 2 * P:(half_of + 1) * 2 * P, :].rearrange(
                            "o (t p) d -> p (o t) d", p=P), res[:, ts]).then_inc(res_out, 16)
                    sp.wait_ge(res_out, 32)

                @block.tensor
                def _(pe):
                    def router(m):
                        if m == 1:
                            pe.wait_ge(in_high, KD)
                            pe.wait_ge(in_low, KD)
                        n = (E1, E2)[m]
                        for t in range(TT):
                            o = MB[:, t * n:(t + 1) * n]
                            for i, j, k in TERMS:
                                last = pe.matmul(o, inT[i][:, k, t * P:(t + 1) * P], router_w[m][j][:, k],
                                                 start=(i, j, k) == TERMS[0], stop=m == 1 and (i, j, k) == TERMS[-1])
                            if m == 0:
                                last = pe.matmul(o, condb[:], wg[:], start=False, stop=True)
                        last.then_inc(logits_psum, 1)

                    def weights_turned(m):
                        pe.wait_ge(parts_ready, m + 1)
                        n = 3 * (E1, E2)[m]
                        for t in range(TT):
                            last = pe.transpose(MB16[0:n, t * P:(t + 1) * P], parts[:, t, 0:n], ident16[:])
                        last.then_inc(wT_psum, 1)

                    def project(q):
                        m, i_item = ITEMS[q]
                        if q >= 2:
                            pe.wait_ge(gate_active, q - 1)
                            pe.wait_ge(mult_up, q - 1)
                        for dst, wts, psum in ((GB, gate, gate_psum), (UB, up, up_psum)):
                            for i, j, k in TERMS:
                                last = pe.matmul(dst[q % 2][:, :], wts[m][j][:, k, i_item], inT[i][:, k],
                                                 start=(i, j, k) == TERMS[0], stop=(i, j, k) == TERMS[-1])
                            last.then_inc(psum, 1)

                    def spread(q):
                        m, i = ITEMS[q]
                        if i == SHARED[m]:
                            weights_turned(m)
                            pe.wait_ge(wT_ready, m + 1)
                        n = 3 * (E1, E2)[m]
                        if n_routed(q) > 1:
                            pe.wait_ge(weighted, n_routed(q) - 1)
                        pe.matmul(WB[:, :], pick[0:n, m, i - SHARED[m]], wT[0:n, :], start=True,
                                  stop=True).then_inc(weight_psum, 1)

                    def project_down(q):
                        m, i_item = ITEMS[q]
                        pe.wait_ge(hid_high, q + 1)
                        pe.wait_ge(hid_low, q + 1)
                        if m == 1 and i_item == 0:
                            pe.wait_ge(in_high, KD)
                            pe.wait_ge(in_low, KD)
                        for k in range(KD):
                            for i, j in ((0, 0), (0, 1), (1, 0)):
                                last = pe.matmul(YB[k][:, :], down[m][j][:, i_item, k * P:(k + 1) * P],
                                                 hid_part[i][:, q % H_SLOTS], start=i_item == 0 and i + j == 0,
                                                 stop=i_item == NI[m] - 1 and i == 1)
                        last.then_inc(hid_used, 1)

                    for m in range(2):
                        first = 0 if m == 0 else N1
                        router(m)
                        last_item = first + NI[m] - 1
                        for q in range(first, last_item + 1):
                            project(q)
                            if q > first and routed(q - 1):
                                spread(q - 1)
                            if q >= first + 2:
                                project_down(q - 2)
                        spread(last_item)
                        project_down(last_item - 1)
                        project_down(last_item)
                    if ahead:
                        pe.wait_ge(x_ahead, 16)
                        pe.wait_ge(gate_active, NQ)
                        turn_rows(pe)
                    pe.wait_ge(outT_act, 1)
                    pe.wait_ge(outT_dve, 1)
                    for half_of in range(2):
                        for tt in range(2):
                            t = 2 * half_of + tt
                            for k in range(KD):
                                last = pe.transpose(UB[half_of][:, tt * D + k * P:tt * D + (k + 1) * P],
                                                    outT[:, k, t * P:(t + 1) * P], ident[:])
                        last.then_inc(rows_back, 1)

                @block.scalar
                def _(act):
                    def exps(m):
                        act.wait_ge(shifted, m + 1)
                        n = (E1, E2)[m]
                        act.activation(ex[:, :, 0:n], lg[:, :, 0:n], ACT.Exp, scale=(1.0, -1.0)[m]).then_inc(exps_ready, 1)

                    def high(q):
                        if routed(q):
                            act.wait_ge(weighted, n_routed(q))
                        else:
                            act.wait_ge(mult_up, q + 1)
                        if q >= H_SLOTS:
                            act.wait_ge(hid_used, q - H_SLOTS + 1)
                        act.copy(hid_part[0][:, q % H_SLOTS], hid[:, q % G_SLOTS]).then_inc(hid_high, 1)

                    for q, (m, i) in enumerate(ITEMS):
                        if i == 0:
                            exps(m)
                        act.wait_ge(gate_psum, q + 1)
                        if q >= G_SLOTS:
                            act.wait_ge(hid_low, q - G_SLOTS + 1)
                        act.activation(hid[:, q % G_SLOTS], GB[q % 2][:, :],
                                       (ACT.Copy, ACT.Silu)[m]).then_inc(gate_active, 1)
                        if i > 0:
                            high(q - 1)
                        if i == NI[m] - 1:
                            high(q)
                            act.wait_ge(hid_used, q + 1)
                            if m == 0:
                                in_highs(act, YB)
                            else:
                                act.copy(outT[:, 0], YB[0][:, :]).then_inc(outT_act, 1)
                    if ahead:
                        in_highs(act, GB, turned)

                @block.gpsimd
                def _(pool):
                    for q in range(NQ):
                        pool.wait_ge(hid_high, q + 1)
                        if q >= H_SLOTS:
                            pool.wait_ge(hid_used, q - H_SLOTS + 1)
                        pool.tensor_tensor(hid_part[1][:, q % H_SLOTS], hid[:, q % G_SLOTS],
                                           hid_part[0][:, q % H_SLOTS].bitcast(F32), ALU.subtract).then_inc(hid_low, 1)

                @block.vector
                def _(dve):
                    link = Chain(dve, dve_chain)
                    def route(m, part):
                        n = (E1, E2)[m]
                        psum = MB[:, 0:TT * n].rearrange("p (t e) -> p t e", e=n)
                        l, e, s = lg[:, :, 0:n], ex[:, :, 0:n], sc[:, :, 0:n]
                        chosen, wn = sel[:, :, 0:n], w[:, :, 0:n]
                        spread_rows = lambda v: v.unsqueeze(2).broadcast_to([P, TT, n])
                        in_groups = lambda v: v.rearrange("p t (g e) -> p (t g) e", g=G2)
                        if part == 0:
                            dve.wait_ge(logits_psum, m + 1)
                            if m == 0:
                                link(dve.tensor_scalar(l, psum, 0.5, None, ALU.mult))
                                link(dve.tensor_reduce(mx[:], l, AX.X, ALU.max))
                                dve.tensor_tensor(l, l, spread_rows(mx[:]), ALU.subtract).then_inc(shifted, 1)
                            else:
                                dve.tensor_copy(l, psum).then_inc(shifted, 1)
                        elif m == 0 and part == 1:
                            dve.wait_ge(exps_ready, 1)
                            link(dve.tensor_reduce(wsum[:], e, AX.X, ALU.add))
                            link(dve.reciprocal(wsum[:], wsum[:]))
                            link(dve.tensor_tensor(s, e, spread_rows(wsum[:]), ALU.mult))
                            rank_below(dve, link, chosen, s, lower, gt, ge, TT, n, 2)
                        elif m == 1 and part == 1:
                            dve.wait_ge(exps_ready, 2)
                            link(dve.tensor_scalar(e, e, 1.0, None, ALU.add))
                            link(dve.reciprocal(s, e))
                            link(dve.tensor_tensor(sbias[:], s, cb[:].unsqueeze(1).broadcast_to([P, TT, E2]), ALU.add))
                            rank_below(dve, link, in_groups(chosen), in_groups(sbias[:]), lower, gt, ge, TT * G2,
                                       E2 // G2, 2)
                            link(dve.tensor_tensor(rest[:], sbias[:], chosen, ALU.mult))
                            link(dve.tensor_reduce(gsum[:].rearrange("p t g -> p (t g)"), in_groups(rest[:]), AX.X, ALU.add))
                        elif m == 1 and part == 2:
                            rank_below(dve, link, gsel[:], gsum[:], lower, gt, ge, TT, G2, 2)
                            link(dve.tensor_scalar(goff[:], gsel[:], 1.0e30, -1.0e30, ALU.mult, ALU.add))
                            of_group = lambda v: v.rearrange("p t g -> p (t g)").unsqueeze(2).broadcast_to(
                                [P, TT * G2, E2 // G2])
                            link(dve.tensor_tensor(in_groups(sbias[:]), in_groups(sbias[:]), of_group(gsel[:]), ALU.mult))
                            link(dve.tensor_tensor(in_groups(sbias[:]), in_groups(sbias[:]), of_group(goff[:]), ALU.add))
                        elif part == 3:
                            if m == 1:
                                rank_below(dve, link, chosen, sbias[:], lower, gt, ge, TT, n, 4)
                            link(dve.tensor_tensor(wn, s, chosen, ALU.mult))
                            link(dve.tensor_reduce(wsum[:], wn, AX.X, ALU.add))
                            link(dve.tensor_scalar(wsum[:], wsum[:], 1e-20, None, ALU.add))
                            link(dve.reciprocal(wsum[:], wsum[:]))
                            link(dve.tensor_tensor(wn, wn, spread_rows(wsum[:]), ALU.mult))
                            r = rest[:, :, 0:n]
                            link(dve.tensor_copy(parts[:, :, 0:n], wn))
                            link(dve.tensor_tensor(r, wn, parts[:, :, 0:n], ALU.subtract))
                            link(dve.tensor_copy(parts[:, :, n:2 * n], r))
                            link(dve.tensor_tensor(r, r, parts[:, :, n:2 * n], ALU.subtract))
                            dve.tensor_copy(parts[:, :, 2 * n:3 * n], r).then_inc(parts_ready, 1)

                    def take_weights(m):
                        n = 3 * (E1, E2)[m]
                        dve.wait_ge(wT_psum, m + 1)
                        if m == 1:
                            dve.wait_ge(weight_psum, E1)
                        dve.tensor_copy(wT[0:n, :], MB16[0:n, 0:L]).then_inc(wT_ready, 1)

                    def weigh(q):
                        m, i = ITEMS[q]
                        if i == SHARED[m]:
                            take_weights(m)
                        h = hid[:, q % G_SLOTS]
                        dve.wait_ge(mult_up, q + 1)
                        dve.wait_ge(weight_psum, n_routed(q))
                        dve.tensor_tensor(h, h, WB[:, :], ALU.mult).then_inc(weighted, 1)

                    BEFORE = ({0: (0, 1), 1: (3,)}, {0: (0, 1), 1: (2,), 2: (3,)})
                    for q, (m, i) in enumerate(ITEMS):
                        for part in BEFORE[m].get(i, ()):
                            route(m, part)
                        h = hid[:, q % G_SLOTS]
                        dve.wait_ge(gate_active, q + 1)
                        if m == 0:
                            link(dve.scalar_tensor_tensor(out=h, in0=h, scalar=0.01, in1=h, op0=ALU.mult, op1=ALU.max))
                        dve.wait_ge(up_psum, q + 1)
                        dve.tensor_tensor(h, h, UB[q % 2][:, :], ALU.mult).then_inc(mult_up, 1)
                        if i > 0 and routed(q - 1):
                            weigh(q - 1)
                        if i == NI[m] - 1:
                            weigh(q)
                            if m == 0:
                                in_lows(dve, 0, YB)
                            else:
                                dve.wait_ge(hid_used, q + 1)
                                dve.tensor_copy(outT[:, 1], YB[1][:, :]).then_inc(outT_dve, 1)
                    if ahead:
                        in_lows(dve, 1, GB)
                        dve.wait_ge(logits_psum, 1)
                        dve.wait_ge(cond_in, 16)
                        dve.tensor_copy(condb[:], cond_now[:].broadcast_to([DH, P]))
                    dve.wait_ge(x_in, 16)
                    for half_of in range(2):
                        ts = slice(2 * half_of, 2 * half_of + 2)
                        dve.wait_ge(rows_back, half_of + 1)
                        dve.tensor_tensor(res[:, ts].rearrange("p t d -> p (t d)"), UB[half_of][:, :],
                                          x1[:, ts].rearrange("p t d -> p (t d)"), ALU.add).then_inc(res_ready, 1)
            clear(nc, sems)

        with nc.Fori(0, B - 1) as b:
            batch(b, True)
        batch(B - 1, False)


def bass_adaln(nc, a, out, scratch):
    bias_phase(nc, a, scratch["bias_rows"])
    attention_phase(nc, a, scratch["bias_rows"], scratch["hT"])
    delta_inputs_phase(nc, a, scratch["hT"], scratch["xg"], scratch["qk"], scratch["vb"], scratch["gates"],
                       scratch["low"])
    inverse_phase(nc, a, scratch["low"], scratch["inv"])
    delta_rule_phase(nc, a, scratch["xg"], scratch["qk"], scratch["vb"], scratch["gates"], scratch["inv"],
                     scratch["x1"])
    mixtures_phase(nc, a, scratch["x1"], out)


def kernel(**inputs):
    import numpy as _np
    import concourse.bacc as _bacc
    from concourse import mybir as _mybir
    from concourse.bass_utils import run_bass_kernel_spmd as _run

    names = [n for n in inputs if n != "mask_BxS_bf1"]
    arrays = {n: _np.ascontiguousarray(inputs[n]) for n in names}
    for n in ("L0_cond_g_norm", "L0_cond_g_out"):
        arrays[n] = _np.ascontiguousarray(arrays[n].reshape(-1, P).T)
    arrays["mask"] = _np.ascontiguousarray(inputs["mask_BxS_bf1"]).view(_np.uint8)
    for n in ("x", "mask"):
        arrays[f"{n}_next"] = _np.concatenate([arrays[n][1:], arrays[n][:1]])
    arrays["c_ident"] = _np.eye(P, dtype=_np.float32)
    arrays["c_turn"] = _np.ascontiguousarray(arrays["c_ident"][::-1])
    arrays["c_pos"] = (L - 1 - _np.arange(L).reshape(TT, P).T).astype(_np.float32)
    arrays["c_lower"] = _np.ascontiguousarray(_np.broadcast_to(_np.tril(_np.ones((E2, E2), _np.float32), -1), (P, E2, E2)))
    pick = _np.zeros((3 * E2, 2, 8, P), _np.float32)
    for s in range(3):
        for i in range(8):
            pick[E1 * s + i, 0, i, :] = 1
            for e in range(2):
                pick[E2 * s + 2 * i + e, 1, i, M2 * e:M2 * (e + 1)] = 1
    arrays["c_pick"] = pick
    arrays["c_cond"] = _np.ascontiguousarray(inputs["cond_64"][:, :, None])
    arrays["conv"] = _np.ascontiguousarray(_np.stack([inputs[f"L0_attn_conv_{n}"] for n in "qkv"])
                                           .reshape(3, KD, P, 4).transpose(2, 0, 1, 3))
    arrays["L0_attn_frac_conv_w"] = _np.ascontiguousarray(
        inputs["L0_attn_frac_conv_w"].reshape(4, KD, P, 2).transpose(2, 1, 0, 3))
    angle = _np.arange(L)[:, None] * (1.0 / 10000.0 ** (_np.arange(0, DH, 2) / DH))[None, :]
    for n, f in (("c_cos", _np.cos), ("c_sin", _np.sin)):
        arrays[n] = _np.ascontiguousarray(f(angle).astype(_np.float32).reshape(TT, P, -1).transpose(1, 0, 2))
    at = _np.arange(P)
    same = at[:, None] // CH == at[None, :] // CH
    arrays["c_causal"] = (same & (at[:, None] <= at[None, :])).astype(_np.float32)
    arrays["c_strict"] = -(at[:, None] % CH > _np.arange(CH)[None, :]).astype(_np.float32)
    arrays["c_chunk_of"] = ((at[:, None] // CH == _np.arange(NC4)[None, :]) / CH).astype(_np.float32)
    arrays["c_eye32"] = _np.ascontiguousarray(_np.broadcast_to(_np.eye(CH, dtype=_np.float32), (P, CH, CH)))
    gates = _np.concatenate([inputs[f"L0_attn_{n}"] for n in ("Wb", "Wgamma", "frac_gate_w")], axis=1)
    arrays["gates"] = _np.ascontiguousarray(gates.reshape(KD, P, -1).transpose(1, 0, 2))
    for n in ("L0_cond2_wt", "L0_ffn_router_w"):
        arrays[n] = _np.ascontiguousarray(arrays[n].T.reshape(KD, P, -1).transpose(1, 0, 2))
    arrays["L0_cond2_wg"] = _np.ascontiguousarray(arrays["L0_cond2_wg"].T)
    for n in ("gate", "up", "down"):
        n = f"L0_ffn_shared_{n}_w"
        arrays[n] = _np.ascontiguousarray(arrays[n].T)
    nc = _bacc.Bacc("TRN2", target_bir_lowering=False, num_devices=1)
    a = {}
    fed = {}
    for n, v in arrays.items():
        a[n] = nc.dram_tensor(f"in_{n}", v.shape, _mybir.dt.from_np(v.dtype), kind="ExternalInput").ap()
        fed[f"in_{n}"] = v
    out = nc.dram_tensor("out", [B, L, D], _mybir.dt.float32, kind="ExternalOutput").ap()
    shapes = {"bias_rows": [NH, BIAS_W + 1], "hT": [B + 1, P, KD, L], "xg": [B, P, TT * D], "qk": [B, P, TT * 2 * D],
              "vb": [B, P, TT * D], "gates": [B, P, TT * (2 * H2 + 1)], "low": [B, TT, H2, NC4, CH, CH],
              "inv": [B, TT, H2, NC4, CH, CH], "x1": [B, L, D]}
    scratch = {n: nc.dram_tensor(f"s_{n}", shape, _mybir.dt.float32, kind="Internal").ap() for n, shape in shapes.items()}
    bass_adaln(nc, a, out, scratch)
    r = _run(nc, [fed], core_ids=[0])
    return r.results[0]["out"]
```
